# Optimizing a Trainium2 kernel written in Bass

```python
import numpy as np
import jax
import jax.numpy as jnp

def _softmax(x, axis=-1):
    return jax.nn.softmax(x, axis=axis)

def _gelu(x):
    return jax.nn.gelu(x, approximate=True)

def _silu(x):
    return jax.nn.silu(x)

def _sigmoid(x):
    return jax.nn.sigmoid(x)

def _layernorm(x, axis=-1, eps=1e-05):
    m = jnp.mean(x, axis=axis, keepdims=True)
    v = jnp.var(x, axis=axis, keepdims=True)
    return (x - m) / jnp.sqrt(v + eps)

def _scatter_add(tgt, idx, src, axis=0):
    return tgt.at[idx].add(src)

def _segment_sum(src, seg, n):
    return jax.ops.segment_sum(src, seg, n)
kernel_name = 'mk_prb_d2_jaxref_r8_a6f717'

def setup_inputs(seed: int=0):
    np.random.seed(seed)
    _w = jnp.asarray

    def _L0_attn_setup():
        import jax, jax.numpy as jnp
        import numpy as np
        HIDDEN = 256
        N_HEADS = 16
        HEAD_DIM = HIDDEN // N_HEADS

        def rotate_half(x):
            x1, x2 = jnp.split(x, 2, axis=-1)
            return jnp.concatenate([-x2, x1], axis=-1)
        key = jax.random.key(seed)
        k0, k1, k2, k3, k4 = jax.random.split(key, 5)
        B, S = (1, 256)
        scale = 1.0 / np.sqrt(HIDDEN)
        return {'hidden_states': jax.random.normal(k0, (B, S, HIDDEN), dtype=jnp.float32), 'Wq': jax.random.normal(k1, (HIDDEN, HIDDEN), dtype=jnp.float32) * scale, 'Wk': jax.random.normal(k2, (HIDDEN, HIDDEN), dtype=jnp.float32) * scale, 'Wv': jax.random.normal(k3, (HIDDEN, HIDDEN), dtype=jnp.float32) * scale, 'Wo': jax.random.normal(k4, (HIDDEN, HIDDEN), dtype=jnp.float32) * scale, 'gate': jnp.zeros((1, N_HEADS, 1, 1), dtype=jnp.float32)}
    _L0_attn_in = _L0_attn_setup()

    def _L0_ffn_setup():
        import jax, jax.numpy as jnp
        import numpy as np
        B, T, D = (1, 128, 256)
        F_DIM = 176
        E = 8
        TOPK = 2
        key = jax.random.key(seed)
        ks = jax.random.split(key, 5)
        x = jax.random.normal(ks[0], (B, T, D), dtype=jnp.float32)
        gate_w = jax.random.normal(ks[1], (E, D), dtype=jnp.float32) * 0.02
        gate_proj = jax.random.normal(ks[2], (E, F_DIM, D), dtype=jnp.float32) * 0.02
        up_proj = jax.random.normal(ks[3], (E, F_DIM, D), dtype=jnp.float32) * 0.02
        down_proj = jax.random.normal(ks[4], (E, D, F_DIM), dtype=jnp.float32) * 0.02
        return {'x': x, 'gate_w': gate_w, 'gate_proj': gate_proj, 'up_proj': up_proj, 'down_proj': down_proj}
    _L0_ffn_in = _L0_ffn_setup()

    def _L1_attn_setup():
        import jax, jax.numpy as jnp
        import numpy as np
        EPS = 1e-05
        CHUNK = 128

        def lightning_attn(q, k, v, ld, chunk=CHUNK):
            b, n, h, d = q.shape
            nc = n // chunk
            idx = jnp.arange(chunk)
            diff = idx[:, None] - idx[None, :]
            mask = diff >= 0
            D = jnp.exp(ld[:, None, None] * jnp.where(mask, diff, 0)) * mask
            q_decay = jnp.exp(ld[None, :] * (idx + 1)[:, None])
            k_decay = jnp.exp(ld[None, :] * (chunk - 1 - idx)[:, None])
            chunk_decay = jnp.exp(ld * chunk)
            qc = jnp.moveaxis(q.reshape(b, nc, chunk, h, d), 1, 0)
            kc = jnp.moveaxis(k.reshape(b, nc, chunk, h, d), 1, 0)
            vc = jnp.moveaxis(v.reshape(b, nc, chunk, h, d), 1, 0)

            def step(S, inp):
                qb, kb, vb = inp
                scores = jnp.einsum('bchd,bshd->bhcs', qb, kb) * D[None]
                o_intra = jnp.einsum('bhcs,bshd->bchd', scores, vb)
                o_inter = jnp.einsum('bchd,bhde->bche', qb, S) * q_decay[None, :, :, None]
                S_new = chunk_decay[None, :, None, None] * S + jnp.einsum('bshd,bshe->bhde', kb * k_decay[None, :, :, None], vb)
                return (S_new, o_intra + o_inter)
            S0 = jnp.zeros((b, h, d, d), dtype=q.dtype)
            S_final, oc = jax.lax.scan(step, S0, (qc, kc, vc))
            out = jnp.moveaxis(oc, 0, 1).reshape(b, n, h, d)
            return (out, S_final)

        def group_rmsnorm_fused_gate(o, gate, w, num_heads):
            b, n, d = o.shape
            hd = d // num_heads
            o = o * jax.nn.sigmoid(gate)
            og = o.reshape(b, n, num_heads, hd)
            og = og * jax.lax.rsqrt(jnp.mean(og * og, axis=-1, keepdims=True) + EPS)
            return og.reshape(b, n, d) * w
        key = jax.random.key(seed)
        ks = jax.random.split(key, 10)
        B, N, D, H = (2, 512, 256, 16)
        HD = D // H
        s = 1.0 / np.sqrt(D)
        x = jax.random.normal(ks[0], (B, N, D), dtype=jnp.float32)
        log_decay = -jax.random.uniform(ks[1], (H,), dtype=jnp.float32, minval=0.01, maxval=1.0)
        Wq = jax.random.normal(ks[2], (D, D), dtype=jnp.float32) * s
        Wk = jax.random.normal(ks[3], (D, D), dtype=jnp.float32) * s
        Wv = jax.random.normal(ks[4], (D, D), dtype=jnp.float32) * s
        Wo = jax.random.normal(ks[5], (D, D), dtype=jnp.float32) * s
        Wg1 = jax.random.normal(ks[6], (D, HD), dtype=jnp.float32) * s
        Wg2 = jax.random.normal(ks[7], (HD, D), dtype=jnp.float32) / np.sqrt(HD)
        norm_w = jnp.ones((D,), dtype=jnp.float32)
        return {'x': x, 'log_decay': log_decay, 'Wq': Wq, 'Wk': Wk, 'Wv': Wv, 'Wo': Wo, 'Wg1': Wg1, 'Wg2': Wg2, 'norm_w': norm_w}
    _L1_attn_in = _L1_attn_setup()

    def _L1_ffn_setup():
        import jax, jax.numpy as jnp
        import numpy as np
        B, S, D, H, E, TOP_K = (4, 256, 256, 512, 8, 2)
        key = jax.random.key(seed)
        k0, k1, k2, k3, k4 = jax.random.split(key, 5)
        scale = 0.02
        return {'hidden_states': jax.random.normal(k0, (B, S, D), jnp.float32), 'w_router': jax.random.normal(k1, (D, E), jnp.float32) * scale, 'w_gate': jax.random.normal(k2, (E, D, H), jnp.float32) * scale, 'w_up': jax.random.normal(k3, (E, D, H), jnp.float32) * scale, 'w_down': jax.random.normal(k4, (E, H, D), jnp.float32) * scale}
    _L1_ffn_in = _L1_ffn_setup()
    _d = {'L0_attn_hidden_states': _L0_attn_in['hidden_states'], 'L0_attn_Wq': _L0_attn_in['Wq'], 'L0_attn_Wk': _L0_attn_in['Wk'], 'L0_attn_Wv': _L0_attn_in['Wv'], 'L0_attn_Wo': _L0_attn_in['Wo'], 'L0_attn_gate': _L0_attn_in['gate'], 'L0_ffn_gate_w': _L0_ffn_in['gate_w'], 'L0_ffn_gate_proj': _L0_ffn_in['gate_proj'], 'L0_ffn_up_proj': _L0_ffn_in['up_proj'], 'L0_ffn_down_proj': _L0_ffn_in['down_proj'], 'L1_attn_log_decay': _L1_attn_in['log_decay'], 'L1_attn_Wq': _L1_attn_in['Wq'], 'L1_attn_Wk': _L1_attn_in['Wk'], 'L1_attn_Wv': _L1_attn_in['Wv'], 'L1_attn_Wo': _L1_attn_in['Wo'], 'L1_attn_Wg1': _L1_attn_in['Wg1'], 'L1_attn_Wg2': _L1_attn_in['Wg2'], 'L1_attn_norm_w': _L1_attn_in['norm_w'], 'L1_ffn_w_router': _L1_ffn_in['w_router'], 'L1_ffn_w_gate': _L1_ffn_in['w_gate'], 'L1_ffn_w_up': _L1_ffn_in['w_up'], 'L1_ffn_w_down': _L1_ffn_in['w_down']}
    _x0 = _d['L0_attn_hidden_states']
    _d['L0_attn_hidden_states'] = jax.random.normal(jax.random.fold_in(jax.random.key(seed), 1), (4, 512, 256), dtype=_x0.dtype)
    del _x0
    return _d

def reference(L0_attn_hidden_states, L0_attn_Wq, L0_attn_Wk, L0_attn_Wv, L0_attn_Wo, L0_attn_gate, L0_ffn_gate_w, L0_ffn_gate_proj, L0_ffn_up_proj, L0_ffn_down_proj, L1_attn_log_decay, L1_attn_Wq, L1_attn_Wk, L1_attn_Wv, L1_attn_Wo, L1_attn_Wg1, L1_attn_Wg2, L1_attn_norm_w, L1_ffn_w_router, L1_ffn_w_gate, L1_ffn_w_up, L1_ffn_w_down):

    def _L0_attn_ref(hidden_states, Wq, Wk, Wv, Wo, gate):
        import jax, jax.numpy as jnp
        import numpy as np
        HIDDEN = 256
        N_HEADS = 16
        HEAD_DIM = HIDDEN // N_HEADS

        def rotate_half(x):
            x1, x2 = jnp.split(x, 2, axis=-1)
            return jnp.concatenate([-x2, x1], axis=-1)
        B, S, H = hidden_states.shape
        q = hidden_states @ Wq.T
        k = hidden_states @ Wk.T
        v = hidden_states @ Wv.T
        inv_freq = 1.0 / 10000.0 ** (jnp.arange(0, H, 2, dtype=jnp.float32) / H)
        t = jnp.arange(S, dtype=jnp.float32)
        freqs = t[:, None] * inv_freq[None, :]
        emb = jnp.concatenate([freqs, freqs], axis=-1)[None]
        cos, sin = (jnp.cos(emb), jnp.sin(emb))
        q = q * cos + rotate_half(q) * sin
        k = k * cos + rotate_half(k) * sin

        def split_heads(x):
            return x.reshape(B, S, N_HEADS, HEAD_DIM).transpose(0, 2, 1, 3)
        q, k, v = (split_heads(q), split_heads(k), split_heads(v))
        k_feat = jax.nn.elu(k) + 1.0
        memory = jnp.einsum('bhsd,bhse->bhde', k_feat, v)
        norm_term = k_feat.sum(axis=2)
        q_feat = jax.nn.elu(q) + 1.0
        mem_out = jnp.einsum('bhsd,bhde->bhse', q_feat, memory)
        denom = jnp.einsum('bhsd,bhd->bhs', q_feat, norm_term)[..., None]
        mem_out = mem_out / denom
        scale = 1.0 / jnp.sqrt(jnp.float32(HEAD_DIM))
        scores = jnp.einsum('bhqd,bhkd->bhqk', q, k) * scale
        attn = jnp.einsum('bhqk,bhkd->bhqd', jax.nn.softmax(scores, axis=-1), v)
        g = jax.nn.sigmoid(gate)
        combined = g * mem_out + (1.0 - g) * attn
        combined = combined.transpose(0, 2, 1, 3).reshape(B, S, H)
        return combined @ Wo.T

    def _L0_ffn_ref(x, gate_w, gate_proj, up_proj, down_proj):
        import jax, jax.numpy as jnp
        import numpy as np
        B, T, D = (1, 128, 256)
        F_DIM = 176
        E = 8
        TOPK = 2
        b, t, d = x.shape
        x_flat = x.reshape(-1, d)
        n = x_flat.shape[0]
        router_logits = x_flat @ gate_w.T
        top_w, sel = jax.lax.top_k(router_logits, TOPK)
        top_w = jax.nn.softmax(top_w, axis=-1)
        tok_ids = jnp.arange(n)[:, None]
        tw = jnp.zeros((n, E), dtype=x.dtype).at[tok_ids, sel].add(top_w)
        g = jnp.einsum('nd,efd->enf', x_flat, gate_proj)
        u = jnp.einsum('nd,efd->enf', x_flat, up_proj)
        h = jax.nn.silu(g) * u
        eo = jnp.einsum('enf,edf->end', h, down_proj)
        out = jnp.einsum('end,ne->nd', eo, tw)
        return out.reshape(b, t, d)

    def _L1_attn_ref(x, log_decay, Wq, Wk, Wv, Wo, Wg1, Wg2, norm_w):
        import jax, jax.numpy as jnp
        import numpy as np
        EPS = 1e-05
        CHUNK = 128

        def lightning_attn(q, k, v, ld, chunk=CHUNK):
            b, n, h, d = q.shape
            nc = n // chunk
            idx = jnp.arange(chunk)
            diff = idx[:, None] - idx[None, :]
            mask = diff >= 0
            D = jnp.exp(ld[:, None, None] * jnp.where(mask, diff, 0)) * mask
            q_decay = jnp.exp(ld[None, :] * (idx + 1)[:, None])
            k_decay = jnp.exp(ld[None, :] * (chunk - 1 - idx)[:, None])
            chunk_decay = jnp.exp(ld * chunk)
            qc = jnp.moveaxis(q.reshape(b, nc, chunk, h, d), 1, 0)
            kc = jnp.moveaxis(k.reshape(b, nc, chunk, h, d), 1, 0)
            vc = jnp.moveaxis(v.reshape(b, nc, chunk, h, d), 1, 0)

            def step(S, inp):
                qb, kb, vb = inp
                scores = jnp.einsum('bchd,bshd->bhcs', qb, kb) * D[None]
                o_intra = jnp.einsum('bhcs,bshd->bchd', scores, vb)
                o_inter = jnp.einsum('bchd,bhde->bche', qb, S) * q_decay[None, :, :, None]
                S_new = chunk_decay[None, :, None, None] * S + jnp.einsum('bshd,bshe->bhde', kb * k_decay[None, :, :, None], vb)
                return (S_new, o_intra + o_inter)
            S0 = jnp.zeros((b, h, d, d), dtype=q.dtype)
            S_final, oc = jax.lax.scan(step, S0, (qc, kc, vc))
            out = jnp.moveaxis(oc, 0, 1).reshape(b, n, h, d)
            return (out, S_final)

        def group_rmsnorm_fused_gate(o, gate, w, num_heads):
            b, n, d = o.shape
            hd = d // num_heads
            o = o * jax.nn.sigmoid(gate)
            og = o.reshape(b, n, num_heads, hd)
            og = og * jax.lax.rsqrt(jnp.mean(og * og, axis=-1, keepdims=True) + EPS)
            return og.reshape(b, n, d) * w
        b, n, d = x.shape
        H = log_decay.shape[0]
        hd = d // H
        q = jax.nn.silu(jnp.einsum('bnd,de->bne', x, Wq).reshape(b, n, H, hd))
        k = jax.nn.silu(jnp.einsum('bnd,de->bne', x, Wk).reshape(b, n, H, hd))
        v = jax.nn.silu(jnp.einsum('bnd,de->bne', x, Wv).reshape(b, n, H, hd))
        o, _ = lightning_attn(q, k, v, log_decay)
        o = o.reshape(b, n, d)
        gate = jnp.einsum('bnk,kd->bnd', jnp.einsum('bnd,dk->bnk', x, Wg1), Wg2)
        o = group_rmsnorm_fused_gate(o, gate, norm_w, H)
        return jnp.einsum('bnd,de->bne', o, Wo)

    def _L1_ffn_ref(hidden_states, w_router, w_gate, w_up, w_down):
        import jax, jax.numpy as jnp
        import numpy as np
        B, S, D, H, E, TOP_K = (4, 256, 256, 512, 8, 2)
        x = hidden_states.reshape(-1, hidden_states.shape[-1])
        T = x.shape[0]
        logits = x @ w_router
        probs = jax.nn.softmax(logits.astype(jnp.float32), axis=-1)
        rw, sel = jax.lax.top_k(probs, TOP_K)
        rw = rw / jnp.sum(rw, axis=-1, keepdims=True)
        rw = rw.astype(x.dtype)
        combine = jnp.zeros((T, E), x.dtype).at[jnp.arange(T)[:, None], sel].set(rw)
        out = jnp.zeros_like(x)
        for e in range(E):
            g = jax.nn.silu(x @ w_gate[e]) * (x @ w_up[e])
            y = g @ w_down[e]
            out = out + combine[:, e:e + 1] * y
        return out.reshape(hidden_states.shape)
    x = L0_attn_hidden_states
    xn = _layernorm(x, axis=-1)
    x = x + _L0_attn_ref(xn, L0_attn_Wq, L0_attn_Wk, L0_attn_Wv, L0_attn_Wo, L0_attn_gate) + _L0_ffn_ref(xn, L0_ffn_gate_w, L0_ffn_gate_proj, L0_ffn_up_proj, L0_ffn_down_proj)
    xn = _layernorm(x, axis=-1)
    x = x + _L1_attn_ref(xn, L1_attn_log_decay, L1_attn_Wq, L1_attn_Wk, L1_attn_Wv, L1_attn_Wo, L1_attn_Wg1, L1_attn_Wg2, L1_attn_norm_w) + _L1_ffn_ref(xn, L1_ffn_w_router, L1_ffn_w_gate, L1_ffn_w_up, L1_ffn_w_down)
    return x

_drawn_inputs = setup_inputs


def setup_inputs(seed=0):
    import zlib

    import numpy as np

    out = dict(_drawn_inputs(seed))
    spreads = {'L0_attn_gate': (0.0, 0.8), 'L1_attn_norm_w': (1.0, 0.2)}
    factors = {'L0_ffn_gate_w': 3.879,
     'L0_ffn_gate_proj': 3.442,
     'L0_ffn_up_proj': 3.367,
     'L0_ffn_down_proj': 3.341,
     'L1_ffn_w_router': 5.643,
     'L1_ffn_w_gate': 4.927,
     'L1_ffn_w_up': 4.874,
     'L1_ffn_w_down': 4.873}
    for name, (base, spread) in spreads.items():
        noise = np.random.default_rng([zlib.crc32(name.encode()), seed]).standard_normal(out[name].shape)
        drawn = base * np.exp(spread * noise) if base else spread * noise
        out[name] = jnp.asarray(drawn.astype(out[name].dtype))
    for name, factor in factors.items():
        out[name] = (out[name] * factor).astype(out[name].dtype)
    return out
```

```python
from contextlib import ExitStack

import concourse.bass as bass
from concourse import mybir

F32 = mybir.dt.float32
F32R = mybir.dt.float32r
BF16 = mybir.dt.bfloat16
U32 = mybir.dt.uint32
ALU = mybir.AluOpType
ACT = mybir.ActivationFunctionType
AX_X = mybir.AxisListType.X

P = 128
BATCHES = 4
SEQ = 512
TOK = BATCHES * SEQ
TILES = SEQ // P
D = 256
KT = D // P
HEADS = 16
HD = D // HEADS
HG = 4
GROUPS = HEADS // HG
HH = HEADS // KT
EPS = 1e-5
E = 8
F0 = 176
FT0 = E * F0 // P
H1 = 512
HT1 = H1 // P
CH = 128
VW = 32
MW = P + HH
Q_PARTS = (0, 0, 1, 0, 2, 1)
K_PARTS = (0, 1, 0, 2, 0, 1)
STACK = len(Q_PARTS) * HD
STACKM = STACK + 2


def three(nc, out, pairs, regions_first=True, last=True, start=True):
    n = len(pairs)
    for i, (ah, al, bh, bl) in enumerate(pairs):
        nc.tensor.matmul(out, ah, bh, start=start and i == 0, stop=False, skip_group_check=True)
        nc.tensor.matmul(out, ah, bl, start=False, stop=False, skip_group_check=True)
        mm = nc.tensor.matmul(out, al, bh, start=False, stop=last and i == n - 1, skip_group_check=True)
    return mm


def stage_semaphore(nc, keep, name):
    handle = nc.alloc_semaphore(name)
    keep["semaphores"].append(handle)
    return handle


def end_stage(nc, keep):
    nc.clear_and_free_semaphores(keep["semaphores"])
    keep["semaphores"] = []
    nc.all_engine_barrier()


class Norm:

    def __init__(self, nc, sb, sem):
        self.nc = nc
        self.stats, self.mv = sb("ln_stats", [P, TILES, 6]), sb("ln_mv", [P, TILES, 2])
        self.vare, self.rstd = sb("ln_vare", [P, TILES]), sb("ln_rstd", [P, TILES])
        self.neghalf, self.held = sb("ln_neghalf", [P, TILES]), sb("ln_held", [P, 1])
        self.neghalf_set, self.stats_done, self.mv_done = sem("ln_neghalf"), sem("ln_stats"), sem("ln_mv")
        self.vare_done, self.rstd_done, self.xn_done = sem("ln_vare"), sem("ln_rstd"), sem("ln_xn")

    def setup(self, pool):
        self.nc.gpsimd.memset(self.neghalf[:, :], -0.5).then_inc(self.neghalf_set, 1)
        pool.wait_ge(self.neghalf_set, 1)

    def power(self, pool, b):
        pool.wait_ge(self.vare_done, b + 1)
        self.nc.gpsimd.tensor_tensor(self.rstd[:, :], self.vare[:, :], self.neghalf[:, :],
                                     ALU.pow).then_inc(self.rstd_done, 1)

    def vector(self, dve, b, xacc, xn):
        nc = self.nc

        def rows(t):
            return xacc[:, bass.ds(b * TILES + t, 1), :].rearrange("p a d -> p (a d)")

        for t in range(TILES):
            last = nc.vector.bn_stats(self.stats[:, t, :], rows(t))
        last.then_inc(self.stats_done, 1)
        dve.wait_ge(self.stats_done, b + 1)
        nc.vector.memset(self.held[:, :], 0.0)
        for t in range(TILES):
            nc.vector.bn_aggr(self.mv[:, t, :], self.stats[:, t, :]).then_inc(self.mv_done, 1)
        dve.wait_ge(self.mv_done, (b + 1) * TILES)
        nc.vector.tensor_scalar(self.vare[:, :], self.mv[:, :, 1], EPS, None, ALU.add).then_inc(self.vare_done, 1)
        dve.wait_ge(self.rstd_done, b + 1)
        for t in range(TILES):
            nc.vector.tensor_scalar(xn[:, t, :], rows(t), self.mv[:, t, 0:1], self.rstd[:, t:t + 1],
                                    ALU.subtract, ALU.mult).then_inc(self.xn_done, 1)


class Routing:

    STEPS = 8

    def __init__(self, nc, sb, sem):
        self.nc = nc
        self.iota8 = sb("rt_iota8", [P, TILES, E])
        self.logits, self.top = sb("rt_logits", [P, TILES, E]), sb("rt_top", [P, TILES, E])
        self.idx, self.idxf = sb("rt_idx", [P, TILES, E], U32), sb("rt_idxf", [P, TILES, 2])
        self.gap, self.w1, self.w2 = sb("rt_gap", [P, TILES]), sb("rt_w1", [P, TILES]), sb("rt_w2", [P, TILES])
        self.eq = [sb(f"rt_eq{i}", [P, TILES, E]) for i in range(2)]
        self.copied, self.top_done, self.gap_done = sem("rt_copied"), sem("rt_top"), sem("rt_gap")
        self.exp_done, self.step, self.comb_done = sem("rt_exp"), sem("rt_step"), sem("rt_comb")
        self.iota_in = sem("rt_iota_in")

    def load(self, sp, io):
        sp.dma_start(self.iota8[:, :, :], io["iota8"].rearrange("p (t e) -> p t e", e=E)).then_inc(self.iota_in, 16)

    def exp(self, act, b):
        act.wait_ge(self.gap_done, b + 1)
        self.nc.scalar.activation(self.gap[:, :], self.gap[:, :], ACT.Exp).then_inc(self.exp_done, 1)

    def vector(self, dve, b, source, comb):
        nc = self.nc
        nc.vector.tensor_copy(self.logits[:, :, :], source).then_inc(self.copied, 1)
        dve.wait_ge(self.iota_in, 16)
        dve.wait_ge(self.copied, b + 1)
        for t in range(TILES):
            nc.vector.max(self.top[:, t, :], self.logits[:, t, :]).then_inc(self.top_done, 1)
        dve.wait_ge(self.top_done, 2 * TILES * b + TILES)
        nc.vector.tensor_tensor(self.gap[:, :], self.top[:, :, 1], self.top[:, :, 0], ALU.subtract).then_inc(self.gap_done, 1)
        for t in range(TILES):
            nc.vector.max_index(self.idx[:, t, :], self.top[:, t, :], self.logits[:, t, :]).then_inc(self.top_done, 1)
        dve.wait_ge(self.top_done, 2 * TILES * (b + 1))
        nc.vector.tensor_copy(self.idxf[:, :, :], self.idx[:, :, 0:2]).then_inc(self.step, 1)
        dve.wait_ge(self.step, self.STEPS * b + 1)
        for i in range(2):
            nc.vector.tensor_tensor(self.eq[i][:, :, :], self.iota8[:, :, :],
                                    self.idxf[:, :, i:i + 1].to_broadcast((P, TILES, E)), ALU.is_equal).then_inc(self.step, 1)
        dve.wait_ge(self.exp_done, b + 1)
        nc.vector.tensor_scalar(self.w1[:, :], self.gap[:, :], 1.0, None, ALU.add).then_inc(self.step, 1)
        dve.wait_ge(self.step, self.STEPS * b + 4)
        nc.vector.reciprocal(self.w1[:, :], self.w1[:, :]).then_inc(self.step, 1)
        dve.wait_ge(self.step, self.STEPS * b + 5)
        nc.vector.tensor_tensor(self.w2[:, :], self.w1[:, :], self.gap[:, :], ALU.mult).then_inc(self.step, 1)
        dve.wait_ge(self.step, self.STEPS * b + 6)
        for i, w in enumerate((self.w1, self.w2)):
            nc.vector.tensor_tensor(self.eq[i][:, :, :], self.eq[i][:, :, :],
                                    w[:, :].unsqueeze(2).to_broadcast((P, TILES, E)), ALU.mult).then_inc(self.step, 1)
        dve.wait_ge(self.step, self.STEPS * b + 8)
        nc.vector.tensor_tensor(comb, self.eq[0][:, :, :], self.eq[1][:, :, :], ALU.add).then_inc(self.comb_done, 1)


def layer0_front(nc, io, scratch, keep):
    with ExitStack() as ctx:
        def sb(name, shape, dt=F32):
            return ctx.enter_context(nc.sbuf_tensor(name, shape, dt))

        def sem(name):
            return stage_semaphore(nc, keep, name)

        xacc, mem = keep["xacc"], keep["mem"]
        ident, cos, sin, = sb("a_ident", [P, P]), sb("a_cos", [P, SEQ]), sb("a_sin", [P, SEQ])
        blockmask, headmask = sb("a_blockmask", [P, P]), sb("a_headmask", [P, HH])
        raw = sb("a_raw", [P, FT0 * D])
        wqk = [sb(f"a_wqk{i}", [P, KT, 2 * D], F32R) for i in range(2)]
        wv = [sb(f"a_wv{i}", [P, KT, D + E], F32R) for i in range(2)]
        wg = [sb(f"a_wg{i}", [P, KT, E * F0], F32R) for i in range(2)]
        wu = [sb(f"a_wu{i}", [P, KT, E * F0], F32R) for i in range(2)]
        wd = [sb(f"a_wd{i}", [P, FT0, D], F32R) for i in range(2)]
        norm = Norm(nc, lambda n, *a: sb("a_" + n, *a), lambda n: sem("a_" + n))
        routing = Routing(nc, lambda n, *a: sb("a_" + n, *a), lambda n: sem("a_" + n))
        xn = sb("a_xn", [P, TILES, D])
        xT = [sb(f"a_xT{i}", [P, KT, SEQ], F32R) for i in range(2)]
        qk = sb("a_qk", [P, 2 * KT, SEQ])
        rot = sb("a_rot", [P, 2 * KT, SEQ])
        parts = [sb(f"a_part{i}", [P, 2 * KT, SEQ], BF16) for i in range(3)]
        vones = sb("a_vones", [P, TILES, KT, P + 2])
        v32 = sb("a_v32", [P, TILES, HEADS, VW])
        kf = sb("a_kf", [P, TILES, D])
        comb = sb("a_comb", [P, TILES, E])
        cT = sb("a_cT", [E, SEQ])
        cbc = sb("a_cbc", [P, FT0, SEQ])
        hs = [sb(f"a_hs{i}", [P, SEQ]) for i in range(2)]
        hh = [[sb(f"a_h{i}{j}", [P, SEQ], F32R) for i in range(2)] for j in range(2)]

        psT = ctx.enter_context(nc.psum_tensor("a_psT", [P, 2, SEQ], F32))
        psG = ctx.enter_context(nc.psum_tensor("a_psG", [P, 4, SEQ], F32))
        psO = ctx.enter_context(nc.psum_tensor("a_psO", [P, TILES, D], F32))

        consts_in, x_in, w_in, raw_in, raw_free = (sem(n) for n in (
            "a_consts_in", "a_x_in", "a_w_in", "a_raw_in", "a_raw_free"))
        w_split = sem("a_w_split")
        dve_done, act_done, pool_done = sem("a_dve"), sem("a_act"), sem("a_pool")
        xT_done, qk_ps, v_ps, rt_ps, kfT_ps, memo_ps, cT_ps, gu_ps, out_ps = (sem("a_" + n) for n in (
            "xTps", "qkps", "vps", "rtps", "kfTps", "memps", "cTps", "gups", "outps"))
        stored, cT_in, cbc_in = sem("a_stored"), sem("a_cT_in"), sem("a_cbc_in")
        S = {}

        def s(name):
            if name not in S:
                S[name] = sem("a_" + name)
            return S[name]

        for n in ("stats", "mv", "vare", "rstd", "xn", "xhi", "xlo", "rope", "roped", "min", "feat", "p1", "r1",
                  "p2", "p3", "vcopy", "kfcopy", "memcopy", "lg", "mx", "gapd", "gexp", "wts", "comb", "cTc",
                  "silu", "su", "h", "hhi", "hlo", "outacc", "ones", "link", "q_st", "f_st", "v_st", "expm"):
            s(n)

        block = ctx.enter_context(nc.Block())

        @block.sync
        def _(sp):
            for b in range(BATCHES):
                sp.dma_start(xacc[:, b * TILES:(b + 1) * TILES, :],
                             io["x"][b].rearrange("(t p) d -> p t d", p=P)).then_inc(x_in, 16)
                if b == 0:
                    for dst, src in ((ident, "ident"), (blockmask, "blockmask"), (headmask, "headmask")):
                        sp.dma_start(dst[:, :], io[src]).then_inc(consts_in, 16)
                    routing.load(sp, io)
            for n, (pieces) in enumerate((
                    (("Wq0", 0, D, 2 * D), ("Wk0", D, 2 * D, 2 * D)),
                    (("Wv0", 0, D, D + E), ("router0", D, D + E, D + E)),
                    (("gate0", 0, E * F0, E * F0),), (("up0", 0, E * F0, E * F0),))):
                if n:
                    sp.wait_ge(raw_free, n)
                for name, lo, hi, w in pieces:
                    sp.dma_start(raw[:, 0:KT * w].rearrange("p (k n) -> p k n", k=KT)[:, :, lo:hi],
                                 io[name].rearrange("(k p) n -> p k n", p=P)).then_inc(raw_in, 16)
                if n == 0:
                    sp.dma_start(cos[:, :], io["cos"]).then_inc(consts_in, 16)
                    sp.dma_start(sin[:, :], io["sin"]).then_inc(consts_in, 16)
            sp.wait_ge(raw_free, 4)
            sp.dma_start(raw[:, :].rearrange("p (k n) -> p k n", n=D),
                         io["down0"].rearrange("(k p) n -> p k n", p=P)).then_inc(raw_in, 16)
            with sp.Fori(0, BATCHES) as b:
                sp.wait_ge(s("cTc"), b + 1)
                sp.dma_start(scratch["cT"][b], cT[:, :]).then_inc(cT_in, 16)
                sp.wait_ge(s("h"), FT0 * b)
                sp.wait_ge(cT_in, 16 * b + 16)
                for e in range(E):
                    f = e * F0
                    while f < (e + 1) * F0:
                        n = min(P - f % P, (e + 1) * F0 - f)
                        sp.dma_start(cbc[f % P:f % P + n, f // P, :],
                                     scratch["cT"][b, e:e + 1, :].to_broadcast((n, SEQ))).then_inc(cbc_in, 16)
                        f += n
                sp.wait_ge(s("vcopy"), 2 * b + 2)
                sp.dma_start(scratch["v"][b].rearrange("(t p) n -> p t n", p=P),
                             v32[:, :, :, :].rearrange("p t h w -> p t (h w)")).then_inc(s("v_st"), 16)
                sp.wait_ge(s("feat"), 2 * b + 2)
                sp.dma_start(scratch["qf"][b].rearrange("k p n -> p k n"), rot[:, 0:KT, :]).then_inc(s("f_st"), 16)
                for i, done in enumerate(("p1", "p2", "p3")):
                    sp.wait_ge(s(done), b + 1)
                    sp.dma_start(scratch["parts"][b, i].rearrange("k p n -> p k n"), parts[i][:, :, :]).then_inc(s("q_st"), 16)
            sp.wait_ge(s("v_st"), 16 * BATCHES)
            sp.wait_ge(s("f_st"), 16 * BATCHES)
            sp.wait_ge(s("q_st"), 48 * BATCHES)

        CBC = sum(1 + ((e + 1) * F0 - 1) // P - e * F0 // P for e in range(E))

        @block.gpsimd
        def _(pool):
            norm.setup(pool)
            nc.gpsimd.memset(v32[:, :, :, HD:HD + 1], 1.0).then_inc(s("ones"), 1)
            nc.gpsimd.memset(v32[:, :, :, HD + 1:VW], 0.0).then_inc(s("ones"), 1)
            nc.gpsimd.memset(vones[:, :, :, P:P + 2], 1.0).then_inc(s("ones"), 1)
            pool.wait_ge(s("ones"), 3)
            with pool.Fori(0, BATCHES) as b:
                norm.power(pool, b)
                pool.wait_ge(s("feat"), 2 * b + 2)
                pool.wait_ge(s("p1"), b + 1)
                nc.gpsimd.tensor_tensor(qk[:, :, :], qk[:, :, :], parts[0][:, :, :], ALU.subtract).then_inc(s("r1"), 1)
                pool.wait_ge(s("p2"), b + 1)
                if True:
                    pool.wait_ge(s("q_st"), 48 * b)
                nc.gpsimd.tensor_tensor(parts[2][:, :, :], qk[:, :, :], parts[1][:, :, :], ALU.subtract).then_inc(s("p3"), 1)
                for j in range(FT0):
                    pool.wait_ge(s("hhi"), b * FT0 + j + 1)
                    nc.gpsimd.tensor_tensor(hh[j % 2][1][:, :], hs[j % 2][:, :], hh[j % 2][0][:, :].bitcast(F32),
                                            ALU.subtract).then_inc(s("hlo"), 1)

        @block.scalar
        def _(act):
            for n, dst in enumerate((wqk, wv, wg, wu, wd)):
                act.wait_ge(raw_in, (32, 64, 80, 96, 112)[n])
                if n:
                    act.wait_ge(raw_free, n)
                src = raw[:, 0:dst[0].shape[1] * dst[0].shape[2]].rearrange("p (k n) -> p k n", k=dst[0].shape[1])
                nc.scalar.activation(dst[0][:, :, :], src, ACT.Copy).then_inc(w_split, 1)
            with act.Fori(0, BATCHES) as b:
                act.wait_ge(xT_done, b + 1)
                act.wait_ge(v_ps, 4 * b)
                act.wait_ge(gu_ps, FT0 * b)
                nc.scalar.activation(xT[0][:, :, :], psT[:, :, :], ACT.Copy).then_inc(s("xhi"), 1)
                act.wait_ge(v_ps, 4 * b + 4)
                act.wait_ge(s("v_st"), 16 * b)
                nc.scalar.activation(v32[:, :, :, 0:HD], psO[:, :, :].rearrange("p t (h d) -> p t h d", d=HD),
                                     ACT.Copy).then_inc(s("vcopy"), 1)
                act.wait_ge(memo_ps, b)
                nc.scalar.activation(vones[:, :, :, 0:P], psO[:, :, :].rearrange("p t (k n) -> p t k n", k=KT),
                                     ACT.Copy).then_inc(s("vcopy"), 1)
                routing.exp(act, b)
                act.wait_ge(s("min"), b + 1)
                nc.scalar.activation(rot[:, :, :], rot[:, :, :], ACT.Exp).then_inc(s("expm"), 1)
                act.wait_ge(s("roped"), b + 1)
                act.wait_ge(s("q_st"), 48 * b)
                nc.scalar.activation(parts[0][:, :, :], qk[:, :, :], ACT.Copy).then_inc(s("p1"), 1)
                act.wait_ge(s("r1"), b + 1)
                nc.scalar.activation(parts[1][:, :, :], qk[:, :, :], ACT.Copy).then_inc(s("p2"), 1)
                act.wait_ge(kfT_ps, b + 1)
                nc.scalar.activation(kf[:, :, :], psT[:, :, :].rearrange("p a (t n) -> p (a t) n", n=D),
                                     ACT.Copy).then_inc(s("kfcopy"), 1)
                for j in range(FT0):
                    act.wait_ge(gu_ps, b * FT0 + j + 1)
                    act.wait_ge(s("hlo"), b * FT0 + j - 1) if j >= 2 else act.wait_ge(s("hlo"), b * FT0)
                    nc.scalar.activation(hs[j % 2][:, :], psG[:, 2 * (j % 2), :], ACT.Silu).then_inc(s("silu"), 1)
                    act.wait_ge(s("h"), b * FT0 + j + 1)
                    act.wait_ge(out_ps, b * FT0 + j - 1) if j >= 2 else act.wait_ge(out_ps, b * FT0)
                    nc.scalar.activation(hh[j % 2][0][:, :], hs[j % 2][:, :], ACT.Copy).then_inc(s("hhi"), 1)

        @block.vector
        def _(dve):
            for n, dst in enumerate((wqk, wv, wg, wu, wd)):
                dve.wait_ge(w_split, n + 1)
                src = raw[:, 0:dst[0].shape[1] * dst[0].shape[2]].rearrange("p (k n) -> p k n", k=dst[0].shape[1])
                nc.vector.tensor_tensor(dst[1][:, :, :], src, dst[0][:, :, :].bitcast(F32), ALU.subtract).then_inc(raw_free, 1)
            dve.wait_ge(x_in, 64)
            dve.wait_ge(consts_in, 80)
            dve.wait_ge(s("ones"), 3)
            with dve.Fori(0, BATCHES) as b:
                norm.vector(dve, b, xacc, xn)
                dve.wait_ge(s("xhi"), b + 1)
                nc.vector.tensor_tensor(xT[1][:, :, :], psT[:, :, :], xT[0][:, :, :].bitcast(F32), ALU.subtract).then_inc(s("xlo"), 1)
                dve.wait_ge(qk_ps, b + 1)
                dve.wait_ge(s("f_st"), 16 * b)
                for i in range(2):
                    for h in range(KT):
                        nc.vector.tensor_tensor(qk[:, 2 * i + h, :], psG[:, 2 * i + h, :], cos[:, :], ALU.mult)
                        nc.vector.tensor_tensor(rot[:, 2 * i + h, :], psG[:, 2 * i + 1 - h, :], sin[:, :],
                                                ALU.mult).then_inc(s("rope"), 1)
                for i in range(2):
                    dve.wait_ge(s("rope"), 4 * b + 2 * i + 2)
                    nc.vector.tensor_tensor(qk[:, 2 * i, :], qk[:, 2 * i, :], rot[:, 2 * i, :], ALU.subtract)
                    last = nc.vector.tensor_tensor(qk[:, 2 * i + 1, :], qk[:, 2 * i + 1, :], rot[:, 2 * i + 1, :], ALU.add)
                last.then_inc(s("roped"), 1)
                dve.wait_ge(s("roped"), b + 1)
                nc.vector.tensor_scalar(rot[:, :, :], qk[:, :, :], 0.0, None, ALU.min).then_inc(s("min"), 1)
                dve.wait_ge(rt_ps, b + 1)
                routing.vector(dve, b, psT[:, 0, 0:TILES * E].rearrange("p (t e) -> p t e", e=E), comb[:, :, :])
                dve.wait_ge(cT_ps, b + 1)
                dve.wait_ge(cT_in, 16 * b)
                nc.vector.tensor_copy(cT[:, :], psT[0:E, 1, :]).then_inc(s("cTc"), 1)
                dve.wait_ge(s("expm"), b + 1)
                for i in (1, 0):
                    nc.vector.scalar_tensor_tensor(rot[:, 2 * i:2 * i + 2, :], qk[:, 2 * i:2 * i + 2, :], 0.0,
                                                   rot[:, 2 * i:2 * i + 2, :], ALU.max, ALU.add).then_inc(s("feat"), 1)
                dve.wait_ge(memo_ps, b + 1)
                for k in range(KT):
                    src = psT[:, 0, 130 * k:130 * k + P]
                    nc.vector.tensor_tensor(mem[:, bass.ds(b * KT + k, 1), 0:P].rearrange("p a n -> p (a n)"), src, blockmask[:, :], ALU.mult)
                    nc.vector.tensor_tensor(mem[:, bass.ds(b * KT + k, 1), P:MW].rearrange("p a n -> p (a n)"), headmask[:, :],
                                            psT[:, 0, 130 * k + P:130 * k + P + 1].to_broadcast((P, HH)), ALU.mult).then_inc(s("memcopy"), 1)
                dve.wait_ge(cbc_in, 16 * CBC * (b + 1))
                for j in range(FT0):
                    dve.wait_ge(s("silu"), b * FT0 + j + 1)
                    nc.vector.tensor_tensor(hs[j % 2][:, :], hs[j % 2][:, :], psG[:, 2 * (j % 2) + 1, :], ALU.mult).then_inc(s("su"), 1)
                    dve.wait_ge(s("su"), b * FT0 + j + 1)
                    nc.vector.tensor_tensor(hs[j % 2][:, :], hs[j % 2][:, :], cbc[:, j, :], ALU.mult).then_inc(s("h"), 1)
                dve.wait_ge(out_ps, (b + 1) * FT0)
                nc.vector.tensor_tensor(xacc[:, bass.ds(b * TILES, TILES), :], psO[:, :, :], xacc[:, bass.ds(b * TILES, TILES), :],
                                        ALU.add).then_inc(s("outacc"), 1)
                dve.wait_ge(s("outacc"), b + 1)

        @block.tensor
        def _(pe):
            pe.wait_ge(consts_in, 80)
            pe.wait_ge(raw_free, 2)
            with pe.Fori(0, BATCHES) as b:
                pe.wait_ge(s("memcopy"), KT * b)
                for t in range(TILES):
                    pe.wait_ge(norm.xn_done, TILES * b + t + 1)
                    for k in range(KT):
                        mm = nc.tensor.transpose(psT[:, k, t * P:(t + 1) * P], xn[:, t, k * P:(k + 1) * P], ident[:, :])
                mm.then_inc(xT_done, 1)
                pe.wait_ge(s("xlo"), b + 1)
                pe.wait_ge(s("h"), FT0 * b)
                for m in range(4):
                    c = slice(m * P, (m + 1) * P)
                    mm = three(nc, psG[:, m, :], [(wqk[0][:, k, c], wqk[1][:, k, c], xT[0][:, k, :], xT[1][:, k, :])
                                                  for k in range(KT)])
                mm.then_inc(qk_ps, 1)
                for t in range(TILES):
                    c = slice(t * P, (t + 1) * P)
                    mm = three(nc, psT[:, 0, t * E:(t + 1) * E],
                               [(xT[0][:, k, c], xT[1][:, k, c], wv[0][:, k, D:D + E], wv[1][:, k, D:D + E])
                                for k in range(KT)])
                mm.then_inc(rt_ps, 1)
                pe.wait_ge(s("outacc"), b)
                for t in range(TILES):
                    c = slice(t * P, (t + 1) * P)
                    three(nc, psO[:, t, :], [(xT[0][:, k, c], xT[1][:, k, c], wv[0][:, k, 0:D], wv[1][:, k, 0:D])
                                             for k in range(KT)]).then_inc(v_ps, 1)
                pe.wait_ge(routing.comb_done, b + 1)
                for t in range(TILES):
                    mm = nc.tensor.transpose(psT[0:E, 1, t * P:(t + 1) * P], comb[:, t, :], ident[:, :])
                mm.then_inc(cT_ps, 1)
                pe.wait_ge(s("cTc"), b + 1)
                pe.wait_ge(s("feat"), 2 * b + 1)
                pe.wait_ge(routing.copied, b + 1)
                for t in range(TILES):
                    for k in range(KT):
                        at = t * D + k * P
                        mm = nc.tensor.transpose(psT[:, at // SEQ, at % SEQ:at % SEQ + P],
                                                 rot[:, 2 + k, t * P:(t + 1) * P], ident[:, :])
                mm.then_inc(kfT_ps, 1)
                pe.wait_ge(s("kfcopy"), b + 1)
                pe.wait_ge(s("vcopy"), 2 * b + 2)
                for k in range(KT):
                    for t in range(TILES):
                        mm = nc.tensor.matmul(psT[:, 0, 130 * k:130 * k + P + 2], kf[:, t, k * P:(k + 1) * P],
                                              vones[:, t, k, :], start=t == 0, stop=t == TILES - 1, skip_group_check=True)
                mm.then_inc(memo_ps, 1)
                pe.wait_ge(s("roped"), b + 1)

                def gate_up(j):
                    pe.wait_ge(raw_free, 4)
                    pe.wait_ge(s("su"), b * FT0 + j - 1) if j >= 2 else pe.wait_ge(s("su"), b * FT0)
                    c = slice(j * P, (j + 1) * P)
                    for i, w in enumerate((wg, wu)):
                        mm = three(nc, psG[:, 2 * (j % 2) + i, :],
                                   [(w[0][:, k, c], w[1][:, k, c], xT[0][:, k, :], xT[1][:, k, :]) for k in range(KT)])
                    mm.then_inc(gu_ps, 1)

                def down(j):
                    pe.wait_ge(raw_free, 5)
                    pe.wait_ge(s("hlo"), b * FT0 + j + 1)
                    for t in range(TILES):
                        c = slice(t * P, (t + 1) * P)
                        mm = three(nc, psO[:, t, :], [(hh[j % 2][0][:, c], hh[j % 2][1][:, c], wd[0][:, j, :], wd[1][:, j, :])],
                                   start=j == 0 and t % 2 == 0, last=j == FT0 - 1)
                    mm.then_inc(out_ps, 1)

                gate_up(0)
                for j in range(1, FT0):
                    gate_up(j)
                    down(j - 1)
                down(FT0 - 1)


def layer0_attention(nc, io, scratch, keep):
    with ExitStack() as ctx:
        def sb(name, shape, dt=F32):
            return ctx.enter_context(nc.sbuf_tensor(name, shape, dt))

        def sem(name):
            return stage_semaphore(nc, keep, "b_" + name)

        ident = sb("b_ident", [P, P])
        identb = sb("b_identb", [P, P], BF16)
        qst = [sb(f"b_qst{g}", [STACKM, HG, SEQ], BF16) for g in range(GROUPS)]
        kst = [sb(f"b_kst{g}", [STACKM, HG, SEQ], BF16) for g in range(GROUPS)]
        vst = [sb(f"b_vst{g}", [P, TILES, HG * VW]) for g in range(GROUPS)]
        probs = [sb(f"b_probs{k}", [P, HG, SEQ]) for k in range(TILES)]
        negmax = [sb(f"b_negmax{i}", [P, TILES, HG]) for i in range(2)]
        nmparts = [sb(f"b_nmparts{i}", [P, TILES, 2, HG], BF16) for i in range(2)]
        nmT = [sb(f"b_nmT{i}", [2 * HG, SEQ], BF16) for i in range(2)]
        outT = [sb(f"b_outT{i}", [P, SEQ]) for i in range(2)]

        psE = [ctx.enter_context(nc.psum_tensor(f"b_psE{i}", [P, 2, SEQ], F32)) for i in range(2)]
        psM = [ctx.enter_context(nc.psum_tensor(f"b_psM{i}", [P, SEQ], F32)) for i in range(2)]
        psV = ctx.enter_context(nc.psum_tensor("b_psV", [P, SEQ], F32))
        psN = ctx.enter_context(nc.psum_tensor("b_psN", [P, SEQ], BF16))

        ident_in, ones, identb_done = sem("ident_in"), sem("ones"), sem("identb")
        stack_in = [sem(f"stack_in{g}") for g in range(GROUPS)]
        max_in, max_out = [sem(f"max_in{g}") for g in range(GROUPS)], sem("max_out")
        scores_ready, scores_used = sem("scores_ready"), [sem(f"scores_used{i}") for i in range(2)]
        probs_used = [sem(f"probs_used{k}") for k in range(TILES)]
        rows_ready, rows_used = sem("rows_ready"), [sem(f"rows_used{i}") for i in range(2)]
        negmax_hi, negmax_parts = sem("negmax_hi"), sem("negmax_parts")
        nmT_ready, nmT_copied = sem("nmT_ready"), sem("nmT_copied")
        out_copied, out_stored = sem("out_copied"), [sem(f"out_stored{i}") for i in range(2)]
        LOADED = 16 * (2 * len(Q_PARTS) + 1)

        def loop(eng, step):
            with eng.Fori(0, BATCHES - 1) as b:
                for g in range(GROUPS):
                    step(b, g, False)
            for g in range(GROUPS):
                step(BATCHES - 1, g, True)

        block = ctx.enter_context(nc.Block())

        @block.sync
        def _(sp):
            sp.dma_start(ident[:, :], io["ident"]).then_inc(ident_in, 16)

            def load(b, g):
                for op, dst, order in ((0, qst, Q_PARTS), (1, kst, K_PARTS)):
                    for i, part in enumerate(order):
                        row = (g % 2) * HG * HD
                        src = scratch["parts"][b, part, KT * op + g // 2, row:row + HG * HD, :]
                        sp.dma_start(dst[g][i * HD:(i + 1) * HD, :, :],
                                     src.rearrange("(h d) t -> d h t", d=HD)).then_inc(stack_in[g], 16)
                sp.dma_start(vst[g][:, :, :], scratch["v"][b, :, g * HG * VW:(g + 1) * HG * VW]
                             .rearrange("(t p) n -> p t n", p=P)).then_inc(stack_in[g], 16)

            def send_max(n, g, i, before=None):
                sp.wait_ge(nmT_copied, n)
                if before is not None:
                    sp.wait_ge(max_in[(g - 1) % GROUPS], before)
                sp.dma_start(scratch["max"], nmT[i][:, :]).then_inc(max_out, 16)
                sp.wait_ge(max_out, 16 * n)
                sp.dma_start(qst[g][STACK:STACKM, :, :],
                             scratch["max"].rearrange("(a h) t -> a h t", a=2)).then_inc(max_in[g], 16)

            for g in range(GROUPS):
                load(0, g)
            send_max(1, 0, 0)

            def step(b, g, last):
                if not (last and g == GROUPS - 1):
                    send_max(GROUPS * b + g + 2, (g + 1) % GROUPS, (g + 1) % 2, 16 * b + 16)
                sp.wait_ge(out_copied, GROUPS * b + g + 1)
                sp.wait_ge(ident_in, 16)
                sp.dma_start(scratch["outT"][b, g], outT[g % 2][:, :]).then_inc(out_stored[g % 2], 16)
                if not last:
                    sp.wait_ge(probs_used[TILES - 1], GROUPS * b + g + 1)
                    sp.wait_ge(ident_in, 16)
                    load(b + 1, g)

            loop(sp, step)
            for i in range(2):
                sp.wait_ge(out_stored[i], 8 * BATCHES * GROUPS)

        @block.gpsimd
        def _(pool):
            for g in range(GROUPS):
                nc.gpsimd.memset(kst[g][STACK:STACKM, :, :], 1.0).then_inc(ones, 1)

        @block.scalar
        def _(act):
            def step(b, g, last):
                for k in range(TILES):
                    act.wait_ge(probs_used[k], GROUPS * b + g)
                    for i in range(2):
                        act.wait_ge(scores_ready, 8 * (GROUPS * b + g) + 2 * k + i + 1)
                        nc.scalar.activation(probs[k][:, 2 * i:2 * i + 2, :], psE[i][:, :, :], ACT.Exp,
                                             scale=float(HD) ** -0.5).then_inc(scores_used[i], 1)

            loop(act, step)

        @block.vector
        def _(dve):
            dve.wait_ge(ident_in, 16)
            nc.vector.tensor_copy(identb[:, :], ident[:, :]).then_inc(identb_done, 1)

            def reduce(n, i, t):
                for h in range(HG):
                    dve.wait_ge(rows_ready, 16 * n + HG * t + h + 1)
                    nc.vector.tensor_reduce(negmax[i][:, t, h:h + 1], psM[h % 2][:, :], AX_X, ALU.max,
                                            negate=True).then_inc(rows_used[h % 2], 1)

            def split_max(n, i, reused=True):
                if reused:
                    dve.wait_ge(nmT_ready, n - 1)
                dve.wait_ge(rows_used[0], 8 * n + 8)
                dve.wait_ge(rows_used[1], 8 * n + 8)
                nc.vector.tensor_copy(nmparts[i][:, :, 0, :], negmax[i][:, :, :]).then_inc(negmax_hi, 1)
                dve.wait_ge(negmax_hi, n + 1)
                nc.vector.tensor_tensor(nmparts[i][:, :, 1, :], negmax[i][:, :, :], nmparts[i][:, :, 0, :],
                                        ALU.subtract).then_inc(negmax_parts, 1)

            for t in range(TILES):
                reduce(0, 0, t)
            split_max(0, 0, reused=False)
            for t in range(TILES):
                reduce(1, 1, t)
            dve.wait_ge(nmT_ready, 1)
            nc.vector.tensor_copy(nmT[0][:, :], psN[0:2 * HG, :]).then_inc(nmT_copied, 1)
            split_max(1, 1, reused=False)

            def step(b, g, last):
                G = GROUPS * b + g
                ahead = not (last and g >= GROUPS - 2)
                if ahead:
                    reduce(G + 2, g % 2, 0)
                if not (last and g == GROUPS - 1):
                    dve.wait_ge(max_out, 16 * G)
                    dve.wait_ge(nmT_ready, G + 2)
                    nc.vector.tensor_copy(nmT[(g + 1) % 2][:, :], psN[0:2 * HG, :]).then_inc(nmT_copied, 1)
                if ahead:
                    for t in range(1, TILES):
                        reduce(G + 2, g % 2, t)
                    split_max(G + 2, g % 2)
                dve.wait_ge(probs_used[TILES - 1], G + 1)
                dve.wait_ge(out_stored[g % 2], 16 * (2 * b + g // 2))
                nc.vector.tensor_copy(outT[g % 2][:, :], psV[:, :]).then_inc(out_copied, 1)

            loop(dve, step)

        @block.tensor
        def _(pe):
            def rows(n, g, t, b):
                if t == 0:
                    pe.wait_ge(stack_in[g], LOADED * (b + 1))
                for h in range(HG):
                    pe.wait_ge(rows_used[h % 2], 8 * n + 2 * t + h // 2)
                    nc.tensor.matmul(psM[h % 2][:, :], qst[g][0:STACK, h, t * P:(t + 1) * P], kst[g][0:STACK, h, :],
                                     start=True, stop=True).then_inc(rows_ready, 1)

            def turn_max(n, i):
                pe.wait_ge(negmax_parts, n + 1)
                pe.wait_ge(nmT_copied, n)
                for t in range(TILES):
                    mm = nc.tensor.transpose(psN[0:2 * HG, t * P:(t + 1) * P],
                                             nmparts[i][:, t, :, :].rearrange("p a h -> p (a h)"), identb[:, :])
                mm.then_inc(nmT_ready, 1)

            for g in range(2):
                for t in range(TILES):
                    rows(g, g, t, 0)
            pe.wait_ge(identb_done, 1)
            turn_max(0, 0)
            pe.wait_ge(ones, GROUPS)

            def step(b, g, last):
                G = GROUPS * b + g
                pe.wait_ge(max_in[g], 16 * b + 16)
                pe.wait_ge(ones, GROUPS)

                def values(k):
                    for i in range(2):
                        pe.wait_ge(scores_used[i], TILES * G + k + 1)
                    if k == 0:
                        pe.wait_ge(out_copied, G)
                    for h in range(HG):
                        mm = nc.tensor.matmul(psV[VW * h:VW * (h + 1), :], vst[g][:, k, VW * h:VW * (h + 1)],
                                              probs[k][:, h, :], start=k == 0, stop=k == TILES - 1,
                                              tile_position=(0, VW * h), skip_group_check=True)
                    mm.then_inc(probs_used[k], 1)
                    return mm

                for k in range(TILES):
                    for i in range(2):
                        pe.wait_ge(scores_used[i], TILES * G + k)
                        for h in (2 * i, 2 * i + 1):
                            mm = nc.tensor.matmul(psE[i][:, h % 2, :], kst[g][0:STACKM, h, k * P:(k + 1) * P],
                                                  qst[g][0:STACKM, h, :], start=True, stop=True)
                        mm.then_inc(scores_ready, 1)
                    if k == 1 and not (last and g == GROUPS - 1):
                        turn_max(G + 1, (g + 1) % 2)
                    if not (last and g >= GROUPS - 2):
                        rows(G + 2, (g + 2) % GROUPS, k, b if g < 2 else b + 1)
                    if k:
                        values(k - 1)
                values(TILES - 1)

            loop(pe, step)


RW = E + HD


def layer1_front(nc, io, scratch, keep):
    with ExitStack() as ctx:
        def sb(name, shape, dt=F32):
            return ctx.enter_context(nc.sbuf_tensor("c_" + name, shape, dt))

        def sem(name):
            return stage_semaphore(nc, keep, "c_" + name)

        xacc, mem, xT1, comb1 = keep["xacc"], keep["mem"], keep["xT1"], keep["comb1"]
        norm, routing = Norm(nc, sb, sem), Routing(nc, sb, sem)
        ident, sel = sb("ident", [P, P]), sb("sel", [P, HG * (HD + 1)])
        g16, omg16 = sb("g16", [P, HEADS]), sb("omg16", [P, HEADS])
        after, before = sb("after", [P, P]), sb("before", [P, 1])
        ldrows, ldall = sb("ldrows", [P, KT]), sb("ldall", [P, HEADS])
        qdec, kdec = sb("qdec", [P, KT, P]), sb("kdec", [P, HEADS])
        wo, wg2 = sb("wo", [P, KT, D]), sb("wg2", [HD, D])
        rqk, rkv, rr = sb("rqk", [P, KT, 2 * D]), sb("rkv", [P, KT, 2 * D]), sb("rr", [P, KT, RW])
        wqk = [sb(f"wqk{i}", [P, KT, 2 * D], F32R) for i in range(2)]
        wkv = [sb(f"wkv{i}", [P, KT, 2 * D], F32R) for i in range(2)]
        wr = [sb(f"wr{i}", [P, KT, RW], F32R) for i in range(2)]
        outT, qf = sb("outT", [P, GROUPS, SEQ]), sb("qf", [P, KT, SEQ])
        r1, r2 = sb("r1", [P, TILES, HEADS]), sb("r2", [P, TILES, HEADS])
        t1, t2 = sb("t1", [P, TILES, D]), sb("t2", [P, TILES, D])
        combT, xn = sb("combT", [P, KT, SEQ]), sb("xn", [P, TILES, D])
        xT = [sb(f"xT{i}", [P, KT, SEQ], F32R) for i in range(2)]
        qk, kv = sb("qk", [P, 2 * KT, SEQ]), sb("kv", [P, TILES, 2 * D])
        parts = [sb(f"part{i}", [P, 2 * KT, SEQ], BF16) for i in range(3)]
        low, lowT, sg = sb("low", [P, TILES, HD]), sb("lowT", [HD, SEQ]), sb("sg", [P, TILES, D])
        qd, kd = sb("qd", [P, KT, SEQ]), sb("kd", [P, TILES, D])

        psA = ctx.enter_context(nc.psum_tensor("c_psA", [P, 4, SEQ], F32))
        psB = ctx.enter_context(nc.psum_tensor("c_psB", [P, 4, SEQ], F32))
        S = {}

        def s(name):
            if name not in S:
                S[name] = sem(name)
            return S[name]

        for n in ("consts_in weights_in w_hi w_lo tables g_done omg_done att_in heads_ps recips scaled terms combined combT_ps "
                  "combT_done y_ps residual xT_ps xhi xlo kept qkT_ps kv_ps silu_qk silu_kv p1 r1d p2 p3 low_ps "
                  "low_done lowT_ps lowT_done gate_ps gate_done qd_done kd_done stored").split():
            s(n)

        block = ctx.enter_context(nc.Block())

        @block.sync
        def _(sp):
            for dst, src in ((ident[:, :], io["ident"]), (sel[:, :], io["sel17"]), (after[:, :], io["after"]),
                             (before[:, :], io["before"]), (ldrows[:, :], io["log_decay_rows"]),
                             (ldall[:, :], io["log_decay"].to_broadcast((P, HEADS))),
                             (g16[:, :], io["gate_attn"].to_broadcast((P, HEADS)))):
                sp.dma_start(dst, src).then_inc(s("consts_in"), 16)
            routing.load(sp, io)
            for dst, src in ((rqk[:, :, 0:D], "Wq1"), (rqk[:, :, D:2 * D], "Wk1"), (rkv[:, :, 0:D], "Wk1"),
                             (rkv[:, :, D:2 * D], "Wv1"), (rr[:, :, 0:E], "router1"), (rr[:, :, E:RW], "Wg1"),
                             (wo[:, :, :], "Wo0")):
                sp.dma_start(dst, io[src].rearrange("(k p) n -> p k n", p=P)).then_inc(s("weights_in"), 16)
            sp.dma_start(wg2[:, :], io["Wg2"]).then_inc(s("weights_in"), 16)
            with sp.Fori(0, BATCHES) as b:
                sp.wait_ge(s("consts_in"), 112)
                sp.wait_ge(s("heads_ps"), b)
                sp.dma_start(outT[:, :, :], scratch["outT"][b].rearrange("g p n -> p g n")).then_inc(s("att_in"), 16)
                sp.dma_start(qf[:, :, :], scratch["qf"][b].rearrange("k p n -> p k n")).then_inc(s("att_in"), 16)
                sp.wait_ge(s("consts_in"), 112)
                sp.wait_ge(s("silu_kv"), b + 1)
                sp.dma_start(scratch["v1"][b].rearrange("(t p) n -> p t n", p=P), kv[:, :, D:2 * D]).then_inc(s("stored"), 16)
                sp.wait_ge(s("consts_in"), 112)
                sp.wait_ge(s("kd_done"), b + 1)
                sp.dma_start(scratch["kd"][b].rearrange("(t p) n -> p t n", p=P), kd[:, :, :]).then_inc(s("stored"), 16)
                sp.wait_ge(s("consts_in"), 112)
                sp.wait_ge(s("qd_done"), b + 1)
                sp.dma_start(scratch["qd"][b].rearrange("k p n -> p k n"), qd[:, :, :]).then_inc(s("stored"), 16)
                for i, done in enumerate(("p1", "p2", "p3")):
                    sp.wait_ge(s("consts_in"), 112)
                    sp.wait_ge(s(done), b + 1)
                    sp.dma_start(scratch["parts1"][b, i].rearrange("k p n -> p k n"), parts[i][:, :, :]).then_inc(s("stored"), 16)
                sp.wait_ge(s("consts_in"), 112)
                sp.wait_ge(s("gate_done"), b + 1)
                sp.dma_start(scratch["sg"][b].rearrange("(t p) n -> p t n", p=P), sg[:, :, :]).then_inc(s("stored"), 16)
            sp.wait_ge(s("stored"), 7 * 16 * BATCHES)

        STORES = 7 * 16

        @block.gpsimd
        def _(pool):
            norm.setup(pool)
            with pool.Fori(0, BATCHES) as b:
                norm.power(pool, b)
                pool.wait_ge(s("xhi"), b + 1)
                pool.wait_ge(s("xlo"), b + 1)
                pool.wait_ge(norm.neghalf_set, 1)
                for i in range(2):
                    nc.gpsimd.tensor_copy(xT1[i][:, :, bass.ds(b * SEQ, SEQ)], xT[i][:, :, :].bitcast(F32)).then_inc(s("kept"), 1)
                pool.wait_ge(s("p1"), b + 1)
                pool.wait_ge(s("qd_done"), b + 1)
                nc.gpsimd.tensor_tensor(qk[:, :, :], qk[:, :, :], parts[0][:, :, :], ALU.subtract).then_inc(s("r1d"), 1)
                pool.wait_ge(s("p2"), b + 1)
                nc.gpsimd.tensor_tensor(parts[2][:, :, :], qk[:, :, :], parts[1][:, :, :], ALU.subtract).then_inc(s("p3"), 1)

        @block.scalar
        def _(act):
            act.wait_ge(s("consts_in"), 112)
            for k in range(KT):
                nc.scalar.activation(qdec[:, k, :], after[:, :], ACT.Exp, scale=ldrows[:, k:k + 1]).then_inc(s("tables"), 1)
            nc.scalar.activation(kdec[:, :], ldall[:, :], ACT.Exp, scale=before[:, 0:1]).then_inc(s("tables"), 1)
            nc.scalar.activation(g16[:, :], g16[:, :], ACT.Sigmoid).then_inc(s("g_done"), 1)
            act.wait_ge(s("weights_in"), 128)
            for dst, src in ((wqk, rqk), (wkv, rkv), (wr, rr)):
                nc.scalar.activation(dst[0][:, :, :], src[:, :, :], ACT.Copy).then_inc(s("w_hi"), 1)
            with act.Fori(0, BATCHES) as b:
                act.wait_ge(s("combT_ps"), b + 1)
                nc.scalar.activation(combT[:, :, :], psA[:, 0:KT, :], ACT.Copy).then_inc(s("combT_done"), 1)
                act.wait_ge(s("xT_ps"), b + 1)
                act.wait_ge(s("kept"), 2 * b)
                nc.scalar.activation(xT[0][:, :, :], psA[:, 2:4, :], ACT.Copy).then_inc(s("xhi"), 1)
                act.wait_ge(s("qkT_ps"), b + 1)
                act.wait_ge(s("stored"), STORES * b)
                nc.scalar.activation(qk[:, :, :], psB[:, :, :], ACT.Silu).then_inc(s("silu_qk"), 1)
                act.wait_ge(s("kv_ps"), b + 1)
                nc.scalar.activation(kv[:, :, :], psA[:, :, :], ACT.Silu).then_inc(s("silu_kv"), 1)
                act.wait_ge(s("silu_qk"), b + 1)
                nc.scalar.activation(parts[0][:, :, :], qk[:, :, :], ACT.Copy).then_inc(s("p1"), 1)
                act.wait_ge(s("r1d"), b + 1)
                nc.scalar.activation(parts[1][:, :, :], qk[:, :, :], ACT.Copy).then_inc(s("p2"), 1)
                routing.exp(act, b)
                act.wait_ge(s("gate_ps"), b + 1)
                nc.scalar.activation(sg[:, :, :], psB[:, 1:3, :].rearrange("p a (t n) -> p (a t) n", n=D),
                                     ACT.Sigmoid).then_inc(s("gate_done"), 1)

        @block.vector
        def _(dve):
            for i, (dst, src) in enumerate(((wqk, rqk), (wkv, rkv), (wr, rr))):
                dve.wait_ge(s("w_hi"), i + 1)
                nc.vector.tensor_tensor(dst[1][:, :, :], src[:, :, :], dst[0][:, :, :].bitcast(F32), ALU.subtract).then_inc(s("w_lo"), 1)
            dve.wait_ge(s("g_done"), 1)
            nc.vector.tensor_scalar(omg16[:, :], g16[:, :], -1.0, 1.0, ALU.mult, ALU.add).then_inc(s("omg_done"), 1)
            dve.wait_ge(s("omg_done"), 1)
            dve.wait_ge(s("tables"), 3)
            with dve.Fori(0, BATCHES) as b:
                dve.wait_ge(s("heads_ps"), b + 1)
                soft = psA[:, :, 0:HEADS * (HD + 1)].rearrange("p t (h w) -> p t h w", w=HD + 1)
                lin = [psB[:, :, MW * k:MW * (k + 1)] for k in range(KT)]
                nc.vector.reciprocal(r1[:, :, :], soft[:, :, :, HD]).then_inc(s("recips"), 1)
                for k in range(KT):
                    nc.vector.reciprocal(r2[:, :, k * HH:(k + 1) * HH], lin[k][:, :, P:MW]).then_inc(s("recips"), 1)
                dve.wait_ge(s("recips"), 3 * b + 3)
                nc.vector.tensor_tensor(r1[:, :, :], r1[:, :, :], omg16[:, :].unsqueeze(1).to_broadcast((P, TILES, HEADS)), ALU.mult).then_inc(s("scaled"), 1)
                nc.vector.tensor_tensor(r2[:, :, :], r2[:, :, :], g16[:, :].unsqueeze(1).to_broadcast((P, TILES, HEADS)), ALU.mult).then_inc(s("scaled"), 1)
                dve.wait_ge(s("scaled"), 2 * b + 2)
                nc.vector.tensor_tensor(t1[:, :, :].rearrange("p t (h e) -> p t h e", e=HD), soft[:, :, :, 0:HD],
                                        r1[:, :, :].unsqueeze(3).to_broadcast((P, TILES, HEADS, HD)), ALU.mult).then_inc(s("terms"), 1)
                for k in range(KT):
                    nc.vector.tensor_tensor(t2[:, :, k * P:(k + 1) * P].rearrange("p t (h e) -> p t h e", e=HD),
                                            lin[k][:, :, 0:P].rearrange("p t (h e) -> p t h e", e=HD),
                                            r2[:, :, k * HH:(k + 1) * HH].unsqueeze(3).to_broadcast((P, TILES, HH, HD)),
                                            ALU.mult).then_inc(s("terms"), 1)
                dve.wait_ge(s("terms"), 3 * b + 3)
                nc.vector.tensor_tensor(t1[:, :, :], t1[:, :, :], t2[:, :, :], ALU.add).then_inc(s("combined"), 1)
                dve.wait_ge(s("y_ps"), b + 1)
                x = xacc[:, bass.ds(b * TILES, TILES), :]
                nc.vector.tensor_tensor(x, psB[:, :, 0:D], x, ALU.add).then_inc(s("residual"), 1)
                dve.wait_ge(s("omg_done"), 1)
                dve.wait_ge(s("residual"), b + 1)
                norm.vector(dve, b, xacc, xn)
                dve.wait_ge(s("xhi"), b + 1)
                dve.wait_ge(s("kept"), 2 * b)
                nc.vector.tensor_tensor(xT[1][:, :, :], psA[:, 2:4, :], xT[0][:, :, :].bitcast(F32), ALU.subtract).then_inc(s("xlo"), 1)
                dve.wait_ge(s("silu_qk"), b + 1)
                dve.wait_ge(s("stored"), STORES * b)
                nc.vector.tensor_tensor(qd[:, :, :].rearrange("p k (c n) -> p k c n", n=CH),
                                        qk[:, 0:KT, :].rearrange("p k (c n) -> p k c n", n=CH),
                                        qdec[:, :, :].unsqueeze(2).to_broadcast((P, KT, SEQ // CH, CH)), ALU.mult).then_inc(s("qd_done"), 1)
                dve.wait_ge(s("silu_kv"), b + 1)
                nc.vector.tensor_tensor(kd[:, :, :].rearrange("p t (h e) -> p t h e", e=HD),
                                        kv[:, :, 0:D].rearrange("p t (h e) -> p t h e", e=HD),
                                        kdec[:, :].unsqueeze(1).unsqueeze(3).to_broadcast((P, TILES, HEADS, HD)), ALU.mult).then_inc(s("kd_done"), 1)
                dve.wait_ge(s("low_ps"), b + 1)
                small = psB[:, 0, 0:TILES * RW].rearrange("p (t n) -> p t n", n=RW)
                nc.vector.tensor_copy(low[:, :, :], small[:, :, E:RW]).then_inc(s("low_done"), 1)
                dve.wait_ge(s("lowT_ps"), b + 1)
                nc.vector.tensor_copy(lowT[:, :], psB[0:HD, 3, :]).then_inc(s("lowT_done"), 1)
                routing.vector(dve, b, small[:, :, 0:E], comb1[:, bass.ds(b * TILES, TILES), :])

        @block.tensor
        def _(pe):
            pe.wait_ge(s("consts_in"), 112)
            pe.wait_ge(s("weights_in"), 128)
            pe.wait_ge(s("w_lo"), 3)
            with pe.Fori(0, BATCHES) as b:
                pe.wait_ge(s("att_in"), 32 * b + 32)
                pe.wait_ge(s("kd_done"), b)
                pe.wait_ge(s("gate_done"), b)
                pe.wait_ge(s("lowT_done"), b)
                pe.wait_ge(routing.copied, b)
                for t in range(TILES):
                    c = slice(t * P, (t + 1) * P)
                    w = HG * (HD + 1)
                    for g in range(GROUPS):
                        nc.tensor.matmul(psA[:, t, g * w:(g + 1) * w], outT[:, g, c], sel[:, :], start=True, stop=True,
                                         skip_group_check=True)
                    for k in range(KT):
                        mm = nc.tensor.matmul(psB[:, t, MW * k:MW * (k + 1)], qf[:, k, c],
                                              mem[:, bass.ds(b * KT + k, 1), :].rearrange("p a n -> p (a n)"),
                                              start=True, stop=True, skip_group_check=True)
                mm.then_inc(s("heads_ps"), 1)
                pe.wait_ge(s("combined"), b + 1)
                for t in range(TILES):
                    for k in range(KT):
                        mm = nc.tensor.transpose(psA[:, k, t * P:(t + 1) * P], t1[:, t, k * P:(k + 1) * P], ident[:, :])
                mm.then_inc(s("combT_ps"), 1)
                pe.wait_ge(s("combT_done"), b + 1)
                for t in range(TILES):
                    for k in range(KT):
                        mm = nc.tensor.matmul(psB[:, t, 0:D], combT[:, k, t * P:(t + 1) * P], wo[:, k, :],
                                              start=k == 0, stop=k == KT - 1)
                mm.then_inc(s("y_ps"), 1)
                pe.wait_ge(norm.xn_done, TILES * b + TILES)
                for t in range(TILES):
                    for k in range(KT):
                        mm = nc.tensor.transpose(psA[:, 2 + k, t * P:(t + 1) * P], xn[:, t, k * P:(k + 1) * P], ident[:, :])
                mm.then_inc(s("xT_ps"), 1)
                pe.wait_ge(s("xlo"), b + 1)
                for m in range(4):
                    c = slice(m * P, (m + 1) * P)
                    mm = three(nc, psB[:, m, :], [(wqk[0][:, k, c], wqk[1][:, k, c], xT[0][:, k, :], xT[1][:, k, :])
                                                  for k in range(KT)])
                mm.then_inc(s("qkT_ps"), 1)
                for t in range(TILES):
                    c = slice(t * P, (t + 1) * P)
                    mm = three(nc, psA[:, t, :], [(xT[0][:, k, c], xT[1][:, k, c], wkv[0][:, k, :], wkv[1][:, k, :])
                                                  for k in range(KT)])
                mm.then_inc(s("kv_ps"), 1)
                pe.wait_ge(s("silu_qk"), b + 1)
                for t in range(TILES):
                    c = slice(t * P, (t + 1) * P)
                    mm = three(nc, psB[:, 0, t * RW:(t + 1) * RW],
                               [(xT[0][:, k, c], xT[1][:, k, c], wr[0][:, k, :], wr[1][:, k, :]) for k in range(KT)])
                mm.then_inc(s("low_ps"), 1)
                pe.wait_ge(s("low_done"), b + 1)
                for t in range(TILES):
                    mm = nc.tensor.transpose(psB[0:HD, 3, t * P:(t + 1) * P], low[:, t, :], ident[:, :])
                mm.then_inc(s("lowT_ps"), 1)
                pe.wait_ge(s("lowT_done"), b + 1)
                for t in range(TILES):
                    mm = nc.tensor.matmul(psB[:, 1 + t // 2, (t % 2) * D:(t % 2 + 1) * D], lowT[:, t * P:(t + 1) * P],
                                          wg2[:, :], start=True, stop=True, skip_group_check=True)
                mm.then_inc(s("gate_ps"), 1)


AHEAD = 2
HSLOTS = 4


def layer1_experts(nc, io, keep):
    with ExitStack() as ctx:
        def sb(name, shape, dt=F32):
            return ctx.enter_context(nc.sbuf_tensor("d_" + name, shape, dt))

        def sem(name):
            return stage_semaphore(nc, keep, "d_" + name)

        xacc, xT, comb1 = keep["xacc"], keep["xT1"], keep["comb1"]
        G, U, DN = KT * H1, KT * H1, HT1 * D
        raw = [sb(f"raw{i}", [P, n]) for i, n in enumerate((G, U, DN))]
        w = [[[sb(f"w{e}{i}{j}", [P, n], F32R) for j in range(2)] for i, n in enumerate((G, U, DN))] for e in range(2)]
        h = [sb(f"h{i}", [P, SEQ]) for i in range(HSLOTS)]
        hh = [[sb(f"hh{i}{j}", [P, SEQ], F32R) for j in range(2)] for i in range(HSLOTS)]
        psG = ctx.enter_context(nc.psum_tensor("d_psG", [P, 4, SEQ], F32))
        psY = [ctx.enter_context(nc.psum_tensor(f"d_psY{i}", [P, TILES, D], F32)) for i in range(2)]

        raw_in, w_hi, w_lo = ([sem(f"{n}{i}") for i in range(3)] for n in ("raw_in", "w_hi", "w_lo"))
        gate_up_ps, silu_done = sem("gate_up_ps"), sem("silu")
        mult_done = [sem(f"mult{i}") for i in range(2)]
        hi_done = sem("hi")
        lo_done, down_ps = ([sem(f"{n}{i}") for i in range(HSLOTS)] for n in ("lo", "down_ps"))
        added = [sem(f"added{i}") for i in range(2)]
        N = BATCHES * HT1
        PAIR = 2 * N

        def loop(eng, experts):
            with eng.Fori(0, E // 2 - 1) as i:
                experts(i, False)
            experts(E // 2 - 1, True)

        def view(t, k):
            return t[:, :].rearrange("p (k n) -> p k n", k=k)

        def other_expert(i, t, last):
            half, piece = t // N, t % N - 1
            if not 0 <= piece < 3 or (last and half):
                return None
            return piece, 2 * i + 1 + half, (PAIR * i + half * N) // HSLOTS if isinstance(i, int) else \
                PAIR // HSLOTS * i + half * N // HSLOTS

        block = ctx.enter_context(nc.Block())

        @block.sync
        def _(sp):
            def load(x):
                for i, (name, k) in enumerate((("gate1", KT), ("up1", KT), ("down1", HT1))):
                    sp.wait_ge(w_lo[i], x)
                    weights = io[name][x] if isinstance(x, int) else io[name][bass.ds(x, 1), :, :].rearrange("a r n -> (a r) n")
                    sp.dma_start(view(raw[i], k), weights.rearrange("(k p) n -> p k n", p=P)).then_inc(raw_in[i], 16)

            load(0)

            def experts(i, last):
                load(2 * i + 1)
                if not last:
                    load(2 * i + 2)

            loop(sp, experts)

        @block.gpsimd
        def _(pool):
            def experts(i, last):
                for t in range(PAIR):
                    s = t % HSLOTS
                    pool.wait_ge(hi_done, PAIR * i + t + 1)
                    nc.gpsimd.tensor_tensor(hh[s][1][:, :], h[s][:, :], hh[s][0][:, :].bitcast(F32),
                                            ALU.subtract).then_inc(lo_done[s], 1)

            loop(pool, experts)

        @block.scalar
        def _(act):
            def split_hi(e, piece, x):
                act.wait_ge(raw_in[piece], 16 * x + 16)
                nc.scalar.activation(w[e][piece][0][:, :], raw[piece][:, :], ACT.Copy).then_inc(w_hi[piece], 1)

            for piece in range(3):
                split_hi(0, piece, 0)

            def experts(i, last):
                for t in range(PAIR):
                    s = t % HSLOTS
                    act.wait_ge(gate_up_ps, PAIR * i + t + 1)
                    act.wait_ge(lo_done[s], PAIR // HSLOTS * i + t // HSLOTS)
                    nc.scalar.activation(h[s][:, :], psG[:, 2 * (t % 2), :], ACT.Silu).then_inc(silu_done, 1)
                    if found := other_expert(i, t, last):
                        act.wait_ge(down_ps[HSLOTS - 1], found[2])
                        split_hi((t // N + 1) % 2, found[0], found[1])
                    act.wait_ge(mult_done[t % 2], PAIR // 2 * i + t // 2 + 1)
                    act.wait_ge(down_ps[s], PAIR // HSLOTS * i + t // HSLOTS)
                    nc.scalar.activation(hh[s][0][:, :], h[s][:, :], ACT.Copy).then_inc(hi_done, 1)

            loop(act, experts)

        @block.vector
        def _(dve):
            def split_lo(e, piece, x):
                dve.wait_ge(w_hi[piece], x + 1)
                nc.vector.tensor_tensor(w[e][piece][1][:, :], raw[piece][:, :], w[e][piece][0][:, :].bitcast(F32),
                                        ALU.subtract).then_inc(w_lo[piece], 1)

            for piece in range(3):
                split_lo(0, piece, 0)

            def add(i, t):
                chunk = t // HT1
                dve.wait_ge(down_ps[HSLOTS - 1], PAIR // HSLOTS * i + t // HSLOTS + 1)
                for k in range(TILES):
                    rows = chunk % BATCHES * TILES + k
                    weight = comb1[:, rows, bass.ds(2 * i + t // N, 1)] if not isinstance(i, int) else \
                        comb1[:, rows, 2 * i + t // N:2 * i + t // N + 1]
                    last = nc.vector.scalar_tensor_tensor(xacc[:, rows, :], psY[chunk % 2][:, k, :], weight,
                                                          xacc[:, rows, :], ALU.mult, ALU.add)
                last.then_inc(added[chunk % 2], 1)

            def experts(i, last):
                for t in range(PAIR):
                    s = t % HSLOTS
                    dve.wait_ge(silu_done, PAIR * i + t + 1)
                    nc.vector.tensor_tensor(h[s][:, :], h[s][:, :], psG[:, 2 * (t % 2) + 1, :],
                                            ALU.mult).then_inc(mult_done[t % 2], 1)
                    if found := other_expert(i, t, last):
                        split_lo((t // N + 1) % 2, found[0], found[1])
                    if t % HT1 == AHEAD and t > HT1:
                        add(i, t - AHEAD - 1)
                add(i, PAIR - 1)

            loop(dve, experts)

        @block.tensor
        def _(pe):
            def gate_up(i, t):
                if t % N == 0:
                    for piece in range(2):
                        pe.wait_ge(w_lo[piece], 2 * i + t // N + 1)
                pe.wait_ge(mult_done[t % 2], PAIR // 2 * i + t // 2)
                m, chunk = t % HT1, t // HT1 % BATCHES
                for j in range(2):
                    hi, lo = (view(x, KT)[:, :, m * P:(m + 1) * P] for x in w[t // N][j])
                    c = slice(chunk * SEQ, (chunk + 1) * SEQ)
                    mm = three(nc, psG[:, 2 * (t % 2) + j, :], [(hi[:, k, :], lo[:, k, :], xT[0][:, k, c], xT[1][:, k, c])
                                                                for k in range(KT)])
                mm.then_inc(gate_up_ps, 1)

            def down(i, t):
                s, m, chunk = t % HSLOTS, t % HT1, t // HT1
                if t % N == 0:
                    pe.wait_ge(w_lo[2], 2 * i + t // N + 1)
                if m == 0:
                    pe.wait_ge(added[chunk % 2], PAIR // HT1 // 2 * i + chunk // 2)
                pe.wait_ge(lo_done[s], PAIR // HSLOTS * i + t // HSLOTS + 1)
                hi, lo = (view(x, HT1)[:, m, :] for x in w[t // N][2])
                for k in range(TILES):
                    c = slice(k * P, (k + 1) * P)
                    mm = three(nc, psY[chunk % 2][:, k, :], [(hh[s][0][:, c], hh[s][1][:, c], hi, lo)],
                               start=m == 0 and k % 2 == 0, last=m == HT1 - 1)
                mm.then_inc(down_ps[s], 1)

            for t in range(AHEAD):
                gate_up(0, t)

            def experts(i, last):
                for t in range(PAIR):
                    if t + AHEAD < PAIR:
                        gate_up(i, t + AHEAD)
                    elif not last:
                        gate_up(i + 1, t + AHEAD - PAIR)
                    down(i, t)

            loop(pe, experts)


NC = SEQ // CH
UPDATES = 2 * (NC - 1)
PASS = 2 * NC


def layer1_attention(nc, io, scratch, keep, out):
    with ExitStack() as ctx:
        def sb(name, shape, dt=F32):
            return ctx.enter_context(nc.sbuf_tensor("e_" + name, shape, dt))

        def sem(name):
            return stage_semaphore(nc, keep, "e_" + name)

        xacc = keep["xacc"]
        ident, sel, blockmask = sb("ident", [P, P]), sb("sel", [P, HG * HD]), sb("blockmask", [P, P])
        rel, causal = sb("rel", [P, P]), sb("causal", [P, P])
        ldall, ldrows, cdec = sb("ldall", [P, HEADS]), sb("ldrows", [P, KT]), sb("cdec", [P, KT])
        normw, neghalf, wo = sb("normw", [P, D]), sb("neghalf", [P, HEADS]), sb("wo", [P, KT, D])
        decay = sb("decay", [P, HEADS, CH])
        qst = [[sb(f"qst{p}{g}", [STACK, HG, SEQ], BF16) for g in range(GROUPS)] for p in range(2)]
        kst = [[sb(f"kst{p}{g}", [STACK, HG, SEQ], BF16) for g in range(GROUPS)] for p in range(2)]
        v, kd, sg = ([sb(f"{n}{p}", [P, NC, D]) for p in range(2)] for n in ("v", "kd", "sg"))
        qd = [sb(f"qd{p}", [P, KT, SEQ]) for p in range(2)]
        probs = [sb(f"probs{g}", [P, HG * CH]) for g in range(GROUPS)]
        headsT = sb("headsT", [P, GROUPS * CH])
        state, update = sb("state", [P, KT, P]), sb("update", [P, KT, P])
        o, sq, ss, rs = sb("o", [P, D]), sb("sq", [P, D]), sb("ss", [P, HEADS]), sb("rs", [P, HEADS])
        normed, normT = [sb(f"normed{i}", [P, D]) for i in range(2)], sb("normT", [P, KT, P])

        psS = [ctx.enter_context(nc.psum_tensor(f"e_psS{g}", [P, HG * CH], F32)) for g in range(GROUPS)]
        psH = ctx.enter_context(nc.psum_tensor("e_psH", [P, GROUPS * CH], F32))
        psO = ctx.enter_context(nc.psum_tensor("e_psO", [P, D], F32))
        psK = ctx.enter_context(nc.psum_tensor("e_psK", [P, 2 * KT, P], F32))
        psY = ctx.enter_context(nc.psum_tensor("e_psY", [P, D], F32))

        consts_in, tables, masked, cleared, cdec_done = (sem(n) for n in ("consts_in", "tables", "masked", "cleared", "cdec"))
        neghalf_set = sem("neghalf")
        heads_in, rows_in = [sem(f"heads_in{p}") for p in range(2)], [sem(f"rows_in{p}") for p in range(2)]
        scores_ps = [sem(f"scores_ps{g}") for g in range(GROUPS)]
        probs_done = [sem(f"probs{g}") for g in range(GROUPS)]
        probs_used = [sem(f"probs_used{g}") for g in range(GROUPS)]
        heads_copied, update_ps, update_done, state_done = (sem(n) for n in ("heads_copied", "update_ps", "update", "state"))
        out_ps, squared, summed, ss_done, rs_done = (sem(n) for n in ("out_ps", "squared", "summed", "ss", "rs"))
        gated = [sem(f"gated{p}") for p in range(2)]
        scaled, normed_done, normT_ps, normT_done, y_ps, y_done = (
            sem(n) for n in ("scaled", "normed", "normT_ps", "normT", "y_ps", "y"))
        stored = sem("stored")

        block = ctx.enter_context(nc.Block())

        @block.sync
        def _(sp):
            for dst, src in ((ident[:, :], io["ident"]), (sel[:, :], io["sel16"]), (blockmask[:, :], io["blockmask"]),
                             (rel[:, :], io["rel"]), (causal[:, :], io["causal"]),
                             (ldall[:, :], io["log_decay"].to_broadcast((P, HEADS))), (ldrows[:, :], io["log_decay_rows"]),
                             (normw[:, :], io["norm_w"].to_broadcast((P, D))),
                             (wo[:, :, :], io["Wo1"].rearrange("(k p) n -> p k n", p=P))):
                sp.dma_start(dst, src).then_inc(consts_in, 16)
            with sp.Fori(0, BATCHES // 2) as i:
                for p in range(2):
                    b = 2 * i + p
                    sp.wait_ge(gated[p], NC * i)
                    for g in range(GROUPS):
                        for op, dst, order in ((0, qst, Q_PARTS), (1, kst, K_PARTS)):
                            for n, part in enumerate(order):
                                row = (g % 2) * HG * HD
                                sp.dma_start(dst[p][g][n * HD:(n + 1) * HD, :, :],
                                             scratch["parts1"][b, part, KT * op + g // 2, row:row + HG * HD, :]
                                             .rearrange("(h d) t -> d h t", d=HD)).then_inc(heads_in[p], 16)
                    for dst, name in ((v, "v1"), (kd, "kd"), (sg, "sg")):
                        sp.dma_start(dst[p][:, :, :], scratch[name][b].rearrange("(t p) n -> p t n", p=P)).then_inc(rows_in[p], 16)
                    sp.dma_start(qd[p][:, :, :], scratch["qd"][b].rearrange("k p n -> p k n")).then_inc(rows_in[p], 16)
                for n in range(PASS):
                    sp.wait_ge(y_done, PASS * i + n + 1)
                    sp.dma_start(out[bass.ds((PASS * i + n) * P, P), :],
                                 xacc[:, bass.ds(PASS * i + n, 1), :].rearrange("p a d -> p (a d)")).then_inc(stored, 16)
            sp.wait_ge(stored, 16 * TOK // P)

        HEADS_IN = 16 * GROUPS * 2 * len(Q_PARTS)

        @block.gpsimd
        def _(pool):
            nc.gpsimd.memset(neghalf[:, :], -0.5).then_inc(neghalf_set, 1)
            pool.wait_ge(neghalf_set, 1)
            with pool.Fori(0, BATCHES // 2) as i:
                for n in range(PASS):
                    pool.wait_ge(ss_done, PASS * i + n + 1)
                    nc.gpsimd.tensor_tensor(rs[:, :], ss[:, :], neghalf[:, :], ALU.pow).then_inc(rs_done, 1)

        @block.scalar
        def _(act):
            act.wait_ge(consts_in, 144)
            for h in range(HEADS):
                nc.scalar.activation(decay[:, h, :], rel[:, :], ACT.Exp, scale=ldall[:, h:h + 1]).then_inc(tables, 1)
            nc.scalar.activation(cdec[:, :], ldrows[:, :], ACT.Exp, scale=float(CH)).then_inc(cdec_done, 1)
            with act.Fori(0, BATCHES // 2) as i:
                def turn(n):
                    act.wait_ge(normT_ps, PASS * i + n + 1)
                    act.wait_ge(y_ps, PASS * i + n)
                    nc.scalar.activation(normT[:, :, :], psK[:, KT:2 * KT, :], ACT.Copy).then_inc(normT_done, 1)

                for n in range(PASS):
                    if n:
                        turn(n - 1)
                    for g in range(GROUPS):
                        act.wait_ge(probs_used[g], PASS * i + n + 1)
                    act.wait_ge(out_ps, PASS * i + n)
                    nc.scalar.activation(headsT[:, :], psH[:, :], ACT.Copy).then_inc(heads_copied, 1)
                turn(PASS - 1)

        @block.vector
        def _(dve):
            nc.vector.memset(psH[:, :], 0.0).then_inc(cleared, 1)
            dve.wait_ge(tables, HEADS)
            nc.vector.tensor_tensor(decay[:, :, :], decay[:, :, :], causal[:, :].unsqueeze(1).to_broadcast((P, HEADS, CH)),
                                    ALU.mult).then_inc(masked, 1)
            dve.wait_ge(cdec_done, 1)
            dve.wait_ge(masked, 1)
            with dve.Fori(0, BATCHES // 2) as i:
                def weigh(n):
                    for g in range(GROUPS):
                        dve.wait_ge(scores_ps[g], PASS * i + n + 1)
                        dve.wait_ge(probs_used[g], PASS * i + n)
                        nc.vector.tensor_tensor(probs[g][:, :], psS[g][:, :],
                                                decay[:, HG * g:HG * g + HG, :].rearrange("p h c -> p (h c)"),
                                                ALU.mult).then_inc(probs_done[g], 1)

                def residual(n):
                    dve.wait_ge(y_ps, PASS * i + n + 1)
                    x = xacc[:, bass.ds(PASS * i + n, 1), :].rearrange("p a d -> p (a d)")
                    nc.vector.tensor_tensor(x, psY[:, :], x, ALU.add).then_inc(y_done, 1)

                weigh(0)
                for n in range(PASS):
                    p, c = n // NC, n % NC
                    if c < NC - 1:
                        dve.wait_ge(update_ps, UPDATES * i + 3 * p + c + 1)
                        if c == 0:
                            dve.wait_ge(out_ps, PASS * i + n)
                        nc.vector.tensor_tensor((update if c else state)[:, :, :], psK[:, 0:KT, :],
                                                blockmask[:, :].unsqueeze(1).to_broadcast((P, KT, P)),
                                                ALU.mult).then_inc(update_done, 1)
                    if n + 1 < PASS:
                        weigh(n + 1)
                    dve.wait_ge(out_ps, PASS * i + n + 1)
                    nc.vector.tensor_tensor(o[:, :], psO[:, :], sg[p][:, c, :], ALU.mult).then_inc(gated[p], 1)
                    if 0 < c < NC - 1:
                        dve.wait_ge(update_done, UPDATES * i + 3 * p + c + 1)
                        dve.wait_ge(state_done, 4 * i + 2 * p + c - 1)
                        for k in range(KT):
                            last = nc.vector.scalar_tensor_tensor(state[:, k, :], state[:, k, :], cdec[:, k:k + 1], update[:, k, :],
                                                                  ALU.mult, ALU.add)
                        last.then_inc(state_done, 1)
                    dve.wait_ge(gated[p], NC * i + c + 1)
                    nc.vector.tensor_tensor(sq[:, :], o[:, :], o[:, :], ALU.mult).then_inc(squared, 1)
                    dve.wait_ge(squared, PASS * i + n + 1)
                    nc.vector.tensor_reduce(ss[:, :], sq[:, :].rearrange("p (h d) -> p h d", d=HD), AX_X, ALU.add).then_inc(summed, 1)
                    dve.wait_ge(summed, PASS * i + n + 1)
                    nc.vector.tensor_scalar(ss[:, :], ss[:, :], 1.0 / HD, EPS, ALU.mult, ALU.add).then_inc(ss_done, 1)
                    if n:
                        residual(n - 1)
                    dve.wait_ge(rs_done, PASS * i + n + 1)
                    nc.vector.tensor_tensor(o[:, :].rearrange("p (h d) -> p h d", d=HD), o[:, :].rearrange("p (h d) -> p h d", d=HD),
                                            rs[:, :].unsqueeze(2).to_broadcast((P, HEADS, HD)), ALU.mult).then_inc(scaled, 1)
                    dve.wait_ge(scaled, PASS * i + n + 1)
                    nc.vector.tensor_tensor(normed[n % 2][:, :], o[:, :], normw[:, :], ALU.mult).then_inc(normed_done, 1)
                residual(PASS - 1)

        @block.tensor
        def _(pe):
            pe.wait_ge(consts_in, 144)
            pe.wait_ge(cleared, 1)
            with pe.Fori(0, BATCHES // 2) as i:
                def scores(n, g):
                    p, c = n // NC, slice(n % NC * CH, (n % NC + 1) * CH)
                    if g == 0 and n % NC == 0:
                        pe.wait_ge(heads_in[p], HEADS_IN * i + HEADS_IN)
                    pe.wait_ge(probs_done[g], PASS * i + n)
                    for h in range(HG):
                        mm = nc.tensor.matmul(psS[g][:, h * CH:(h + 1) * CH], kst[p][g][:, h, c], qst[p][g][:, h, c],
                                              start=True, stop=True, skip_group_check=True)
                    mm.then_inc(scores_ps[g], 1)

                def turn(n):
                    pe.wait_ge(update_done, UPDATES * i + 3 * (n // NC) + min(n % NC + 1, 3))
                    pe.wait_ge(normed_done, PASS * i + n + 1)
                    pe.wait_ge(normT_done, PASS * i + n)
                    for k in range(KT):
                        mm = nc.tensor.transpose(psK[:, KT + k, :], normed[n % 2][:, k * P:(k + 1) * P], ident[:, :])
                    mm.then_inc(normT_ps, 1)

                def project(n):
                    pe.wait_ge(normT_done, PASS * i + n + 1)
                    pe.wait_ge(y_done, PASS * i + n)
                    for k in range(KT):
                        mm = nc.tensor.matmul(psY[:, :], normT[:, k, :], wo[:, k, :], start=k == 0, stop=k == KT - 1)
                    mm.then_inc(y_ps, 1)

                for g in range(GROUPS):
                    scores(0, g)
                for n in range(PASS):
                    p, c = n // NC, n % NC
                    if c == 0:
                        pe.wait_ge(rows_in[p], 64 * i + 64)
                    if n:
                        turn(n - 1)
                    for g in range(GROUPS):
                        pe.wait_ge(probs_done[g], PASS * i + n + 1)
                        if g == 0:
                            pe.wait_ge(heads_copied, PASS * i + n)
                        for h in range(HG):
                            at = (HG * g + h) * HD
                            mm = nc.tensor.matmul(psH[VW * h:VW * h + HD, g * CH:(g + 1) * CH], v[p][:, c, at:at + HD],
                                                  probs[g][:, h * CH:(h + 1) * CH], start=True, stop=True,
                                                  tile_position=(0, VW * h), skip_group_check=True)
                        mm.then_inc(probs_used[g], 1)
                        if n + 1 < PASS:
                            scores(n + 1, g)
                    if c < NC - 1:
                        pe.wait_ge(update_done, UPDATES * i + 3 * p + c)
                        pe.wait_ge(normT_done, PASS * i + n)
                        for k in range(KT):
                            mm = nc.tensor.matmul(psK[:, k, :], kd[p][:, c, k * P:(k + 1) * P], v[p][:, c, k * P:(k + 1) * P],
                                                  start=True, stop=True, skip_group_check=True)
                        mm.then_inc(update_ps, 1)
                    pe.wait_ge(gated[(n - 1) % PASS // NC], NC * i + ((n - 1) % NC + 1 if n else 0))
                    if c:
                        if c == 1:
                            pe.wait_ge(update_done, UPDATES * i + 3 * p + 1)
                        else:
                            pe.wait_ge(state_done, 4 * i + 2 * p + c - 1)
                        for k in range(KT):
                            nc.tensor.matmul(psO[:, k * P:(k + 1) * P], qd[p][:, k, c * CH:(c + 1) * CH], state[:, k, :],
                                             start=k == 0, stop=False, skip_group_check=True)
                    pe.wait_ge(heads_copied, PASS * i + n + 1)
                    for g in range(GROUPS):
                        mm = nc.tensor.matmul(psO[:, g * HG * HD:(g + 1) * HG * HD], headsT[:, g * CH:(g + 1) * CH], sel[:, :],
                                              start=c == 0 and g == 0, stop=g == GROUPS - 1, skip_group_check=True)
                    mm.then_inc(out_ps, 1)
                    if n:
                        project(n - 1)
                turn(PASS - 1)
                project(PASS - 1)


def two_layers(nc, io, out):
    with ExitStack() as ctx:
        def sb(name, shape, dt=F32):
            return ctx.enter_context(nc.sbuf_tensor(name, shape, dt))

        def dram(name, shape, dt=F32):
            return nc.dram_tensor("scratch_" + name, shape, dt, kind="Internal").ap()

        scratch = {
            "cT": dram("cT", (BATCHES, E, SEQ)),
            "v": dram("v", (BATCHES, SEQ, HEADS * VW)),
            "qf": dram("qf", (BATCHES, KT, P, SEQ)),
            "parts": dram("parts", (BATCHES, 3, 2 * KT, P, SEQ), BF16),
            "max": dram("max", (2 * HG, SEQ), BF16),
            "outT": dram("outT", (BATCHES, GROUPS, P, SEQ)),
            "v1": dram("v1", (BATCHES, SEQ, D)),
            "kd": dram("kd", (BATCHES, SEQ, D)),
            "qd": dram("qd", (BATCHES, KT, P, SEQ)),
            "parts1": dram("parts1", (BATCHES, 3, 2 * KT, P, SEQ), BF16),
            "sg": dram("sg", (BATCHES, SEQ, D)),
        }
        keep = {"xacc": sb("xacc", [P, TOK // P, D]), "semaphores": []}
        with ExitStack() as inner:
            keep["mem"] = inner.enter_context(nc.sbuf_tensor("mem", [P, BATCHES * KT, MW], F32))
            layer0_front(nc, io, scratch, keep)
            end_stage(nc, keep)
            layer0_attention(nc, io, scratch, keep)
            end_stage(nc, keep)
            with ExitStack() as last:
                keep["xT1"] = [last.enter_context(nc.sbuf_tensor(f"xT1{i}", [P, KT, TOK], F32R)) for i in range(2)]
                keep["comb1"] = last.enter_context(nc.sbuf_tensor("comb1", [P, TOK // P, E], F32))
                layer1_front(nc, io, scratch, keep)
                end_stage(nc, keep)
                layer1_experts(nc, io, keep)
                end_stage(nc, keep)
        layer1_attention(nc, io, scratch, keep, out)


def constants():
    import numpy as np
    f = np.arange(512, dtype=np.float32)[None, :] * (np.float32(1.0) / np.float32(10000.0) ** (np.arange(0, 256, 2, dtype=np.float32) / np.float32(256)))[:, None]
    p = np.arange(128)
    c = {}
    c['ident'] = np.eye(128, dtype=np.float32)
    c['cos'], c['sin'] = np.cos(f).astype(np.float32), np.sin(f).astype(np.float32)
    c['blockmask'] = (p[:, None] // 16 == p[None, :] // 16).astype(np.float32)
    c['headmask'] = (p[:, None] // 16 == np.arange(8)[None, :]).astype(np.float32)
    c['iota8'] = np.tile(np.arange(8, dtype=np.float32), (128, 4))
    sel = np.zeros((128, 4, 17), np.float32)
    for g in range(4):
        for j in range(17):
            sel[32 * g + j, g, j] = 1
    c['sel17'] = sel.reshape(128, 68)
    c['sel16'] = np.ascontiguousarray(sel[:, :, :16]).reshape(128, 64)
    c['rel'] = np.maximum(p[None, :] - p[:, None], 0).astype(np.float32)
    c['causal'] = (p[None, :] >= p[:, None]).astype(np.float32)
    c['after'] = np.tile((p + 1).astype(np.float32), (128, 1))
    c['before'] = (127 - p).astype(np.float32)[:, None].copy()
    return c


def layout(g):
    import numpy as np
    C = np.ascontiguousarray
    arrays = {"x": g["L0_attn_hidden_states"]}
    for n in ("Wq", "Wk", "Wv", "Wo"):
        arrays[n + "0"] = C(g["L0_attn_" + n].T)
        arrays[n + "1"] = g["L1_attn_" + n]
    arrays["gate_attn"] = C(g["L0_attn_gate"].reshape(1, HEADS))
    arrays["router0"] = C(g["L0_ffn_gate_w"].T)
    arrays["gate0"] = C(g["L0_ffn_gate_proj"].reshape(E * F0, D).T)
    arrays["up0"] = C(g["L0_ffn_up_proj"].reshape(E * F0, D).T)
    arrays["down0"] = C(g["L0_ffn_down_proj"].transpose(0, 2, 1)).reshape(E * F0, D)
    arrays["log_decay"] = g["L1_attn_log_decay"].reshape(1, HEADS)
    arrays["log_decay_rows"] = C(np.repeat(g["L1_attn_log_decay"].reshape(KT, HH), HD, axis=1).T)
    arrays["Wg1"], arrays["Wg2"] = g["L1_attn_Wg1"], g["L1_attn_Wg2"]
    arrays["norm_w"] = g["L1_attn_norm_w"].reshape(1, D)
    arrays["router1"] = g["L1_ffn_w_router"]
    arrays["gate1"], arrays["up1"], arrays["down1"] = g["L1_ffn_w_gate"], g["L1_ffn_w_up"], g["L1_ffn_w_down"]
    return arrays


def kernel(**inputs):
    import numpy as np
    import concourse.bacc as bacc
    from concourse.bass_utils import run_bass_kernel_spmd

    arrays = layout({name: np.asarray(a) for name, a in inputs.items()})
    arrays.update(constants())
    nc = bacc.Bacc("TRN2", target_bir_lowering=False, num_devices=1)
    io = {}
    for name, a in arrays.items():
        io[name] = nc.dram_tensor(f"in_{name}_dram", a.shape, mybir.dt.from_np(a.dtype), kind="ExternalInput").ap()
    out = nc.dram_tensor("out_0_dram", (BATCHES, SEQ, D), F32, kind="ExternalOutput").ap()
    two_layers(nc, io, out.rearrange("b s d -> (b s) d"))
    r = run_bass_kernel_spmd(nc, [{f"in_{name}_dram": np.ascontiguousarray(a) for name, a in arrays.items()}], core_ids=[0])
    return r.results[0]["out_0_dram"]
```

```python
from contextlib import ExitStack

import concourse.bass as bass
from concourse import mybir

F32 = mybir.dt.float32
F32R = mybir.dt.float32r
BF16 = mybir.dt.bfloat16
U32 = mybir.dt.uint32
ALU = mybir.AluOpType
ACT = mybir.ActivationFunctionType
AX_X = mybir.AxisListType.X

P = 128
BATCHES = 4
SEQ = 512
TOK = BATCHES * SEQ
TILES = SEQ // P
D = 256
KT = D // P
HEADS = 16
HD = D // HEADS
HG = 4
GROUPS = HEADS // HG
HH = HEADS // KT
EPS = 1e-5
E = 8
F0 = 176
FT0 = E * F0 // P
H1 = 512
HT1 = H1 // P
CH = 128
VW = 32
MW = P + HH
Q_PARTS = (0, 0, 1, 0, 2, 1)
K_PARTS = (0, 1, 0, 2, 0, 1)
STACK = len(Q_PARTS) * HD
STACKM = STACK + 2


def three(nc, out, pairs, regions_first=True, last=True, start=True):
    n = len(pairs)
    for i, (ah, al, bh, bl) in enumerate(pairs):
        nc.tensor.matmul(out, ah, bh, start=start and i == 0, stop=False, skip_group_check=True)
        nc.tensor.matmul(out, ah, bl, start=False, stop=False, skip_group_check=True)
        mm = nc.tensor.matmul(out, al, bh, start=False, stop=last and i == n - 1, skip_group_check=True)
    return mm


def stage_semaphore(nc, keep, name):
    handle = nc.alloc_semaphore(name)
    keep["semaphores"].append(handle)
    return handle


def end_stage(nc, keep):
    nc.clear_and_free_semaphores(keep["semaphores"])
    keep["semaphores"] = []
    nc.all_engine_barrier()


class Norm:

    def __init__(self, nc, sb, sem):
        self.nc = nc
        self.stats, self.mv = sb("ln_stats", [P, TILES, 6]), sb("ln_mv", [P, TILES, 2])
        self.vare, self.rstd = sb("ln_vare", [P, TILES]), sb("ln_rstd", [P, TILES])
        self.neghalf, self.held = sb("ln_neghalf", [P, TILES]), sb("ln_held", [P, 1])
        self.neghalf_set, self.stats_done, self.mv_done = sem("ln_neghalf"), sem("ln_stats"), sem("ln_mv")
        self.vare_done, self.rstd_done, self.xn_done = sem("ln_vare"), sem("ln_rstd"), sem("ln_xn")

    def setup(self, pool):
        self.nc.gpsimd.memset(self.neghalf[:, :], -0.5).then_inc(self.neghalf_set, 1)
        pool.wait_ge(self.neghalf_set, 1)

    def power(self, pool, b):
        pool.wait_ge(self.vare_done, b + 1)
        self.nc.gpsimd.tensor_tensor(self.rstd[:, :], self.vare[:, :], self.neghalf[:, :],
                                     ALU.pow).then_inc(self.rstd_done, 1)

    def vector(self, dve, b, xacc, xn):
        nc = self.nc

        def rows(t):
            return xacc[:, bass.ds(b * TILES + t, 1), :].rearrange("p a d -> p (a d)")

        for t in range(TILES):
            last = nc.vector.bn_stats(self.stats[:, t, :], rows(t))
        last.then_inc(self.stats_done, 1)
        dve.wait_ge(self.stats_done, b + 1)
        nc.vector.memset(self.held[:, :], 0.0)
        for t in range(TILES):
            nc.vector.bn_aggr(self.mv[:, t, :], self.stats[:, t, :]).then_inc(self.mv_done, 1)
        dve.wait_ge(self.mv_done, (b + 1) * TILES)
        nc.vector.tensor_scalar(self.vare[:, :], self.mv[:, :, 1], EPS, None, ALU.add).then_inc(self.vare_done, 1)
        dve.wait_ge(self.rstd_done, b + 1)
        for t in range(TILES):
            nc.vector.tensor_scalar(xn[:, t, :], rows(t), self.mv[:, t, 0:1], self.rstd[:, t:t + 1],
                                    ALU.subtract, ALU.mult).then_inc(self.xn_done, 1)


class Routing:

    STEPS = 8

    def __init__(self, nc, sb, sem):
        self.nc = nc
        self.iota8 = sb("rt_iota8", [P, TILES, E])
        self.logits, self.top = sb("rt_logits", [P, TILES, E]), sb("rt_top", [P, TILES, E])
        self.idx, self.idxf = sb("rt_idx", [P, TILES, E], U32), sb("rt_idxf", [P, TILES, 2])
        self.gap, self.w1, self.w2 = sb("rt_gap", [P, TILES]), sb("rt_w1", [P, TILES]), sb("rt_w2", [P, TILES])
        self.eq = [sb(f"rt_eq{i}", [P, TILES, E]) for i in range(2)]
        self.copied, self.top_done, self.gap_done = sem("rt_copied"), sem("rt_top"), sem("rt_gap")
        self.exp_done, self.step, self.comb_done = sem("rt_exp"), sem("rt_step"), sem("rt_comb")
        self.iota_in = sem("rt_iota_in")

    def load(self, sp, io):
        sp.dma_start(self.iota8[:, :, :], io["iota8"].rearrange("p (t e) -> p t e", e=E)).then_inc(self.iota_in, 16)

    def exp(self, act, b):
        act.wait_ge(self.gap_done, b + 1)
        self.nc.scalar.activation(self.gap[:, :], self.gap[:, :], ACT.Exp).then_inc(self.exp_done, 1)

    def vector(self, dve, b, source, comb):
        nc = self.nc
        nc.vector.tensor_copy(self.logits[:, :, :], source).then_inc(self.copied, 1)
        dve.wait_ge(self.iota_in, 16)
        dve.wait_ge(self.copied, b + 1)
        for t in range(TILES):
            nc.vector.max(self.top[:, t, :], self.logits[:, t, :]).then_inc(self.top_done, 1)
        dve.wait_ge(self.top_done, 2 * TILES * b + TILES)
        nc.vector.tensor_tensor(self.gap[:, :], self.top[:, :, 1], self.top[:, :, 0], ALU.subtract).then_inc(self.gap_done, 1)
        for t in range(TILES):
            nc.vector.max_index(self.idx[:, t, :], self.top[:, t, :], self.logits[:, t, :]).then_inc(self.top_done, 1)
        dve.wait_ge(self.top_done, 2 * TILES * (b + 1))
        nc.vector.tensor_copy(self.idxf[:, :, :], self.idx[:, :, 0:2]).then_inc(self.step, 1)
        dve.wait_ge(self.step, self.STEPS * b + 1)
        for i in range(2):
            nc.vector.tensor_tensor(self.eq[i][:, :, :], self.iota8[:, :, :],
                                    self.idxf[:, :, i:i + 1].to_broadcast((P, TILES, E)), ALU.is_equal).then_inc(self.step, 1)
        dve.wait_ge(self.exp_done, b + 1)
        nc.vector.tensor_scalar(self.w1[:, :], self.gap[:, :], 1.0, None, ALU.add).then_inc(self.step, 1)
        dve.wait_ge(self.step, self.STEPS * b + 4)
        nc.vector.reciprocal(self.w1[:, :], self.w1[:, :]).then_inc(self.step, 1)
        dve.wait_ge(self.step, self.STEPS * b + 5)
        nc.vector.tensor_tensor(self.w2[:, :], self.w1[:, :], self.gap[:, :], ALU.mult).then_inc(self.step, 1)
        dve.wait_ge(self.step, self.STEPS * b + 6)
        for i, w in enumerate((self.w1, self.w2)):
            nc.vector.tensor_tensor(self.eq[i][:, :, :], self.eq[i][:, :, :],
                                    w[:, :].unsqueeze(2).to_broadcast((P, TILES, E)), ALU.mult).then_inc(self.step, 1)
        dve.wait_ge(self.step, self.STEPS * b + 8)
        nc.vector.tensor_tensor(comb, self.eq[0][:, :, :], self.eq[1][:, :, :], ALU.add).then_inc(self.comb_done, 1)


def layer0_front(nc, io, scratch, keep):
    with ExitStack() as ctx:
        def sb(name, shape, dt=F32):
            return ctx.enter_context(nc.sbuf_tensor(name, shape, dt))

        def sem(name):
            return stage_semaphore(nc, keep, name)

        xacc, mem = keep["xacc"], keep["mem"]
        ident, cos, sin, = sb("a_ident", [P, P]), sb("a_cos", [P, SEQ]), sb("a_sin", [P, SEQ])
        blockmask, headmask = sb("a_blockmask", [P, P]), sb("a_headmask", [P, HH])
        raw = sb("a_raw", [P, FT0 * D])
        wqk = [sb(f"a_wqk{i}", [P, KT, 2 * D], F32R) for i in range(2)]
        wv = [sb(f"a_wv{i}", [P, KT, D + E], F32R) for i in range(2)]
        wg = [sb(f"a_wg{i}", [P, KT, E * F0], F32R) for i in range(2)]
        wu = [sb(f"a_wu{i}", [P, KT, E * F0], F32R) for i in range(2)]
        wd = [sb(f"a_wd{i}", [P, FT0, D], F32R) for i in range(2)]
        norm = Norm(nc, lambda n, *a: sb("a_" + n, *a), lambda n: sem("a_" + n))
        routing = Routing(nc, lambda n, *a: sb("a_" + n, *a), lambda n: sem("a_" + n))
        xn = sb("a_xn", [P, TILES, D])
        xT = [sb(f"a_xT{i}", [P, KT, SEQ], F32R) for i in range(2)]
        qk = sb("a_qk", [P, 2 * KT, SEQ])
        rot = sb("a_rot", [P, 2 * KT, SEQ])
        parts = [sb(f"a_part{i}", [P, 2 * KT, SEQ], BF16) for i in range(3)]
        vones = sb("a_vones", [P, TILES, KT, P + 2])
        v32 = sb("a_v32", [P, TILES, HEADS, VW])
        kf = sb("a_kf", [P, TILES, D])
        comb = sb("a_comb", [P, TILES, E])
        cT = sb("a_cT", [E, SEQ])
        cbc = sb("a_cbc", [P, FT0, SEQ])
        hs = [sb(f"a_hs{i}", [P, SEQ]) for i in range(2)]
        hh = [[sb(f"a_h{i}{j}", [P, SEQ], F32R) for i in range(2)] for j in range(2)]

        psT = ctx.enter_context(nc.psum_tensor("a_psT", [P, 2, SEQ], F32))
        psG = ctx.enter_context(nc.psum_tensor("a_psG", [P, 4, SEQ], F32))
        psO = ctx.enter_context(nc.psum_tensor("a_psO", [P, TILES, D], F32))

        consts_in, x_in, w_in, raw_in, raw_free = (sem(n) for n in (
            "a_consts_in", "a_x_in", "a_w_in", "a_raw_in", "a_raw_free"))
        w_split = sem("a_w_split")
        dve_done, act_done, pool_done = sem("a_dve"), sem("a_act"), sem("a_pool")
        xT_done, qk_ps, v_ps, rt_ps, kfT_ps, memo_ps, cT_ps, gu_ps, out_ps = (sem("a_" + n) for n in (
            "xTps", "qkps", "vps", "rtps", "kfTps", "memps", "cTps", "gups", "outps"))
        stored, cT_in, cbc_in = sem("a_stored"), sem("a_cT_in"), sem("a_cbc_in")
        S = {}

        def s(name):
            if name not in S:
                S[name] = sem("a_" + name)
            return S[name]

        for n in ("stats", "mv", "vare", "rstd", "xn", "xhi", "xlo", "rope", "roped", "min", "feat", "p1", "r1",
                  "p2", "p3", "vcopy", "kfcopy", "memcopy", "lg", "mx", "gapd", "gexp", "wts", "comb", "cTc",
                  "silu", "su", "h", "hhi", "hlo", "outacc", "ones", "link", "q_st", "f_st", "v_st", "expm"):
            s(n)

        block = ctx.enter_context(nc.Block())

        @block.sync
        def _(sp):
            for b in range(BATCHES):
                sp.dma_start(xacc[:, b * TILES:(b + 1) * TILES, :],
                             io["x"][b].rearrange("(t p) d -> p t d", p=P)).then_inc(x_in, 16)
                if b == 0:
                    for dst, src in ((ident, "ident"), (blockmask, "blockmask"), (headmask, "headmask")):
                        sp.dma_start(dst[:, :], io[src]).then_inc(consts_in, 16)
                    routing.load(sp, io)
            for n, (pieces) in enumerate((
                    (("Wq0", 0, D, 2 * D), ("Wk0", D, 2 * D, 2 * D)),
                    (("Wv0", 0, D, D + E), ("router0", D, D + E, D + E)),
                    (("gate0", 0, E * F0, E * F0),), (("up0", 0, E * F0, E * F0),))):
                if n:
                    sp.wait_ge(raw_free, n)
                for name, lo, hi, w in pieces:
                    sp.dma_start(raw[:, 0:KT * w].rearrange("p (k n) -> p k n", k=KT)[:, :, lo:hi],
                                 io[name].rearrange("(k p) n -> p k n", p=P)).then_inc(raw_in, 16)
                if n == 0:
                    sp.dma_start(cos[:, :], io["cos"]).then_inc(consts_in, 16)
                    sp.dma_start(sin[:, :], io["sin"]).then_inc(consts_in, 16)
            sp.wait_ge(raw_free, 4)
            sp.dma_start(raw[:, :].rearrange("p (k n) -> p k n", n=D),
                         io["down0"].rearrange("(k p) n -> p k n", p=P)).then_inc(raw_in, 16)
            with sp.Fori(0, BATCHES) as b:
                sp.wait_ge(s("cTc"), b + 1)
                sp.dma_start(scratch["cT"][b], cT[:, :]).then_inc(cT_in, 16)
                sp.wait_ge(s("h"), FT0 * b)
                sp.wait_ge(cT_in, 16 * b + 16)
                for e in range(E):
                    f = e * F0
                    while f < (e + 1) * F0:
                        n = min(P - f % P, (e + 1) * F0 - f)
                        sp.dma_start(cbc[f % P:f % P + n, f // P, :],
                                     scratch["cT"][b, e:e + 1, :].to_broadcast((n, SEQ))).then_inc(cbc_in, 16)
                        f += n
                sp.wait_ge(s("vcopy"), 2 * b + 2)
                sp.dma_start(scratch["v"][b].rearrange("(t p) n -> p t n", p=P),
                             v32[:, :, :, :].rearrange("p t h w -> p t (h w)")).then_inc(s("v_st"), 16)
                sp.wait_ge(s("feat"), 2 * b + 2)
                sp.dma_start(scratch["qf"][b].rearrange("k p n -> p k n"), rot[:, 0:KT, :]).then_inc(s("f_st"), 16)
                for i, done in enumerate(("p1", "p2", "p3")):
                    sp.wait_ge(s(done), b + 1)
                    sp.dma_start(scratch["parts"][b, i].rearrange("k p n -> p k n"), parts[i][:, :, :]).then_inc(s("q_st"), 16)
            sp.wait_ge(s("v_st"), 16 * BATCHES)
            sp.wait_ge(s("f_st"), 16 * BATCHES)
            sp.wait_ge(s("q_st"), 48 * BATCHES)

        CBC = sum(1 + ((e + 1) * F0 - 1) // P - e * F0 // P for e in range(E))

        @block.gpsimd
        def _(pool):
            norm.setup(pool)
            nc.gpsimd.memset(v32[:, :, :, HD:HD + 1], 1.0).then_inc(s("ones"), 1)
            nc.gpsimd.memset(v32[:, :, :, HD + 1:VW], 0.0).then_inc(s("ones"), 1)
            nc.gpsimd.memset(vones[:, :, :, P:P + 2], 1.0).then_inc(s("ones"), 1)
            pool.wait_ge(s("ones"), 3)
            with pool.Fori(0, BATCHES) as b:
                norm.power(pool, b)
                pool.wait_ge(s("feat"), 2 * b + 2)
                pool.wait_ge(s("p1"), b + 1)
                nc.gpsimd.tensor_tensor(qk[:, :, :], qk[:, :, :], parts[0][:, :, :], ALU.subtract).then_inc(s("r1"), 1)
                pool.wait_ge(s("p2"), b + 1)
                if True:
                    pool.wait_ge(s("q_st"), 48 * b)
                nc.gpsimd.tensor_tensor(parts[2][:, :, :], qk[:, :, :], parts[1][:, :, :], ALU.subtract).then_inc(s("p3"), 1)
                for j in range(FT0):
                    pool.wait_ge(s("hhi"), b * FT0 + j + 1)
                    nc.gpsimd.tensor_tensor(hh[j % 2][1][:, :], hs[j % 2][:, :], hh[j % 2][0][:, :].bitcast(F32),
                                            ALU.subtract).then_inc(s("hlo"), 1)

        @block.scalar
        def _(act):
            for n, dst in enumerate((wqk, wv, wg, wu, wd)):
                act.wait_ge(raw_in, (32, 64, 80, 96, 112)[n])
                if n:
                    act.wait_ge(raw_free, n)
                src = raw[:, 0:dst[0].shape[1] * dst[0].shape[2]].rearrange("p (k n) -> p k n", k=dst[0].shape[1])
                nc.scalar.activation(dst[0][:, :, :], src, ACT.Copy).then_inc(w_split, 1)
            with act.Fori(0, BATCHES) as b:
                act.wait_ge(xT_done, b + 1)
                act.wait_ge(v_ps, 4 * b)
                act.wait_ge(gu_ps, FT0 * b)
                nc.scalar.activation(xT[0][:, :, :], psT[:, :, :], ACT.Copy).then_inc(s("xhi"), 1)
                act.wait_ge(v_ps, 4 * b + 4)
                act.wait_ge(s("v_st"), 16 * b)
                nc.scalar.activation(v32[:, :, :, 0:HD], psO[:, :, :].rearrange("p t (h d) -> p t h d", d=HD),
                                     ACT.Copy).then_inc(s("vcopy"), 1)
                act.wait_ge(memo_ps, b)
                nc.scalar.activation(vones[:, :, :, 0:P], psO[:, :, :].rearrange("p t (k n) -> p t k n", k=KT),
                                     ACT.Copy).then_inc(s("vcopy"), 1)
                routing.exp(act, b)
                act.wait_ge(s("min"), b + 1)
                nc.scalar.activation(rot[:, :, :], rot[:, :, :], ACT.Exp).then_inc(s("expm"), 1)
                act.wait_ge(s("roped"), b + 1)
                act.wait_ge(s("q_st"), 48 * b)
                nc.scalar.activation(parts[0][:, :, :], qk[:, :, :], ACT.Copy).then_inc(s("p1"), 1)
                act.wait_ge(s("r1"), b + 1)
                nc.scalar.activation(parts[1][:, :, :], qk[:, :, :], ACT.Copy).then_inc(s("p2"), 1)
                act.wait_ge(kfT_ps, b + 1)
                nc.scalar.activation(kf[:, :, :], psT[:, :, :].rearrange("p a (t n) -> p (a t) n", n=D),
                                     ACT.Copy).then_inc(s("kfcopy"), 1)
                for j in range(FT0):
                    act.wait_ge(gu_ps, b * FT0 + j + 1)
                    act.wait_ge(s("hlo"), b * FT0 + j - 1) if j >= 2 else act.wait_ge(s("hlo"), b * FT0)
                    nc.scalar.activation(hs[j % 2][:, :], psG[:, 2 * (j % 2), :], ACT.Silu).then_inc(s("silu"), 1)
                    act.wait_ge(s("h"), b * FT0 + j + 1)
                    act.wait_ge(out_ps, b * FT0 + j - 1) if j >= 2 else act.wait_ge(out_ps, b * FT0)
                    nc.scalar.activation(hh[j % 2][0][:, :], hs[j % 2][:, :], ACT.Copy).then_inc(s("hhi"), 1)

        @block.vector
        def _(dve):
            for n, dst in enumerate((wqk, wv, wg, wu, wd)):
                dve.wait_ge(w_split, n + 1)
                src = raw[:, 0:dst[0].shape[1] * dst[0].shape[2]].rearrange("p (k n) -> p k n", k=dst[0].shape[1])
                nc.vector.tensor_tensor(dst[1][:, :, :], src, dst[0][:, :, :].bitcast(F32), ALU.subtract).then_inc(raw_free, 1)
            dve.wait_ge(x_in, 64)
            dve.wait_ge(consts_in, 80)
            dve.wait_ge(s("ones"), 3)
            with dve.Fori(0, BATCHES) as b:
                norm.vector(dve, b, xacc, xn)
                dve.wait_ge(s("xhi"), b + 1)
                nc.vector.tensor_tensor(xT[1][:, :, :], psT[:, :, :], xT[0][:, :, :].bitcast(F32), ALU.subtract).then_inc(s("xlo"), 1)
                dve.wait_ge(qk_ps, b + 1)
                dve.wait_ge(s("f_st"), 16 * b)
                for i in range(2):
                    for h in range(KT):
                        nc.vector.tensor_tensor(qk[:, 2 * i + h, :], psG[:, 2 * i + h, :], cos[:, :], ALU.mult)
                        nc.vector.tensor_tensor(rot[:, 2 * i + h, :], psG[:, 2 * i + 1 - h, :], sin[:, :],
                                                ALU.mult).then_inc(s("rope"), 1)
                for i in range(2):
                    dve.wait_ge(s("rope"), 4 * b + 2 * i + 2)
                    nc.vector.tensor_tensor(qk[:, 2 * i, :], qk[:, 2 * i, :], rot[:, 2 * i, :], ALU.subtract)
                    last = nc.vector.tensor_tensor(qk[:, 2 * i + 1, :], qk[:, 2 * i + 1, :], rot[:, 2 * i + 1, :], ALU.add)
                last.then_inc(s("roped"), 1)
                dve.wait_ge(s("roped"), b + 1)
                nc.vector.tensor_scalar(rot[:, :, :], qk[:, :, :], 0.0, None, ALU.min).then_inc(s("min"), 1)
                dve.wait_ge(rt_ps, b + 1)
                routing.vector(dve, b, psT[:, 0, 0:TILES * E].rearrange("p (t e) -> p t e", e=E), comb[:, :, :])
                dve.wait_ge(cT_ps, b + 1)
                dve.wait_ge(cT_in, 16 * b)
                nc.vector.tensor_copy(cT[:, :], psT[0:E, 1, :]).then_inc(s("cTc"), 1)
                dve.wait_ge(s("expm"), b + 1)
                for i in (1, 0):
                    nc.vector.scalar_tensor_tensor(rot[:, 2 * i:2 * i + 2, :], qk[:, 2 * i:2 * i + 2, :], 0.0,
                                                   rot[:, 2 * i:2 * i + 2, :], ALU.max, ALU.add).then_inc(s("feat"), 1)
                dve.wait_ge(memo_ps, b + 1)
                for k in range(KT):
                    src = psT[:, 0, 130 * k:130 * k + P]
                    nc.vector.tensor_tensor(mem[:, bass.ds(b * KT + k, 1), 0:P].rearrange("p a n -> p (a n)"), src, blockmask[:, :], ALU.mult)
                    nc.vector.tensor_tensor(mem[:, bass.ds(b * KT + k, 1), P:MW].rearrange("p a n -> p (a n)"), headmask[:, :],
                                            psT[:, 0, 130 * k + P:130 * k + P + 1].to_broadcast((P, HH)), ALU.mult).then_inc(s("memcopy"), 1)
                dve.wait_ge(cbc_in, 16 * CBC * (b + 1))
                for j in range(FT0):
                    dve.wait_ge(s("silu"), b * FT0 + j + 1)
                    nc.vector.tensor_tensor(hs[j % 2][:, :], hs[j % 2][:, :], psG[:, 2 * (j % 2) + 1, :], ALU.mult).then_inc(s("su"), 1)
                    dve.wait_ge(s("su"), b * FT0 + j + 1)
                    nc.vector.tensor_tensor(hs[j % 2][:, :], hs[j % 2][:, :], cbc[:, j, :], ALU.mult).then_inc(s("h"), 1)
                dve.wait_ge(out_ps, (b + 1) * FT0)
                nc.vector.tensor_tensor(xacc[:, bass.ds(b * TILES, TILES), :], psO[:, :, :], xacc[:, bass.ds(b * TILES, TILES), :],
                                        ALU.add).then_inc(s("outacc"), 1)
                dve.wait_ge(s("outacc"), b + 1)

        @block.tensor
        def _(pe):
            pe.wait_ge(consts_in, 80)
            pe.wait_ge(raw_free, 2)
            with pe.Fori(0, BATCHES) as b:
                pe.wait_ge(s("memcopy"), KT * b)
                for t in range(TILES):
                    pe.wait_ge(norm.xn_done, TILES * b + t + 1)
                    for k in range(KT):
                        mm = nc.tensor.transpose(psT[:, k, t * P:(t + 1) * P], xn[:, t, k * P:(k + 1) * P], ident[:, :])
                mm.then_inc(xT_done, 1)
                pe.wait_ge(s("xlo"), b + 1)
                pe.wait_ge(s("h"), FT0 * b)
                for m in range(4):
                    c = slice(m * P, (m + 1) * P)
                    mm = three(nc, psG[:, m, :], [(wqk[0][:, k, c], wqk[1][:, k, c], xT[0][:, k, :], xT[1][:, k, :])
                                                  for k in range(KT)])
                mm.then_inc(qk_ps, 1)
                for t in range(TILES):
                    c = slice(t * P, (t + 1) * P)
                    mm = three(nc, psT[:, 0, t * E:(t + 1) * E],
                               [(xT[0][:, k, c], xT[1][:, k, c], wv[0][:, k, D:D + E], wv[1][:, k, D:D + E])
                                for k in range(KT)])
                mm.then_inc(rt_ps, 1)
                pe.wait_ge(s("outacc"), b)
                for t in range(TILES):
                    c = slice(t * P, (t + 1) * P)
                    three(nc, psO[:, t, :], [(xT[0][:, k, c], xT[1][:, k, c], wv[0][:, k, 0:D], wv[1][:, k, 0:D])
                                             for k in range(KT)]).then_inc(v_ps, 1)
                pe.wait_ge(routing.comb_done, b + 1)
                for t in range(TILES):
                    mm = nc.tensor.transpose(psT[0:E, 1, t * P:(t + 1) * P], comb[:, t, :], ident[:, :])
                mm.then_inc(cT_ps, 1)
                pe.wait_ge(s("cTc"), b + 1)
                pe.wait_ge(s("feat"), 2 * b + 1)
                pe.wait_ge(routing.copied, b + 1)
                for t in range(TILES):
                    for k in range(KT):
                        at = t * D + k * P
                        mm = nc.tensor.transpose(psT[:, at // SEQ, at % SEQ:at % SEQ + P],
                                                 rot[:, 2 + k, t * P:(t + 1) * P], ident[:, :])
                mm.then_inc(kfT_ps, 1)
                pe.wait_ge(s("kfcopy"), b + 1)
                pe.wait_ge(s("vcopy"), 2 * b + 2)
                for k in range(KT):
                    for t in range(TILES):
                        mm = nc.tensor.matmul(psT[:, 0, 130 * k:130 * k + P + 2], kf[:, t, k * P:(k + 1) * P],
                                              vones[:, t, k, :], start=t == 0, stop=t == TILES - 1, skip_group_check=True)
                mm.then_inc(memo_ps, 1)
                pe.wait_ge(s("roped"), b + 1)

                def gate_up(j):
                    pe.wait_ge(raw_free, 4)
                    pe.wait_ge(s("su"), b * FT0 + j - 1) if j >= 2 else pe.wait_ge(s("su"), b * FT0)
                    c = slice(j * P, (j + 1) * P)
                    for i, w in enumerate((wg, wu)):
                        mm = three(nc, psG[:, 2 * (j % 2) + i, :],
                                   [(w[0][:, k, c], w[1][:, k, c], xT[0][:, k, :], xT[1][:, k, :]) for k in range(KT)])
                    mm.then_inc(gu_ps, 1)

                def down(j):
                    pe.wait_ge(raw_free, 5)
                    pe.wait_ge(s("hlo"), b * FT0 + j + 1)
                    for t in range(TILES):
                        c = slice(t * P, (t + 1) * P)
                        mm = three(nc, psO[:, t, :], [(hh[j % 2][0][:, c], hh[j % 2][1][:, c], wd[0][:, j, :], wd[1][:, j, :])],
                                   start=j == 0 and t % 2 == 0, last=j == FT0 - 1)
                    mm.then_inc(out_ps, 1)

                gate_up(0)
                for j in range(1, FT0):
                    gate_up(j)
                    down(j - 1)
                down(FT0 - 1)


def layer0_attention(nc, io, scratch, keep):
    with ExitStack() as ctx:
        def sb(name, shape, dt=F32):
            return ctx.enter_context(nc.sbuf_tensor(name, shape, dt))

        def sem(name):
            return stage_semaphore(nc, keep, "b_" + name)

        ident = sb("b_ident", [P, P])
        identb = sb("b_identb", [P, P], BF16)
        qst = [sb(f"b_qst{g}", [STACKM, HG, SEQ], BF16) for g in range(GROUPS)]
        kst = [sb(f"b_kst{g}", [STACKM, HG, SEQ], BF16) for g in range(GROUPS)]
        vst = [sb(f"b_vst{g}", [P, TILES, HG * VW]) for g in range(GROUPS)]
        probs = [sb(f"b_probs{k}", [P, HG, SEQ]) for k in range(TILES)]
        negmax = [sb(f"b_negmax{i}", [P, TILES, HG]) for i in range(2)]
        nmparts = [sb(f"b_nmparts{i}", [P, TILES, 2, HG], BF16) for i in range(2)]
        nmT = [sb(f"b_nmT{i}", [2 * HG, SEQ], BF16) for i in range(2)]
        outT = [sb(f"b_outT{i}", [P, SEQ]) for i in range(2)]

        psE = [ctx.enter_context(nc.psum_tensor(f"b_psE{i}", [P, 2, SEQ], F32)) for i in range(2)]
        psM = [ctx.enter_context(nc.psum_tensor(f"b_psM{i}", [P, SEQ], F32)) for i in range(2)]
        psV = ctx.enter_context(nc.psum_tensor("b_psV", [P, SEQ], F32))
        psN = ctx.enter_context(nc.psum_tensor("b_psN", [P, SEQ], BF16))

        ident_in, ones, identb_done = sem("ident_in"), sem("ones"), sem("identb")
        stack_in = [sem(f"stack_in{g}") for g in range(GROUPS)]
        max_in, max_out = [sem(f"max_in{g}") for g in range(GROUPS)], sem("max_out")
        scores_ready, scores_used = sem("scores_ready"), [sem(f"scores_used{i}") for i in range(2)]
        probs_used = [sem(f"probs_used{k}") for k in range(TILES)]
        rows_ready, rows_used = sem("rows_ready"), [sem(f"rows_used{i}") for i in range(2)]
        negmax_hi, negmax_parts = sem("negmax_hi"), sem("negmax_parts")
        nmT_ready, nmT_copied = sem("nmT_ready"), sem("nmT_copied")
        out_copied, out_stored = sem("out_copied"), [sem(f"out_stored{i}") for i in range(2)]
        LOADED = 16 * (2 * len(Q_PARTS) + 1)

        def loop(eng, step):
            with eng.Fori(0, BATCHES - 1) as b:
                for g in range(GROUPS):
                    step(b, g, False)
            for g in range(GROUPS):
                step(BATCHES - 1, g, True)

        block = ctx.enter_context(nc.Block())

        @block.sync
        def _(sp):
            sp.dma_start(ident[:, :], io["ident"]).then_inc(ident_in, 16)

            def load(b, g):
                for op, dst, order in ((0, qst, Q_PARTS), (1, kst, K_PARTS)):
                    for i, part in enumerate(order):
                        row = (g % 2) * HG * HD
                        src = scratch["parts"][b, part, KT * op + g // 2, row:row + HG * HD, :]
                        sp.dma_start(dst[g][i * HD:(i + 1) * HD, :, :],
                                     src.rearrange("(h d) t -> d h t", d=HD)).then_inc(stack_in[g], 16)
                sp.dma_start(vst[g][:, :, :], scratch["v"][b, :, g * HG * VW:(g + 1) * HG * VW]
                             .rearrange("(t p) n -> p t n", p=P)).then_inc(stack_in[g], 16)

            def send_max(n, g, i, before=None):
                sp.wait_ge(nmT_copied, n)
                if before is not None:
                    sp.wait_ge(max_in[(g - 1) % GROUPS], before)
                sp.dma_start(scratch["max"], nmT[i][:, :]).then_inc(max_out, 16)
                sp.wait_ge(max_out, 16 * n)
                sp.dma_start(qst[g][STACK:STACKM, :, :],
                             scratch["max"].rearrange("(a h) t -> a h t", a=2)).then_inc(max_in[g], 16)

            for g in range(GROUPS):
                load(0, g)
            send_max(1, 0, 0)

            def step(b, g, last):
                if not (last and g == GROUPS - 1):
                    send_max(GROUPS * b + g + 2, (g + 1) % GROUPS, (g + 1) % 2, 16 * b + 16)
                sp.wait_ge(out_copied, GROUPS * b + g + 1)
                sp.wait_ge(ident_in, 16)
                sp.dma_start(scratch["outT"][b, g], outT[g % 2][:, :]).then_inc(out_stored[g % 2], 16)
                if not last:
                    sp.wait_ge(probs_used[TILES - 1], GROUPS * b + g + 1)
                    sp.wait_ge(ident_in, 16)
                    load(b + 1, g)

            loop(sp, step)
            for i in range(2):
                sp.wait_ge(out_stored[i], 8 * BATCHES * GROUPS)

        @block.gpsimd
        def _(pool):
            for g in range(GROUPS):
                nc.gpsimd.memset(kst[g][STACK:STACKM, :, :], 1.0).then_inc(ones, 1)

        @block.scalar
        def _(act):
            def step(b, g, last):
                for k in range(TILES):
                    act.wait_ge(probs_used[k], GROUPS * b + g)
                    for i in range(2):
                        act.wait_ge(scores_ready, 8 * (GROUPS * b + g) + 2 * k + i + 1)
                        nc.scalar.activation(probs[k][:, 2 * i:2 * i + 2, :], psE[i][:, :, :], ACT.Exp,
                                             scale=float(HD) ** -0.5).then_inc(scores_used[i], 1)

            loop(act, step)

        @block.vector
        def _(dve):
            dve.wait_ge(ident_in, 16)
            nc.vector.tensor_copy(identb[:, :], ident[:, :]).then_inc(identb_done, 1)

            def reduce(n, i, t):
                for h in range(HG):
                    dve.wait_ge(rows_ready, 16 * n + HG * t + h + 1)
                    nc.vector.tensor_reduce(negmax[i][:, t, h:h + 1], psM[h % 2][:, :], AX_X, ALU.max,
                                            negate=True).then_inc(rows_used[h % 2], 1)

            def split_max(n, i, reused=True):
                if reused:
                    dve.wait_ge(nmT_ready, n - 1)
                dve.wait_ge(rows_used[0], 8 * n + 8)
                dve.wait_ge(rows_used[1], 8 * n + 8)
                nc.vector.tensor_copy(nmparts[i][:, :, 0, :], negmax[i][:, :, :]).then_inc(negmax_hi, 1)
                dve.wait_ge(negmax_hi, n + 1)
                nc.vector.tensor_tensor(nmparts[i][:, :, 1, :], negmax[i][:, :, :], nmparts[i][:, :, 0, :],
                                        ALU.subtract).then_inc(negmax_parts, 1)

            for t in range(TILES):
                reduce(0, 0, t)
            split_max(0, 0, reused=False)
            for t in range(TILES):
                reduce(1, 1, t)
            dve.wait_ge(nmT_ready, 1)
            nc.vector.tensor_copy(nmT[0][:, :], psN[0:2 * HG, :]).then_inc(nmT_copied, 1)
            split_max(1, 1, reused=False)

            def step(b, g, last):
                G = GROUPS * b + g
                ahead = not (last and g >= GROUPS - 2)
                if ahead:
                    reduce(G + 2, g % 2, 0)
                if not (last and g == GROUPS - 1):
                    dve.wait_ge(max_out, 16 * G)
                    dve.wait_ge(nmT_ready, G + 2)
                    nc.vector.tensor_copy(nmT[(g + 1) % 2][:, :], psN[0:2 * HG, :]).then_inc(nmT_copied, 1)
                if ahead:
                    for t in range(1, TILES):
                        reduce(G + 2, g % 2, t)
                    split_max(G + 2, g % 2)
                dve.wait_ge(probs_used[TILES - 1], G + 1)
                dve.wait_ge(out_stored[g % 2], 16 * (2 * b + g // 2))
                nc.vector.tensor_copy(outT[g % 2][:, :], psV[:, :]).then_inc(out_copied, 1)

            loop(dve, step)

        @block.tensor
        def _(pe):
            def rows(n, g, t, b):
                if t == 0:
                    pe.wait_ge(stack_in[g], LOADED * (b + 1))
                for h in range(HG):
                    pe.wait_ge(rows_used[h % 2], 8 * n + 2 * t + h // 2)
                    nc.tensor.matmul(psM[h % 2][:, :], qst[g][0:STACK, h, t * P:(t + 1) * P], kst[g][0:STACK, h, :],
                                     start=True, stop=True).then_inc(rows_ready, 1)

            def turn_max(n, i):
                pe.wait_ge(negmax_parts, n + 1)
                pe.wait_ge(nmT_copied, n)
                for t in range(TILES):
                    mm = nc.tensor.transpose(psN[0:2 * HG, t * P:(t + 1) * P],
                                             nmparts[i][:, t, :, :].rearrange("p a h -> p (a h)"), identb[:, :])
                mm.then_inc(nmT_ready, 1)

            for g in range(2):
                for t in range(TILES):
                    rows(g, g, t, 0)
            pe.wait_ge(identb_done, 1)
            turn_max(0, 0)
            pe.wait_ge(ones, GROUPS)

            def step(b, g, last):
                G = GROUPS * b + g
                pe.wait_ge(max_in[g], 16 * b + 16)
                pe.wait_ge(ones, GROUPS)

                def values(k):
                    for i in range(2):
                        pe.wait_ge(scores_used[i], TILES * G + k + 1)
                    if k == 0:
                        pe.wait_ge(out_copied, G)
                    for h in range(HG):
                        mm = nc.tensor.matmul(psV[VW * h:VW * (h + 1), :], vst[g][:, k, VW * h:VW * (h + 1)],
                                              probs[k][:, h, :], start=k == 0, stop=k == TILES - 1,
                                              tile_position=(0, VW * h), skip_group_check=True)
                    mm.then_inc(probs_used[k], 1)
                    return mm

                for k in range(TILES):
                    for i in range(2):
                        pe.wait_ge(scores_used[i], TILES * G + k)
                        for h in (2 * i, 2 * i + 1):
                            mm = nc.tensor.matmul(psE[i][:, h % 2, :], kst[g][0:STACKM, h, k * P:(k + 1) * P],
                                                  qst[g][0:STACKM, h, :], start=True, stop=True)
                        mm.then_inc(scores_ready, 1)
                    if k == 1 and not (last and g == GROUPS - 1):
                        turn_max(G + 1, (g + 1) % 2)
                    if not (last and g >= GROUPS - 2):
                        rows(G + 2, (g + 2) % GROUPS, k, b if g < 2 else b + 1)
                    if k:
                        values(k - 1)
                values(TILES - 1)

            loop(pe, step)


RW = E + HD


def layer1_front(nc, io, scratch, keep):
    with ExitStack() as ctx:
        def sb(name, shape, dt=F32):
            return ctx.enter_context(nc.sbuf_tensor("c_" + name, shape, dt))

        def sem(name):
            return stage_semaphore(nc, keep, "c_" + name)

        xacc, mem, xT1, comb1 = keep["xacc"], keep["mem"], keep["xT1"], keep["comb1"]
        norm, routing = Norm(nc, sb, sem), Routing(nc, sb, sem)
        ident, sel = sb("ident", [P, P]), sb("sel", [P, HG * (HD + 1)])
        g16, omg16 = sb("g16", [P, HEADS]), sb("omg16", [P, HEADS])
        after, before = sb("after", [P, P]), sb("before", [P, 1])
        ldrows, ldall = sb("ldrows", [P, KT]), sb("ldall", [P, HEADS])
        qdec, kdec = sb("qdec", [P, KT, P]), sb("kdec", [P, HEADS])
        wo, wg2 = sb("wo", [P, KT, D]), sb("wg2", [HD, D])
        rqk, rkv, rr = sb("rqk", [P, KT, 2 * D]), sb("rkv", [P, KT, 2 * D]), sb("rr", [P, KT, RW])
        wqk = [sb(f"wqk{i}", [P, KT, 2 * D], F32R) for i in range(2)]
        wkv = [sb(f"wkv{i}", [P, KT, 2 * D], F32R) for i in range(2)]
        wr = [sb(f"wr{i}", [P, KT, RW], F32R) for i in range(2)]
        outT, qf = sb("outT", [P, GROUPS, SEQ]), sb("qf", [P, KT, SEQ])
        r1, r2 = sb("r1", [P, TILES, HEADS]), sb("r2", [P, TILES, HEADS])
        t1, t2 = sb("t1", [P, TILES, D]), sb("t2", [P, TILES, D])
        combT, xn = sb("combT", [P, KT, SEQ]), sb("xn", [P, TILES, D])
        xT = [sb(f"xT{i}", [P, KT, SEQ], F32R) for i in range(2)]
        qk, kk = sb("qk", [P, 2 * KT, SEQ]), sb("kk", [P, TILES, D])
        v32 = sb("v32", [P, TILES, HEADS, VW])
        parts = [sb(f"part{i}", [P, 2 * KT, SEQ], BF16) for i in range(3)]
        low, lowT, sg = sb("low", [P, TILES, HD]), sb("lowT", [HD, SEQ]), sb("sg", [P, TILES, D])
        qd, kd = sb("qd", [P, KT, SEQ]), sb("kd", [P, TILES, D])

        psA = ctx.enter_context(nc.psum_tensor("c_psA", [P, 4, SEQ], F32))
        psB = ctx.enter_context(nc.psum_tensor("c_psB", [P, 4, SEQ], F32))
        S = {}

        def s(name):
            if name not in S:
                S[name] = sem(name)
            return S[name]

        for n in ("padded consts_in weights_in w_hi w_lo tables g_done omg_done att_in heads_ps recips scaled terms combined combT_ps "
                  "combT_done y_ps residual xT_ps xhi xlo kept qkT_ps kv_ps silu_qk silu_kv p1 r1d p2 p3 low_ps "
                  "low_done lowT_ps lowT_done gate_ps gate_done qd_done kd_done stored").split():
            s(n)

        block = ctx.enter_context(nc.Block())

        @block.sync
        def _(sp):
            for dst, src in ((ident[:, :], io["ident"]), (sel[:, :], io["sel17"]), (after[:, :], io["after"]),
                             (before[:, :], io["before"]), (ldrows[:, :], io["log_decay_rows"]),
                             (ldall[:, :], io["log_decay"].to_broadcast((P, HEADS))),
                             (g16[:, :], io["gate_attn"].to_broadcast((P, HEADS)))):
                sp.dma_start(dst, src).then_inc(s("consts_in"), 16)
            routing.load(sp, io)
            for dst, src in ((rqk[:, :, 0:D], "Wq1"), (rqk[:, :, D:2 * D], "Wk1"), (rkv[:, :, 0:D], "Wk1"),
                             (rkv[:, :, D:2 * D], "Wv1"), (rr[:, :, 0:E], "router1"), (rr[:, :, E:RW], "Wg1"),
                             (wo[:, :, :], "Wo0")):
                sp.dma_start(dst, io[src].rearrange("(k p) n -> p k n", p=P)).then_inc(s("weights_in"), 16)
            sp.dma_start(wg2[:, :], io["Wg2"]).then_inc(s("weights_in"), 16)
            with sp.Fori(0, BATCHES) as b:
                sp.wait_ge(s("consts_in"), 112)
                sp.wait_ge(s("heads_ps"), b)
                sp.dma_start(outT[:, :, :], scratch["outT"][b].rearrange("g p n -> p g n")).then_inc(s("att_in"), 16)
                sp.dma_start(qf[:, :, :], scratch["qf"][b].rearrange("k p n -> p k n")).then_inc(s("att_in"), 16)
                sp.wait_ge(s("consts_in"), 112)
                sp.wait_ge(s("silu_kv"), b + 1)
                sp.dma_start(scratch["v1"][b].rearrange("(t p) n -> p t n", p=P), v32[:, :, :, :].rearrange("p t h w -> p t (h w)")).then_inc(s("stored"), 16)
                sp.wait_ge(s("consts_in"), 112)
                sp.wait_ge(s("kd_done"), b + 1)
                sp.dma_start(scratch["kd"][b].rearrange("(t p) n -> p t n", p=P), kd[:, :, :]).then_inc(s("stored"), 16)
                sp.wait_ge(s("consts_in"), 112)
                sp.wait_ge(s("qd_done"), b + 1)
                sp.dma_start(scratch["qd"][b].rearrange("k p n -> p k n"), qd[:, :, :]).then_inc(s("stored"), 16)
                for i, done in enumerate(("p1", "p2", "p3")):
                    sp.wait_ge(s("consts_in"), 112)
                    sp.wait_ge(s(done), b + 1)
                    sp.dma_start(scratch["parts1"][b, i].rearrange("k p n -> p k n"), parts[i][:, :, :]).then_inc(s("stored"), 16)
                sp.wait_ge(s("consts_in"), 112)
                sp.wait_ge(s("gate_done"), b + 1)
                sp.dma_start(scratch["sg"][b].rearrange("(t p) n -> p t n", p=P), sg[:, :, :]).then_inc(s("stored"), 16)
            sp.wait_ge(s("stored"), 7 * 16 * BATCHES)

        STORES = 7 * 16

        @block.gpsimd
        def _(pool):
            norm.setup(pool)
            nc.gpsimd.memset(v32[:, :, :, HD:VW], 0.0).then_inc(s("padded"), 1)
            with pool.Fori(0, BATCHES) as b:
                norm.power(pool, b)
                pool.wait_ge(s("xhi"), b + 1)
                pool.wait_ge(s("xlo"), b + 1)
                pool.wait_ge(norm.neghalf_set, 1)
                for i in range(2):
                    nc.gpsimd.tensor_copy(xT1[i][:, :, bass.ds(b * SEQ, SEQ)], xT[i][:, :, :].bitcast(F32)).then_inc(s("kept"), 1)
                pool.wait_ge(s("p1"), b + 1)
                pool.wait_ge(s("qd_done"), b + 1)
                nc.gpsimd.tensor_tensor(qk[:, :, :], qk[:, :, :], parts[0][:, :, :], ALU.subtract).then_inc(s("r1d"), 1)
                pool.wait_ge(s("p2"), b + 1)
                nc.gpsimd.tensor_tensor(parts[2][:, :, :], qk[:, :, :], parts[1][:, :, :], ALU.subtract).then_inc(s("p3"), 1)

        @block.scalar
        def _(act):
            act.wait_ge(s("consts_in"), 112)
            for k in range(KT):
                nc.scalar.activation(qdec[:, k, :], after[:, :], ACT.Exp, scale=ldrows[:, k:k + 1]).then_inc(s("tables"), 1)
            nc.scalar.activation(kdec[:, :], ldall[:, :], ACT.Exp, scale=before[:, 0:1]).then_inc(s("tables"), 1)
            nc.scalar.activation(g16[:, :], g16[:, :], ACT.Sigmoid).then_inc(s("g_done"), 1)
            act.wait_ge(s("weights_in"), 128)
            act.wait_ge(s("padded"), 1)
            for dst, src in ((wqk, rqk), (wkv, rkv), (wr, rr)):
                nc.scalar.activation(dst[0][:, :, :], src[:, :, :], ACT.Copy).then_inc(s("w_hi"), 1)
            with act.Fori(0, BATCHES) as b:
                act.wait_ge(s("combT_ps"), b + 1)
                nc.scalar.activation(combT[:, :, :], psA[:, 0:KT, :], ACT.Copy).then_inc(s("combT_done"), 1)
                act.wait_ge(s("xT_ps"), b + 1)
                act.wait_ge(s("kept"), 2 * b)
                nc.scalar.activation(xT[0][:, :, :], psA[:, 2:4, :], ACT.Copy).then_inc(s("xhi"), 1)
                act.wait_ge(s("qkT_ps"), b + 1)
                act.wait_ge(s("stored"), STORES * b)
                nc.scalar.activation(qk[:, :, :], psB[:, :, :], ACT.Silu).then_inc(s("silu_qk"), 1)
                act.wait_ge(s("kv_ps"), b + 1)
                nc.scalar.activation(kk[:, :, :], psA[:, :, 0:D], ACT.Silu)
                nc.scalar.activation(v32[:, :, :, 0:HD], psA[:, :, D:2 * D].rearrange("p t (h d) -> p t h d", d=HD),
                                     ACT.Silu).then_inc(s("silu_kv"), 1)
                act.wait_ge(s("silu_qk"), b + 1)
                nc.scalar.activation(parts[0][:, :, :], qk[:, :, :], ACT.Copy).then_inc(s("p1"), 1)
                act.wait_ge(s("r1d"), b + 1)
                nc.scalar.activation(parts[1][:, :, :], qk[:, :, :], ACT.Copy).then_inc(s("p2"), 1)
                routing.exp(act, b)
                act.wait_ge(s("gate_ps"), b + 1)
                nc.scalar.activation(sg[:, :, :], psB[:, 1:3, :].rearrange("p a (t n) -> p (a t) n", n=D),
                                     ACT.Sigmoid).then_inc(s("gate_done"), 1)

        @block.vector
        def _(dve):
            for i, (dst, src) in enumerate(((wqk, rqk), (wkv, rkv), (wr, rr))):
                dve.wait_ge(s("w_hi"), i + 1)
                nc.vector.tensor_tensor(dst[1][:, :, :], src[:, :, :], dst[0][:, :, :].bitcast(F32), ALU.subtract).then_inc(s("w_lo"), 1)
            dve.wait_ge(s("g_done"), 1)
            nc.vector.tensor_scalar(omg16[:, :], g16[:, :], -1.0, 1.0, ALU.mult, ALU.add).then_inc(s("omg_done"), 1)
            dve.wait_ge(s("omg_done"), 1)
            dve.wait_ge(s("tables"), 3)
            with dve.Fori(0, BATCHES) as b:
                dve.wait_ge(s("heads_ps"), b + 1)
                soft = psA[:, :, 0:HEADS * (HD + 1)].rearrange("p t (h w) -> p t h w", w=HD + 1)
                lin = [psB[:, :, MW * k:MW * (k + 1)] for k in range(KT)]
                nc.vector.reciprocal(r1[:, :, :], soft[:, :, :, HD]).then_inc(s("recips"), 1)
                for k in range(KT):
                    nc.vector.reciprocal(r2[:, :, k * HH:(k + 1) * HH], lin[k][:, :, P:MW]).then_inc(s("recips"), 1)
                dve.wait_ge(s("recips"), 3 * b + 3)
                nc.vector.tensor_tensor(r1[:, :, :], r1[:, :, :], omg16[:, :].unsqueeze(1).to_broadcast((P, TILES, HEADS)), ALU.mult).then_inc(s("scaled"), 1)
                nc.vector.tensor_tensor(r2[:, :, :], r2[:, :, :], g16[:, :].unsqueeze(1).to_broadcast((P, TILES, HEADS)), ALU.mult).then_inc(s("scaled"), 1)
                dve.wait_ge(s("scaled"), 2 * b + 2)
                nc.vector.tensor_tensor(t1[:, :, :].rearrange("p t (h e) -> p t h e", e=HD), soft[:, :, :, 0:HD],
                                        r1[:, :, :].unsqueeze(3).to_broadcast((P, TILES, HEADS, HD)), ALU.mult).then_inc(s("terms"), 1)
                for k in range(KT):
                    nc.vector.tensor_tensor(t2[:, :, k * P:(k + 1) * P].rearrange("p t (h e) -> p t h e", e=HD),
                                            lin[k][:, :, 0:P].rearrange("p t (h e) -> p t h e", e=HD),
                                            r2[:, :, k * HH:(k + 1) * HH].unsqueeze(3).to_broadcast((P, TILES, HH, HD)),
                                            ALU.mult).then_inc(s("terms"), 1)
                dve.wait_ge(s("terms"), 3 * b + 3)
                nc.vector.tensor_tensor(t1[:, :, :], t1[:, :, :], t2[:, :, :], ALU.add).then_inc(s("combined"), 1)
                dve.wait_ge(s("y_ps"), b + 1)
                x = xacc[:, bass.ds(b * TILES, TILES), :]
                nc.vector.tensor_tensor(x, psB[:, :, 0:D], x, ALU.add).then_inc(s("residual"), 1)
                dve.wait_ge(s("omg_done"), 1)
                dve.wait_ge(s("residual"), b + 1)
                norm.vector(dve, b, xacc, xn)
                dve.wait_ge(s("xhi"), b + 1)
                dve.wait_ge(s("kept"), 2 * b)
                nc.vector.tensor_tensor(xT[1][:, :, :], psA[:, 2:4, :], xT[0][:, :, :].bitcast(F32), ALU.subtract).then_inc(s("xlo"), 1)
                dve.wait_ge(s("silu_qk"), b + 1)
                dve.wait_ge(s("stored"), STORES * b)
                nc.vector.tensor_tensor(qd[:, :, :].rearrange("p k (c n) -> p k c n", n=CH),
                                        qk[:, 0:KT, :].rearrange("p k (c n) -> p k c n", n=CH),
                                        qdec[:, :, :].unsqueeze(2).to_broadcast((P, KT, SEQ // CH, CH)), ALU.mult).then_inc(s("qd_done"), 1)
                dve.wait_ge(s("silu_kv"), b + 1)
                nc.vector.tensor_tensor(kd[:, :, :].rearrange("p t (h e) -> p t h e", e=HD),
                                        kk[:, :, :].rearrange("p t (h e) -> p t h e", e=HD),
                                        kdec[:, :].unsqueeze(1).unsqueeze(3).to_broadcast((P, TILES, HEADS, HD)), ALU.mult).then_inc(s("kd_done"), 1)
                dve.wait_ge(s("low_ps"), b + 1)
                small = psB[:, 0, 0:TILES * RW].rearrange("p (t n) -> p t n", n=RW)
                nc.vector.tensor_copy(low[:, :, :], small[:, :, E:RW]).then_inc(s("low_done"), 1)
                dve.wait_ge(s("lowT_ps"), b + 1)
                nc.vector.tensor_copy(lowT[:, :], psB[0:HD, 3, :]).then_inc(s("lowT_done"), 1)
                routing.vector(dve, b, small[:, :, 0:E], comb1[:, bass.ds(b * TILES, TILES), :])

        @block.tensor
        def _(pe):
            pe.wait_ge(s("consts_in"), 112)
            pe.wait_ge(s("weights_in"), 128)
            pe.wait_ge(s("w_lo"), 3)
            with pe.Fori(0, BATCHES) as b:
                pe.wait_ge(s("att_in"), 32 * b + 32)
                pe.wait_ge(s("kd_done"), b)
                pe.wait_ge(s("gate_done"), b)
                pe.wait_ge(s("lowT_done"), b)
                pe.wait_ge(routing.copied, b)
                for t in range(TILES):
                    c = slice(t * P, (t + 1) * P)
                    w = HG * (HD + 1)
                    for g in range(GROUPS):
                        nc.tensor.matmul(psA[:, t, g * w:(g + 1) * w], outT[:, g, c], sel[:, :], start=True, stop=True,
                                         skip_group_check=True)
                    for k in range(KT):
                        mm = nc.tensor.matmul(psB[:, t, MW * k:MW * (k + 1)], qf[:, k, c],
                                              mem[:, bass.ds(b * KT + k, 1), :].rearrange("p a n -> p (a n)"),
                                              start=True, stop=True, skip_group_check=True)
                mm.then_inc(s("heads_ps"), 1)
                pe.wait_ge(s("combined"), b + 1)
                for t in range(TILES):
                    for k in range(KT):
                        mm = nc.tensor.transpose(psA[:, k, t * P:(t + 1) * P], t1[:, t, k * P:(k + 1) * P], ident[:, :])
                mm.then_inc(s("combT_ps"), 1)
                pe.wait_ge(s("combT_done"), b + 1)
                for t in range(TILES):
                    for k in range(KT):
                        mm = nc.tensor.matmul(psB[:, t, 0:D], combT[:, k, t * P:(t + 1) * P], wo[:, k, :],
                                              start=k == 0, stop=k == KT - 1)
                mm.then_inc(s("y_ps"), 1)
                pe.wait_ge(norm.xn_done, TILES * b + TILES)
                for t in range(TILES):
                    for k in range(KT):
                        mm = nc.tensor.transpose(psA[:, 2 + k, t * P:(t + 1) * P], xn[:, t, k * P:(k + 1) * P], ident[:, :])
                mm.then_inc(s("xT_ps"), 1)
                pe.wait_ge(s("xlo"), b + 1)
                for m in range(4):
                    c = slice(m * P, (m + 1) * P)
                    mm = three(nc, psB[:, m, :], [(wqk[0][:, k, c], wqk[1][:, k, c], xT[0][:, k, :], xT[1][:, k, :])
                                                  for k in range(KT)])
                mm.then_inc(s("qkT_ps"), 1)
                for t in range(TILES):
                    c = slice(t * P, (t + 1) * P)
                    mm = three(nc, psA[:, t, :], [(xT[0][:, k, c], xT[1][:, k, c], wkv[0][:, k, :], wkv[1][:, k, :])
                                                  for k in range(KT)])
                mm.then_inc(s("kv_ps"), 1)
                pe.wait_ge(s("silu_qk"), b + 1)
                for t in range(TILES):
                    c = slice(t * P, (t + 1) * P)
                    mm = three(nc, psB[:, 0, t * RW:(t + 1) * RW],
                               [(xT[0][:, k, c], xT[1][:, k, c], wr[0][:, k, :], wr[1][:, k, :]) for k in range(KT)])
                mm.then_inc(s("low_ps"), 1)
                pe.wait_ge(s("low_done"), b + 1)
                for t in range(TILES):
                    mm = nc.tensor.transpose(psB[0:HD, 3, t * P:(t + 1) * P], low[:, t, :], ident[:, :])
                mm.then_inc(s("lowT_ps"), 1)
                pe.wait_ge(s("lowT_done"), b + 1)
                for t in range(TILES):
                    mm = nc.tensor.matmul(psB[:, 1 + t // 2, (t % 2) * D:(t % 2 + 1) * D], lowT[:, t * P:(t + 1) * P],
                                          wg2[:, :], start=True, stop=True, skip_group_check=True)
                mm.then_inc(s("gate_ps"), 1)


AHEAD = 2
HSLOTS = 4
NC = SEQ // CH
UPDATES = NC - 1
SPAN = BATCHES * HT1 * 2 // NC


def layer1_main(nc, io, scratch, keep, out):
    with ExitStack() as ctx:
        def sb(name, shape, dt=F32):
            return ctx.enter_context(nc.sbuf_tensor("d_" + name, shape, dt))

        def sem(name):
            return stage_semaphore(nc, keep, "d_" + name)

        def sems(name, n):
            return [sem(f"{name}{i}") for i in range(n)]

        xacc, xT, comb1 = keep["xacc"], keep["xT1"], keep["comb1"]
        G, U, DN = KT * H1, KT * H1, HT1 * D
        raw = [sb(f"raw{i}", [P, n]) for i, n in enumerate((G, U, DN))]
        w = [[[sb(f"w{e}{i}{j}", [P, n], F32R) for j in range(2)] for i, n in enumerate((G, U, DN))] for e in range(2)]
        h = [sb(f"h{i}", [P, SEQ]) for i in range(HSLOTS)]
        hh = [[sb(f"hh{i}{j}", [P, SEQ], F32R) for j in range(2)] for i in range(HSLOTS)]
        ident, sel, blockmask = sb("ident", [P, P]), sb("sel", [P, HG * HD]), sb("blockmask", [P, P])
        rel, causal = sb("rel", [P, P]), sb("causal", [P, P])
        ldall, ldrows, cdec = sb("ldall", [P, HEADS]), sb("ldrows", [P, KT]), sb("cdec", [P, KT])
        normw, neghalf, wo = sb("normw", [P, D]), sb("neghalf", [P, HEADS]), sb("wo", [P, KT, D])
        decay = sb("decay", [P, HEADS, CH])
        qst, kst = ([sb(f"{n}{s}", [STACK, HEADS, CH], BF16) for s in range(2)] for n in ("qst", "kst"))
        v = [sb(f"v{s}", [P, HEADS, VW]) for s in range(2)]
        kd, sg, qd = ([sb(f"{n}{s}", [P, D]) for s in range(2)] for n in ("kd", "sg", "qd"))
        probs = [sb(f"probs{g}", [P, HG * CH]) for g in range(GROUPS)]
        headsT = sb("headsT", [P, GROUPS * CH])
        state, update = sb("state", [P, KT, P]), sb("update", [P, KT, P])
        o, sq, ss, rs = sb("o", [P, D]), sb("sq", [P, D]), sb("ss", [P, HEADS]), sb("rs", [P, HEADS])
        normed, normT = sb("normed", [P, D]), sb("normT", [P, KT, P])

        psG = ctx.enter_context(nc.psum_tensor("d_psG", [P, 4, SEQ], F32))
        psY = ctx.enter_context(nc.psum_tensor("d_psY", [P, TILES, D], F32))
        ps0, ps1 = (ctx.enter_context(nc.psum_tensor(f"d_ps{i}", [P, SEQ], F32)) for i in range(2))

        raw_in, w_hi, w_lo = sems("raw_in", 3), sems("w_hi", 3), sems("w_lo", 3)
        gate_up_ps, silu_done, hi_done, added = sem("gate_up_ps"), sem("silu"), sem("hi"), sem("added")
        mult_done, lo_done, down_ps = sems("mult", 2), sems("lo", HSLOTS), sems("down_ps", HSLOTS)
        consts_in, tables, masked, cdec_done, neghalf_set = (sem(n) for n in ("consts", "tables", "masked", "cdec", "neghalf"))
        chunk_in, gated = sems("chunk_in", 2), sems("gated", 2)
        scores_ps, probs_done, probs_used = sems("scores_ps", GROUPS), sems("probs", GROUPS), sem("probs_used")
        heads_copied, update_ps, update_done, state_done = (sem(n) for n in ("heads_copied", "update_ps", "update", "state"))
        out_ps, squared, summed, ss_done, rs_done = (sem(n) for n in ("out_ps", "squared", "summed", "ss", "rs"))
        scaled, normed_done, normT_ps, normT_done, y_ps, y_done = (
            sem(n) for n in ("scaled", "normed", "normT_ps", "normT", "y_ps", "y"))
        stored = sem("stored")
        N = BATCHES * HT1
        PAIR = 2 * N
        CONSTS = 9
        CHUNK_IN = 16 * (2 * len(Q_PARTS) + 4)

        def loop(eng, run):
            with eng.Fori(0, E // 2 - 1) as i:
                run(i, False)
            run(E // 2 - 1, True)

        def tiles(i, last, tile, steps):
            for t in range(PAIR):
                if t + AHEAD < PAIR:
                    tile(i, t + AHEAD, last)
                elif not last:
                    tile(i + 1, t + AHEAD - PAIR, False)
                yield t, steps.get((t % SPAN, 0)), steps.get((t % SPAN, 1))

        def view(t, k):
            return t[:, :].rearrange("p (k n) -> p k n", k=k)

        def other_expert(i, t, last):
            half, piece = t // N, t % N - 1
            if not 0 <= piece < 3 or (last and half):
                return None
            return piece, 2 * i + 1 + half, PAIR // HSLOTS * i + half * N // HSLOTS

        block = ctx.enter_context(nc.Block())

        @block.sync
        def _(sp):
            def load_weights(x):
                for i, (name, k) in enumerate((("gate1", KT), ("up1", KT), ("down1", HT1))):
                    sp.wait_ge(w_lo[i], x)
                    weights = io[name][x] if isinstance(x, int) else io[name][bass.ds(x, 1), :, :].rearrange("a r n -> (a r) n")
                    sp.dma_start(view(raw[i], k), weights.rearrange("(k p) n -> p k n", p=P)).then_inc(raw_in[i], 16)

            def load_chunk(b, c):
                s, t = c % 2, slice(c * CH, (c + 1) * CH)
                sp.wait_ge(gated[s], 2 * b + c // 2)
                for op, dst, order in ((0, qst, Q_PARTS), (1, kst, K_PARTS)):
                    for n, part in enumerate(order):
                        sp.dma_start(dst[s][n * HD:(n + 1) * HD, :, :],
                                     scratch["parts1"][b, part, KT * op:KT * (op + 1), :, t]
                                     .rearrange("k (h d) t -> d (k h) t", d=HD)).then_inc(chunk_in[s], 16)
                sp.dma_start(v[s][:, :, :].rearrange("p h w -> p (h w)"), scratch["v1"][b, t, :]).then_inc(chunk_in[s], 16)
                sp.dma_start(kd[s][:, :], scratch["kd"][b, t, :]).then_inc(chunk_in[s], 16)
                sp.dma_start(sg[s][:, :], scratch["sg"][b, t, :]).then_inc(chunk_in[s], 16)
                sp.dma_start(view(qd[s], KT), scratch["qd"][b, :, :, t].rearrange("k p n -> p k n")).then_inc(chunk_in[s], 16)

            load_weights(0)
            for dst, src in ((ident[:, :], io["ident"]), (sel[:, :], io["sel16"]), (blockmask[:, :], io["blockmask"]),
                             (rel[:, :], io["rel"]), (causal[:, :], io["causal"]),
                             (ldall[:, :], io["log_decay"].to_broadcast((P, HEADS))), (ldrows[:, :], io["log_decay_rows"]),
                             (normw[:, :], io["norm_w"].to_broadcast((P, D))),
                             (wo[:, :, :], io["Wo1"].rearrange("(k p) n -> p k n", p=P))):
                sp.dma_start(dst, src).then_inc(consts_in, 16)
            load_chunk(0, 0)
            load_chunk(0, 1)
            load_weights(1)

            def run(i, last):
                load_chunk(i, 2)
                if not last:
                    load_weights(2 * i + 2)
                load_chunk(i, 3)
                if not last:
                    load_weights(2 * i + 3)
                    load_chunk(i + 1, 0)
                    load_chunk(i + 1, 1)

            loop(sp, run)
            for b in range(BATCHES):
                sp.wait_ge(added, 2 * BATCHES * (E // 2 - 1) + BATCHES + b + 1)
                sp.wait_ge(y_done, NC * min(b + 1, BATCHES))
                sp.dma_start(out[b * SEQ:(b + 1) * SEQ, :].rearrange("(t p) d -> p t d", p=P),
                             xacc[:, b * TILES:(b + 1) * TILES, :]).then_inc(stored, 16)
            sp.wait_ge(stored, 16 * BATCHES)

        @block.gpsimd
        def _(pool):
            def tile(i, t, last):
                s = t % HSLOTS
                pool.wait_ge(hi_done, PAIR * i + t + 1)
                nc.gpsimd.tensor_tensor(hh[s][1][:, :], h[s][:, :], hh[s][0][:, :].bitcast(F32),
                                        ALU.subtract).then_inc(lo_done[s], 1)

            def power(i, c):
                pool.wait_ge(ss_done, NC * i + c + 1)
                nc.gpsimd.tensor_tensor(rs[:, :], ss[:, :], neghalf[:, :], ALU.pow).then_inc(rs_done, 1)

            nc.gpsimd.memset(neghalf[:, :], -0.5).then_inc(neghalf_set, 1)
            pool.wait_ge(neghalf_set, 1)
            for t in range(AHEAD):
                tile(0, t, False)

            def run(i, last):
                for t, *steps in tiles(i, last, tile, {(5, 0): power}):
                    for step in filter(None, steps):
                        step(i, t // SPAN)

            loop(pool, run)

        @block.scalar
        def _(act):
            def split_hi(e, piece, x):
                act.wait_ge(raw_in[piece], 16 * x + 16)
                nc.scalar.activation(w[e][piece][0][:, :], raw[piece][:, :], ACT.Copy).then_inc(w_hi[piece], 1)

            def tile(i, t, last):
                s = t % HSLOTS
                act.wait_ge(gate_up_ps, PAIR * i + t + 1)
                act.wait_ge(lo_done[s], PAIR // HSLOTS * i + t // HSLOTS)
                nc.scalar.activation(h[s][:, :], psG[:, 2 * (t % 2), :], ACT.Silu).then_inc(silu_done, 1)
                if found := other_expert(i, t, last):
                    act.wait_ge(down_ps[HSLOTS - 1], found[2])
                    split_hi((t // N + 1) % 2, found[0], found[1])
                act.wait_ge(mult_done[t % 2], PAIR // 2 * i + t // 2 + 1)
                act.wait_ge(down_ps[s], PAIR // HSLOTS * i + t // HSLOTS)
                nc.scalar.activation(hh[s][0][:, :], h[s][:, :], ACT.Copy).then_inc(hi_done, 1)

            def copy_heads(i, c):
                act.wait_ge(probs_used, NC * i + c + 1)
                act.wait_ge(out_ps, NC * i + c)
                nc.scalar.activation(headsT[:, :], ps0[:, :], ACT.Copy).then_inc(heads_copied, 1)

            def copy_normT(i, c):
                act.wait_ge(normT_ps, NC * i + c + 1)
                act.wait_ge(y_ps, NC * i + c)
                nc.scalar.activation(normT[:, :, :], ps1[:, 0:KT * P].rearrange("p (k n) -> p k n", k=KT),
                                     ACT.Copy).then_inc(normT_done, 1)

            for piece in range(3):
                split_hi(0, piece, 0)
            for t in range(AHEAD):
                tile(0, t, False)
            act.wait_ge(consts_in, 16 * CONSTS)
            for n in range(HEADS):
                nc.scalar.activation(decay[:, n, :], rel[:, :], ACT.Exp, scale=ldall[:, n:n + 1]).then_inc(tables, 1)
            nc.scalar.activation(cdec[:, :], ldrows[:, :], ACT.Exp, scale=float(CH)).then_inc(cdec_done, 1)

            def run(i, last):
                for t, *steps in tiles(i, last, tile, {(3, 1): copy_heads, (6, 1): copy_normT}):
                    for step in filter(None, steps):
                        step(i, t // SPAN)

            loop(act, run)

        @block.vector
        def _(dve):
            def split_lo(e, piece, x):
                dve.wait_ge(w_hi[piece], x + 1)
                nc.vector.tensor_tensor(w[e][piece][1][:, :], raw[piece][:, :], w[e][piece][0][:, :].bitcast(F32),
                                        ALU.subtract).then_inc(w_lo[piece], 1)

            def tile(i, t, last):
                s = t % HSLOTS
                dve.wait_ge(silu_done, PAIR * i + t + 1)
                nc.vector.tensor_tensor(h[s][:, :], h[s][:, :], psG[:, 2 * (t % 2) + 1, :],
                                        ALU.mult).then_inc(mult_done[t % 2], 1)
                if found := other_expert(i, t, last):
                    split_lo((t // N + 1) % 2, found[0], found[1])

            def add(i, t):
                dve.wait_ge(down_ps[HSLOTS - 1], PAIR // HSLOTS * i + t // HSLOTS + 1)
                dve.wait_ge(y_done, NC * i + (t + 1) // SPAN)
                for k in range(TILES):
                    rows = t // HT1 % BATCHES * TILES + k
                    weight = comb1[:, rows, bass.ds(2 * i + t // N, 1)] if not isinstance(i, int) else \
                        comb1[:, rows, 2 * i + t // N:2 * i + t // N + 1]
                    last = nc.vector.scalar_tensor_tensor(xacc[:, rows, :], psY[:, k, :], weight,
                                                          xacc[:, rows, :], ALU.mult, ALU.add)
                last.then_inc(added, 1)

            def weigh(g):
                def step(i, c):
                    dve.wait_ge(scores_ps[g], NC * i + c + 1)
                    dve.wait_ge(probs_used, NC * i + c)
                    nc.vector.tensor_tensor(probs[g][:, :], (ps1 if g % 2 else ps0)[:, :],
                                            decay[:, HG * g:HG * g + HG, :].rearrange("p h c -> p (h c)"),
                                            ALU.mult).then_inc(probs_done[g], 1)
                return step

            def take_update(i, c):
                if c == NC - 1:
                    return
                dve.wait_ge(update_ps, UPDATES * i + c + 1)
                nc.vector.tensor_tensor((update if c else state)[:, :, :], ps1[:, 0:KT * P].rearrange("p (k n) -> p k n", k=KT),
                                        blockmask[:, :].unsqueeze(1).to_broadcast((P, KT, P)), ALU.mult).then_inc(update_done, 1)

            def gate(i, c):
                s = c % 2
                dve.wait_ge(out_ps, NC * i + c + 1)
                nc.vector.tensor_tensor(o[:, :], ps0[:, 0:D], sg[s][:, :], ALU.mult).then_inc(gated[s], 1)
                if 0 < c < NC - 1:
                    dve.wait_ge(update_done, UPDATES * i + c + 1)
                    dve.wait_ge(state_done, (UPDATES - 1) * i + c - 1)
                    for k in range(KT):
                        last = nc.vector.scalar_tensor_tensor(state[:, k, :], state[:, k, :], cdec[:, k:k + 1], update[:, k, :],
                                                              ALU.mult, ALU.add)
                    last.then_inc(state_done, 1)
                dve.wait_ge(gated[s], 2 * i + c // 2 + 1)
                nc.vector.tensor_tensor(sq[:, :], o[:, :], o[:, :], ALU.mult).then_inc(squared, 1)
                dve.wait_ge(squared, NC * i + c + 1)
                nc.vector.tensor_reduce(ss[:, :], sq[:, :].rearrange("p (h d) -> p h d", d=HD), AX_X, ALU.add).then_inc(summed, 1)
                dve.wait_ge(summed, NC * i + c + 1)
                nc.vector.tensor_scalar(ss[:, :], ss[:, :], 1.0 / HD, EPS, ALU.mult, ALU.add).then_inc(ss_done, 1)

            def normalise(i, c):
                dve.wait_ge(rs_done, NC * i + c + 1)
                nc.vector.tensor_tensor(o[:, :].rearrange("p (h d) -> p h d", d=HD), o[:, :].rearrange("p (h d) -> p h d", d=HD),
                                        rs[:, :].unsqueeze(2).to_broadcast((P, HEADS, HD)), ALU.mult).then_inc(scaled, 1)
                dve.wait_ge(scaled, NC * i + c + 1)
                dve.wait_ge(normT_ps, NC * i + c)
                nc.vector.tensor_tensor(normed[:, :], o[:, :], normw[:, :], ALU.mult).then_inc(normed_done, 1)

            def residual(i, c):
                dve.wait_ge(y_ps, NC * i + c + 1)
                dve.wait_ge(added, PAIR // HT1 * i + (SPAN * (c + 1) - 1) // HT1)
                x = xacc[:, bass.ds(NC * i + c, 1), :].rearrange("p a d -> p (a d)")
                nc.vector.tensor_tensor(x, ps0[:, 0:D], x, ALU.add).then_inc(y_done, 1)

            for piece in range(3):
                split_lo(0, piece, 0)
            for t in range(AHEAD):
                tile(0, t, False)
            dve.wait_ge(tables, HEADS)
            nc.vector.tensor_tensor(decay[:, :, :], decay[:, :, :], causal[:, :].unsqueeze(1).to_broadcast((P, HEADS, CH)),
                                    ALU.mult).then_inc(masked, 1)
            dve.wait_ge(cdec_done, 1)
            dve.wait_ge(masked, 1)

            def run(i, last):
                steps = {(0, 0): weigh(0), (0, 1): weigh(1), (1, 1): weigh(2), (2, 0): weigh(3), (4, 0): take_update,
                         (5, 0): gate, (6, 0): normalise, (7, 1): residual}
                for t, *found in tiles(i, last, tile, steps):
                    for step in filter(None, found):
                        step(i, t // SPAN)
                    if t % HT1 == HT1 - 1:
                        add(i, t)

            loop(dve, run)

        @block.tensor
        def _(pe):
            def tile(i, t, last):
                if t % N == 0:
                    for piece in range(2):
                        pe.wait_ge(w_lo[piece], 2 * i + t // N + 1)
                pe.wait_ge(mult_done[t % 2], PAIR // 2 * i + t // 2)
                m, chunk = t % HT1, t // HT1 % BATCHES
                for j in range(2):
                    hi, lo = (view(x, KT)[:, :, m * P:(m + 1) * P] for x in w[t // N][j])
                    c = slice(chunk * SEQ, (chunk + 1) * SEQ)
                    mm = three(nc, psG[:, 2 * (t % 2) + j, :], [(hi[:, k, :], lo[:, k, :], xT[0][:, k, c], xT[1][:, k, c])
                                                                for k in range(KT)])
                mm.then_inc(gate_up_ps, 1)

            def down(i, t):
                s, m, chunk = t % HSLOTS, t % HT1, t // HT1
                if t % N == 0:
                    pe.wait_ge(w_lo[2], 2 * i + t // N + 1)
                if m == 0:
                    pe.wait_ge(added, PAIR // HT1 * i + chunk)
                pe.wait_ge(lo_done[s], PAIR // HSLOTS * i + t // HSLOTS + 1)
                hi, lo = (view(x, HT1)[:, m, :] for x in w[t // N][2])
                for k in range(TILES):
                    c = slice(k * P, (k + 1) * P)
                    mm = three(nc, psY[:, k, :], [(hh[s][0][:, c], hh[s][1][:, c], hi, lo)],
                               start=m == 0 and k % 2 == 0, last=m == HT1 - 1)
                mm.then_inc(down_ps[s], 1)

            def scores(g):
                def step(i, c):
                    s = c % 2
                    if g == 0:
                        pe.wait_ge(chunk_in[s], CHUNK_IN * (2 * i + c // 2 + 1))
                        pe.wait_ge(y_done, NC * i + c)
                    elif g == 1:
                        pe.wait_ge(normT_done, NC * i + c)
                    else:
                        pe.wait_ge(probs_done[g - 2], NC * i + c + 1)
                    for n in range(HG):
                        mm = nc.tensor.matmul((ps1 if g % 2 else ps0)[:, n * CH:(n + 1) * CH], kst[s][:, HG * g + n, :],
                                              qst[s][:, HG * g + n, :], start=True, stop=True, skip_group_check=True)
                    mm.then_inc(scores_ps[g], 1)
                return step

            def own(i, c):
                for g in range(GROUPS):
                    pe.wait_ge(probs_done[g], NC * i + c + 1)
                for g in range(GROUPS):
                    for n in range(HG):
                        mm = nc.tensor.matmul(ps0[VW * n:VW * (n + 1), g * CH:(g + 1) * CH], v[c % 2][:, HG * g + n, :],
                                              probs[g][:, n * CH:(n + 1) * CH], start=True, stop=True,
                                              tile_position=(0, VW * n), skip_group_check=True)
                mm.then_inc(probs_used, 1)

            def updates(i, c):
                if c == NC - 1:
                    return
                pe.wait_ge(probs_done[GROUPS - 1], NC * i + c + 1)
                for k in range(KT):
                    mm = nc.tensor.matmul(ps1[:, k * P:(k + 1) * P], kd[c % 2][:, k * P:(k + 1) * P],
                                          v[c % 2][:, k * HH:(k + 1) * HH, 0:HD], start=True, stop=True, skip_group_check=True)
                mm.then_inc(update_ps, 1)

            def outputs(i, c):
                pe.wait_ge(heads_copied, NC * i + c + 1)
                if c == 1:
                    pe.wait_ge(update_done, UPDATES * i + 1)
                elif c:
                    pe.wait_ge(state_done, (UPDATES - 1) * i + c - 1)
                if c:
                    for k in range(KT):
                        nc.tensor.matmul(ps0[:, k * P:(k + 1) * P], qd[c % 2][:, k * P:(k + 1) * P], state[:, k, :],
                                         start=k == 0, stop=False, skip_group_check=True)
                for g in range(GROUPS):
                    mm = nc.tensor.matmul(ps0[:, g * HG * HD:(g + 1) * HG * HD], headsT[:, g * CH:(g + 1) * CH], sel[:, :],
                                          start=c == 0 and g == 0, stop=g == GROUPS - 1, skip_group_check=True)
                mm.then_inc(out_ps, 1)

            def turn(i, c):
                pe.wait_ge(normed_done, NC * i + c + 1)
                if c < NC - 1:
                    pe.wait_ge(update_done, UPDATES * i + c + 1)
                for k in range(KT):
                    mm = nc.tensor.transpose(ps1[:, k * P:(k + 1) * P], normed[:, k * P:(k + 1) * P], ident[:, :])
                mm.then_inc(normT_ps, 1)

            def project(i, c):
                pe.wait_ge(normT_done, NC * i + c + 1)
                pe.wait_ge(gated[c % 2], 2 * i + c // 2 + 1)
                for k in range(KT):
                    mm = nc.tensor.matmul(ps0[:, 0:D], normT[:, k, :], wo[:, k, :], start=k == 0, stop=k == KT - 1)
                mm.then_inc(y_ps, 1)

            pe.wait_ge(consts_in, 16 * CONSTS)
            for t in range(AHEAD):
                tile(0, t, False)

            def run(i, last):
                steps = {(0, 0): scores(0), (0, 1): scores(1), (1, 1): scores(2), (2, 0): scores(3), (3, 1): own,
                         (4, 0): updates, (5, 0): outputs, (6, 1): turn, (7, 1): project}
                for t, before, behind in tiles(i, last, tile, steps):
                    if before:
                        before(i, t // SPAN)
                    down(i, t)
                    if behind:
                        behind(i, t // SPAN)

            loop(pe, run)


def two_layers(nc, io, out):
    with ExitStack() as ctx:
        def sb(name, shape, dt=F32):
            return ctx.enter_context(nc.sbuf_tensor(name, shape, dt))

        def dram(name, shape, dt=F32):
            return nc.dram_tensor("scratch_" + name, shape, dt, kind="Internal").ap()

        scratch = {
            "cT": dram("cT", (BATCHES, E, SEQ)),
            "v": dram("v", (BATCHES, SEQ, HEADS * VW)),
            "qf": dram("qf", (BATCHES, KT, P, SEQ)),
            "parts": dram("parts", (BATCHES, 3, 2 * KT, P, SEQ), BF16),
            "max": dram("max", (2 * HG, SEQ), BF16),
            "outT": dram("outT", (BATCHES, GROUPS, P, SEQ)),
            "v1": dram("v1", (BATCHES, SEQ, HEADS * VW)),
            "kd": dram("kd", (BATCHES, SEQ, D)),
            "qd": dram("qd", (BATCHES, KT, P, SEQ)),
            "parts1": dram("parts1", (BATCHES, 3, 2 * KT, P, SEQ), BF16),
            "sg": dram("sg", (BATCHES, SEQ, D)),
        }
        keep = {"xacc": sb("xacc", [P, TOK // P, D]), "semaphores": []}
        with ExitStack() as inner:
            keep["mem"] = inner.enter_context(nc.sbuf_tensor("mem", [P, BATCHES * KT, MW], F32))
            layer0_front(nc, io, scratch, keep)
            end_stage(nc, keep)
            layer0_attention(nc, io, scratch, keep)
            end_stage(nc, keep)
            keep["xT1"] = [inner.enter_context(nc.sbuf_tensor(f"xT1{i}", [P, KT, TOK], F32R)) for i in range(2)]
            keep["comb1"] = inner.enter_context(nc.sbuf_tensor("comb1", [P, TOK // P, E], F32))
            layer1_front(nc, io, scratch, keep)
            end_stage(nc, keep)
            layer1_main(nc, io, scratch, keep, out)


def constants():
    import numpy as np
    f = np.arange(512, dtype=np.float32)[None, :] * (np.float32(1.0) / np.float32(10000.0) ** (np.arange(0, 256, 2, dtype=np.float32) / np.float32(256)))[:, None]
    p = np.arange(128)
    c = {}
    c['ident'] = np.eye(128, dtype=np.float32)
    c['cos'], c['sin'] = np.cos(f).astype(np.float32), np.sin(f).astype(np.float32)
    c['blockmask'] = (p[:, None] // 16 == p[None, :] // 16).astype(np.float32)
    c['headmask'] = (p[:, None] // 16 == np.arange(8)[None, :]).astype(np.float32)
    c['iota8'] = np.tile(np.arange(8, dtype=np.float32), (128, 4))
    sel = np.zeros((128, 4, 17), np.float32)
    for g in range(4):
        for j in range(17):
            sel[32 * g + j, g, j] = 1
    c['sel17'] = sel.reshape(128, 68)
    c['sel16'] = np.ascontiguousarray(sel[:, :, :16]).reshape(128, 64)
    c['rel'] = np.maximum(p[None, :] - p[:, None], 0).astype(np.float32)
    c['causal'] = (p[None, :] >= p[:, None]).astype(np.float32)
    c['after'] = np.tile((p + 1).astype(np.float32), (128, 1))
    c['before'] = (127 - p).astype(np.float32)[:, None].copy()
    return c


def layout(g):
    import numpy as np
    C = np.ascontiguousarray
    arrays = {"x": g["L0_attn_hidden_states"]}
    for n in ("Wq", "Wk", "Wv", "Wo"):
        arrays[n + "0"] = C(g["L0_attn_" + n].T)
        arrays[n + "1"] = g["L1_attn_" + n]
    arrays["gate_attn"] = C(g["L0_attn_gate"].reshape(1, HEADS))
    arrays["router0"] = C(g["L0_ffn_gate_w"].T)
    arrays["gate0"] = C(g["L0_ffn_gate_proj"].reshape(E * F0, D).T)
    arrays["up0"] = C(g["L0_ffn_up_proj"].reshape(E * F0, D).T)
    arrays["down0"] = C(g["L0_ffn_down_proj"].transpose(0, 2, 1)).reshape(E * F0, D)
    arrays["log_decay"] = g["L1_attn_log_decay"].reshape(1, HEADS)
    arrays["log_decay_rows"] = C(np.repeat(g["L1_attn_log_decay"].reshape(KT, HH), HD, axis=1).T)
    arrays["Wg1"], arrays["Wg2"] = g["L1_attn_Wg1"], g["L1_attn_Wg2"]
    arrays["norm_w"] = g["L1_attn_norm_w"].reshape(1, D)
    arrays["router1"] = g["L1_ffn_w_router"]
    arrays["gate1"], arrays["up1"], arrays["down1"] = g["L1_ffn_w_gate"], g["L1_ffn_w_up"], g["L1_ffn_w_down"]
    return arrays


def kernel(**inputs):
    import numpy as np
    import concourse.bacc as bacc
    from concourse.bass_utils import run_bass_kernel_spmd

    arrays = layout({name: np.asarray(a) for name, a in inputs.items()})
    arrays.update(constants())
    nc = bacc.Bacc("TRN2", target_bir_lowering=False, num_devices=1)
    io = {}
    for name, a in arrays.items():
        io[name] = nc.dram_tensor(f"in_{name}_dram", a.shape, mybir.dt.from_np(a.dtype), kind="ExternalInput").ap()
    out = nc.dram_tensor("out_0_dram", (BATCHES, SEQ, D), F32, kind="ExternalOutput").ap()
    two_layers(nc, io, out.rearrange("b s d -> (b s) d"))
    r = run_bass_kernel_spmd(nc, [{f"in_{name}_dram": np.ascontiguousarray(a) for name, a in arrays.items()}], core_ids=[0])
    return r.results[0]["out_0_dram"]
```

```python
from contextlib import ExitStack

import concourse.bass as bass
from concourse import mybir

F32 = mybir.dt.float32
F32R = mybir.dt.float32r
BF16 = mybir.dt.bfloat16
U32 = mybir.dt.uint32
ALU = mybir.AluOpType
ACT = mybir.ActivationFunctionType
AX_X = mybir.AxisListType.X

P = 128
BATCHES = 4
SEQ = 512
TOK = BATCHES * SEQ
TILES = SEQ // P
D = 256
KT = D // P
HEADS = 16
HD = D // HEADS
HG = 4
GROUPS = HEADS // HG
HH = HEADS // KT
EPS = 1e-5
E = 8
F0 = 176
FT0 = E * F0 // P
H1 = 512
HT1 = H1 // P
HSLOTS = 4
EXPERT_WEIGHTS = (("gate1", KT), ("up1", KT), ("down1", HT1))
STORES1 = 4
PARTS1 = 3
CH = 128
VW = 32
MW = HH * (HD + 1)
Q_PARTS = (0, 0, 1, 0, 2, 1)
K_PARTS = (0, 1, 0, 2, 0, 1)
STACK = len(Q_PARTS) * HD
STACKM = STACK + 2


def three(nc, out, pairs, last=True, start=True):
    n = len(pairs)
    for i, (ah, al, bh, bl) in enumerate(pairs):
        nc.tensor.matmul(out, ah, bh, start=start and i == 0, stop=False, skip_group_check=True)
        nc.tensor.matmul(out, ah, bl, start=False, stop=False, skip_group_check=True)
        mm = nc.tensor.matmul(out, al, bh, start=False, stop=last and i == n - 1, skip_group_check=True)
    return mm


def stage_semaphore(nc, keep, name):
    handle = nc.alloc_semaphore(name)
    keep["semaphores"].append(handle)
    return handle


def end_stage(nc, keep):
    nc.clear_and_free_semaphores(keep["semaphores"])
    keep["semaphores"] = []
    nc.all_engine_barrier()


class Norm:

    def __init__(self, nc, sb, sem):
        self.nc = nc
        self.stats, self.mv = sb("ln_stats", [P, TILES, 6]), sb("ln_mv", [P, TILES, 2])
        self.vare, self.rstd = sb("ln_vare", [P, TILES]), sb("ln_rstd", [P, TILES])
        self.neghalf, self.held = sb("ln_neghalf", [P, TILES]), sb("ln_held", [P, 1])
        self.neghalf_set, self.stats_done, self.mv_done = sem("ln_neghalf"), sem("ln_stats"), sem("ln_mv")
        self.vare_done, self.rstd_done, self.xn_done = sem("ln_vare"), sem("ln_rstd"), sem("ln_xn")

    def setup(self, pool):
        self.nc.gpsimd.memset(self.neghalf[:, :], -0.5).then_inc(self.neghalf_set, 1)
        pool.wait_ge(self.neghalf_set, 1)

    def power(self, pool, b):
        pool.wait_ge(self.vare_done, b + 1)
        self.nc.gpsimd.tensor_tensor(self.rstd[:, :], self.vare[:, :], self.neghalf[:, :],
                                     ALU.pow).then_inc(self.rstd_done, 1)

    def rows(self, xacc, b, t):
        return xacc[:, bass.ds(b * TILES + t, 1), :].rearrange("p a d -> p (a d)")

    def moments(self, dve, b, xacc):
        nc = self.nc
        for t in range(TILES):
            last = nc.vector.bn_stats(self.stats[:, t, :], self.rows(xacc, b, t))
        last.then_inc(self.stats_done, 1)
        dve.wait_ge(self.stats_done, b + 1)
        nc.vector.memset(self.held[:, :], 0.0)
        for t in range(TILES):
            nc.vector.bn_aggr(self.mv[:, t, :], self.stats[:, t, :]).then_inc(self.mv_done, 1)
        dve.wait_ge(self.mv_done, (b + 1) * TILES)
        nc.vector.tensor_scalar(self.vare[:, :], self.mv[:, :, 1], EPS, None, ALU.add).then_inc(self.vare_done, 1)

    def apply(self, dve, b, xacc, xn):
        nc = self.nc
        dve.wait_ge(self.rstd_done, b + 1)
        for t in range(TILES):
            nc.vector.tensor_scalar(xn[:, t, :], self.rows(xacc, b, t), self.mv[:, t, 0:1], self.rstd[:, t:t + 1],
                                    ALU.subtract, ALU.mult).then_inc(self.xn_done, 1)


class Routing:

    STEPS = 8

    def __init__(self, nc, sb, sem):
        self.nc = nc
        self.iota8 = sb("rt_iota8", [P, TILES, E])
        self.logits, self.top = sb("rt_logits", [P, TILES, E]), sb("rt_top", [P, TILES, E])
        self.idx, self.idxf = sb("rt_idx", [P, TILES, E], U32), sb("rt_idxf", [P, TILES, 2])
        self.gap, self.w1, self.w2 = sb("rt_gap", [P, TILES]), sb("rt_w1", [P, TILES]), sb("rt_w2", [P, TILES])
        self.eq = [sb(f"rt_eq{i}", [P, TILES, E]) for i in range(2)]
        self.copied, self.top_done, self.gap_done = sem("rt_copied"), sem("rt_top"), sem("rt_gap")
        self.exp_done, self.step, self.comb_done = sem("rt_exp"), sem("rt_step"), sem("rt_comb")
        self.iota_in = sem("rt_iota_in")

    def load(self, sp, io):
        sp.dma_start(self.iota8[:, :, :], io["iota8"].rearrange("p (t e) -> p t e", e=E)).then_inc(self.iota_in, 16)

    def exp(self, act, b):
        act.wait_ge(self.gap_done, b + 1)
        self.nc.scalar.activation(self.gap[:, :], self.gap[:, :], ACT.Exp).then_inc(self.exp_done, 1)

    def choose(self, dve, b, source):
        nc = self.nc
        nc.vector.tensor_copy(self.logits[:, :, :], source).then_inc(self.copied, 1)
        dve.wait_ge(self.iota_in, 16)
        dve.wait_ge(self.copied, b + 1)
        for t in range(TILES):
            nc.vector.max(self.top[:, t, :], self.logits[:, t, :]).then_inc(self.top_done, 1)
        dve.wait_ge(self.top_done, 2 * TILES * b + TILES)
        nc.vector.tensor_tensor(self.gap[:, :], self.top[:, :, 1], self.top[:, :, 0], ALU.subtract).then_inc(self.gap_done, 1)
        for t in range(TILES):
            nc.vector.max_index(self.idx[:, t, :], self.top[:, t, :], self.logits[:, t, :]).then_inc(self.top_done, 1)
        dve.wait_ge(self.top_done, 2 * TILES * (b + 1))
        nc.vector.tensor_copy(self.idxf[:, :, :], self.idx[:, :, 0:2]).then_inc(self.step, 1)
        dve.wait_ge(self.step, self.STEPS * b + 1)
        for i in range(2):
            nc.vector.tensor_tensor(self.eq[i][:, :, :], self.iota8[:, :, :],
                                    self.idxf[:, :, i:i + 1].to_broadcast((P, TILES, E)), ALU.is_equal).then_inc(self.step, 1)

    def weigh(self, dve, b, comb):
        nc = self.nc
        dve.wait_ge(self.exp_done, b + 1)
        nc.vector.tensor_scalar(self.w1[:, :], self.gap[:, :], 1.0, None, ALU.add).then_inc(self.step, 1)
        dve.wait_ge(self.step, self.STEPS * b + 4)
        nc.vector.reciprocal(self.w1[:, :], self.w1[:, :]).then_inc(self.step, 1)
        dve.wait_ge(self.step, self.STEPS * b + 5)
        nc.vector.tensor_tensor(self.w2[:, :], self.w1[:, :], self.gap[:, :], ALU.mult).then_inc(self.step, 1)
        dve.wait_ge(self.step, self.STEPS * b + 6)
        for i, w in enumerate((self.w1, self.w2)):
            nc.vector.tensor_tensor(self.eq[i][:, :, :], self.eq[i][:, :, :],
                                    w[:, :].unsqueeze(2).to_broadcast((P, TILES, E)), ALU.mult).then_inc(self.step, 1)
        dve.wait_ge(self.step, self.STEPS * b + 8)
        nc.vector.tensor_tensor(comb, self.eq[0][:, :, :], self.eq[1][:, :, :], ALU.add).then_inc(self.comb_done, 1)




FAHEAD = 2
FRONT_TILES = FT0 // 2 + 1


def layer0_front(nc, io, scratch, keep):
    with ExitStack() as ctx:
        def sb(name, shape, dt=F32):
            return ctx.enter_context(nc.sbuf_tensor("a_" + name, shape, dt))

        def sem(name):
            return stage_semaphore(nc, keep, "a_" + name)

        xacc, mem = keep["xacc"], keep["mem"]
        ident, cos, sin, = sb("ident", [P, P]), sb("cos", [P, SEQ]), sb("sin", [P, SEQ])
        headmask = sb("headmask", [P, MW])
        wqk = [sb(f"wqk{i}", [P, KT, 2 * D], F32R) for i in range(2)]
        wv = [sb(f"wv{i}", [P, KT, D + E], F32R) for i in range(2)]
        wg = [sb(f"wg{i}", [P, KT, E * F0], F32R) for i in range(2)]
        wu = [sb(f"wu{i}", [P, KT, E * F0], F32R) for i in range(2)]
        wd = [sb(f"wd{i}", [P, FT0, D], F32R) for i in range(2)]
        weights = (wqk, wv, wg, wu, wd)
        norm, routing = Norm(nc, sb, sem), Routing(nc, sb, sem)
        xn = sb("xn", [P, TILES, D])
        kf = xn
        xT = [sb(f"xT{i}", [P, KT, SEQ], F32R) for i in range(2)]
        xTf = [sb(f"xTf{i}", [P, KT, SEQ], F32R) for i in range(2)]
        qk = sb("qk", [P, 2 * KT, SEQ])
        rot = sb("rot", [P, 2 * KT, SEQ])
        parts = [sb(f"part{i}", [P, 2 * KT, SEQ], BF16) for i in range(3)]
        v32 = sb("v32", [P, TILES, HEADS, VW])
        comb = sb("comb", [P, TILES, E])
        cT = sb("cT", [E, SEQ])
        cbc = sb("cbc", [P, FT0 * SEQ])
        h = [sb(f"h{i}", [P, SEQ]) for i in range(2)]
        hh = [[sb(f"hh{i}{j}", [P, SEQ], F32R) for j in range(2)] for i in range(HSLOTS)]

        psT = ctx.enter_context(nc.psum_tensor("a_psT", [P, 2, SEQ], F32))
        psG = ctx.enter_context(nc.psum_tensor("a_psG", [P, 4, SEQ], F32))
        psO = ctx.enter_context(nc.psum_tensor("a_psO", [P, TILES, D], F32))

        ident_in = sem("ident_in")
        consts_in, x0_in, x_in, w_split = (sem(n) for n in ("consts_in", "x0_in", "x_in", "w_split"))
        w_done = [sem(f"w_done{n}") for n in range(len(weights))]
        raw_in = [sem(f"raw_in{i}") for i in range(2)]
        ones, xT_ps, xhi, xlo, xf_hi, xf_lo = (sem(n) for n in ("ones", "xT_ps", "xhi", "xlo", "xf_hi", "xf_lo"))
        logits_ps, combT_ps, cT_copied, qk_ps, v_ps, v_copied, kfT_ps, kf_copied, memory_ps, memory_copied = (
            sem(n) for n in ("logits_ps", "combT_ps", "cT_copied", "qk_ps", "v_ps", "v_copied", "kfT_ps", "kf_copied",
                             "memory_ps", "memory_copied"))
        sined, rotated, min_done, exp_done, features = (sem(n) for n in ("sined", "rotated", "min", "exp", "features"))
        part_done, rest_done = [sem(f"part{i}") for i in range(3)], sem("rest")
        v_stored, qf_stored, parts_stored, cT_stored = (sem(n) for n in ("v_st", "qf_st", "parts_st", "cT_st"))
        cbc_in = [sem(f"cbc_in{i}") for i in range(2)]
        gate_up_ps, silu_done, mult_done, weighted, hi_done, lo_done, down_ps = (
            sem(n) for n in ("gate_up_ps", "silu", "mult", "weighted", "hi", "lo", "down_ps"))
        added = sem("added")

        pieces = []
        for e in range(E):
            f = e * F0
            while f < (e + 1) * F0:
                n = min(P - f % P, (e + 1) * F0 - f)
                pieces.append((e, f // P, f % P, n))
                f += n
        cbc_pieces = [[p for p in pieces if (p[1] >= FRONT_TILES) == bool(i)] for i in range(2)]

        def raw(n, w):
            size = FT0 * SEQ // 2
            return cbc[:, n % 2 * size:n % 2 * size + w[0].shape[1] * w[0].shape[2]].rearrange(
                "p (k n) -> p k n", k=w[0].shape[1])

        RAW_IN = (32, 32, 48, 48, 64)

        def last_use(j, slots):
            j, batch = j % FT0, j // FT0 * FT0
            last = j - slots if j >= slots else max(m for m in range(FT0) if m % slots == j % slots) - FT0
            return max(batch + last + 1, 0)

        def loop(eng, run):
            with eng.Fori(0, BATCHES - 1) as b:
                run(b, False)
            run(BATCHES - 1, True)

        def tiles(b, last, tile, steps):
            for t in range(FT0):
                before, behind = (() if last else steps.get((t, place), ()) for place in range(2))
                for step in before:
                    step(b + 1)
                if not (last and t + FAHEAD >= FT0):
                    tile(b, t + FAHEAD)
                yield t
                for step in behind:
                    step(b + 1)

        def start(tile, steps):
            for place in sorted(steps):
                for step in steps[place]:
                    step(0)
            for t in range(FAHEAD if tile else 0):
                tile(0, t)

        def run_steps(eng, tile, steps):
            def run(b, last):
                for t in tiles(b, last, tile, steps):
                    pass
            return run

        block = ctx.enter_context(nc.Block())

        @block.sync
        def _(sp):
            def load_weights(n, names):
                lo = 0
                for name in names:
                    dst = raw(n, weights[n])
                    width = io[name].shape[1]
                    sp.dma_start(dst[:, :, lo:lo + width],
                                 io[name].rearrange("(k p) n -> p k n", p=P)).then_inc(raw_in[n % 2], 16)
                    lo += width

            def load_x(b, done):
                sp.dma_start(xacc[:, b * TILES:(b + 1) * TILES, :],
                             io["x"][b].rearrange("(t p) d -> p t d", p=P)).then_inc(done, 16)

            def cbc_load(n, i):
                if isinstance(n, int):
                    for done in w_done:
                        sp.wait_ge(done, 1)
                else:
                    sp.wait_ge(weighted, FT0 * n - FT0 + (FRONT_TILES, FT0)[i])
                sp.wait_ge(cT_stored, 16 * n + 16)
                for e, tile, row, rows in cbc_pieces[i]:
                    sp.dma_start(cbc[row:row + rows, tile * SEQ:(tile + 1) * SEQ],
                                 scratch["cT"][n, e:e + 1, :].to_broadcast((rows, SEQ))).then_inc(cbc_in[i], 16)

            def front(n):
                sp.wait_ge(cT_copied, n + 1)
                sp.dma_start(scratch["cT"][n], cT[:, :]).then_inc(cT_stored, 16)
                cbc_load(n, 0)
                sp.wait_ge(v_copied, n + 1)
                sp.dma_start(scratch["v"][n].rearrange("(t p) n -> p t n", p=P),
                             v32[:, :, :, :].rearrange("p t h w -> p t (h w)")).then_inc(v_stored, 16)
                cbc_load(n, 1)
                sp.wait_ge(features, 2 * n + 2)
                sp.dma_start(scratch["qf"][n].rearrange("k p n -> p k n"), rot[:, 0:KT, :]).then_inc(qf_stored, 16)
                for i in range(3):
                    sp.wait_ge(part_done[i], 2 * n + 2)
                    sp.dma_start(scratch["parts"][n, i].rearrange("k p n -> p k n"), parts[i][:, :, :]).then_inc(parts_stored, 16)

            load_x(0, x0_in)
            sp.dma_start(ident[:, :], io["ident"]).then_inc(ident_in, 16)
            load_weights(0, ("Wq0", "Wk0"))
            load_weights(1, ("Wv0", "router0"))
            for dst, src in ((cos, "cos"), (sin, "sin"), (headmask, "headmask")):
                sp.dma_start(dst[:, :], io[src]).then_inc(consts_in, 16)
            routing.load(sp, io)
            for n, name in ((2, "gate0"), (3, "up0"), (4, "down0")):
                sp.wait_ge(w_done[n - 2], 1)
                load_weights(n, (name,))
            for b in range(1, BATCHES):
                load_x(b, x_in)
            front(0)
            with sp.Fori(0, BATCHES - 1) as b:
                front(b + 1)
            for done, n in ((v_stored, 1), (qf_stored, 1), (parts_stored, 3), (cT_stored, 1)):
                sp.wait_ge(done, 16 * n * BATCHES)

        @block.gpsimd
        def _(pool):
            def tile(b, j):
                s = j % FT0
                pool.wait_ge(hi_done, FT0 * b + j + 1)
                nc.gpsimd.tensor_tensor(hh[s % HSLOTS][1][:, :], h[s % 2][:, :], hh[s % HSLOTS][0][:, :].bitcast(F32),
                                        ALU.subtract).then_inc(lo_done, 1)

            def power(n):
                norm.power(pool, n)

            def rest(i):
                def step(n):
                    half = slice(KT * i, KT * (i + 1))
                    pool.wait_ge(part_done[0], 2 * n + i + 1)
                    pool.wait_ge(features, 2 * n + i + 1)
                    nc.gpsimd.tensor_tensor(qk[:, half, :], qk[:, half, :], parts[0][:, half, :],
                                            ALU.subtract).then_inc(rest_done, 1)
                return step

            def third(i):
                def step(n):
                    half = slice(KT * i, KT * (i + 1))
                    pool.wait_ge(part_done[1], 2 * n + i + 1)
                    pool.wait_ge(parts_stored, 48 * n)
                    nc.gpsimd.tensor_tensor(parts[2][:, half, :], qk[:, half, :], parts[1][:, half, :],
                                            ALU.subtract).then_inc(part_done[2], 1)
                return step

            norm.setup(pool)
            nc.gpsimd.memset(v32[:, :, :, HD:HD + 1], 1.0).then_inc(ones, 1)
            nc.gpsimd.memset(v32[:, :, :, HD + 1:VW], 0.0).then_inc(ones, 1)
            steps = {(0, 0): (power,), (8, 0): (rest(0),), (9, 0): (third(0), rest(1)), (10, 0): (third(1),)}
            def split_lo(n):
                pool.wait_ge(w_split, n + 1)
                nc.gpsimd.tensor_tensor(weights[n][1][:, :, :], raw(n, weights[n]), weights[n][0][:, :, :].bitcast(F32),
                                        ALU.subtract).then_inc(w_done[n], 1)

            at_first = dict(steps)
            at_first[1, 0] = tuple(lambda b, n=n: split_lo(n) for n in (2, 3))
            at_first[6, 1] = (lambda b: split_lo(4),)
            start(tile, at_first)
            loop(pool, run_steps(pool, tile, steps))

        @block.scalar
        def _(act):
            def split_hi(n):
                act.wait_ge(raw_in[n % 2], RAW_IN[n])
                nc.scalar.activation(weights[n][0][:, :, :], raw(n, weights[n]), ACT.Copy).then_inc(w_split, 1)

            def tile(b, j):
                s = j % FT0
                act.wait_ge(gate_up_ps, FT0 * b + j + 1)
                act.wait_ge(lo_done, FT0 * b + last_use(j, 2))
                nc.scalar.activation(h[s % 2][:, :], psG[:, 2 * (s % 2), :], ACT.Silu).then_inc(silu_done, 1)
                act.wait_ge(weighted, FT0 * b + j + 1)
                act.wait_ge(down_ps, FT0 * b + last_use(j, HSLOTS))
                nc.scalar.activation(hh[s % HSLOTS][0][:, :], h[s % 2][:, :], ACT.Copy).then_inc(hi_done, 1)

            def copy_xT(n):
                act.wait_ge(xT_ps, n + 1)
                act.wait_ge(v_ps, n)
                act.wait_ge(xf_lo, n)
                act.wait_ge(xf_hi, n)
                nc.scalar.activation(xT[0][:, :, :], psT[:, :, :], ACT.Copy).then_inc(xhi, 1)

            def gap_exp(n):
                routing.exp(act, n)

            def exp_part(i):
                def step(n):
                    half = slice(KT * i, KT * (i + 1))
                    act.wait_ge(min_done, 2 * n + i + 1)
                    nc.scalar.activation(rot[:, half, :], rot[:, half, :], ACT.Exp).then_inc(exp_done, 1)
                return step

            def first(i):
                def step(n):
                    half = slice(KT * i, KT * (i + 1))
                    act.wait_ge(rotated, 2 * n + i + 1)
                    act.wait_ge(parts_stored, 48 * n)
                    nc.scalar.activation(parts[0][:, half, :], qk[:, half, :], ACT.Copy).then_inc(part_done[0], 1)
                return step

            def second(i):
                def step(n):
                    half = slice(KT * i, KT * (i + 1))
                    act.wait_ge(rest_done, 2 * n + i + 1)
                    nc.scalar.activation(parts[1][:, half, :], qk[:, half, :], ACT.Copy).then_inc(part_done[1], 1)
                return step

            def copy_v(n):
                act.wait_ge(v_ps, n + 1)
                act.wait_ge(v_stored, 16 * n)
                act.wait_ge(memory_ps, n)
                nc.scalar.activation(v32[:, :, :, 0:HD], psT[:, :, :].rearrange("p a (t h d) -> p (a t) h d", t=2, d=HD),
                                     ACT.Copy).then_inc(v_copied, 1)

            def copy_kf(n):
                act.wait_ge(kfT_ps, n + 1)
                nc.scalar.activation(kf[:, :, :], psT[:, :, :].rearrange("p a (t n) -> p (a t) n", n=D),
                                     ACT.Copy).then_inc(kf_copied, 1)

            def copy_xTf(n):
                act.wait_ge(gate_up_ps, FT0 * n)
                act.wait_ge(xhi, n + 1)
                nc.scalar.activation(xTf[0][:, :, :], xT[0][:, :, :].bitcast(F32), ACT.Copy).then_inc(xf_hi, 1)

            split_hi(0)
            split_hi(1)
            steps = {(2, 0): (copy_xT,), (3, 1): (gap_exp,), (6, 1): (exp_part(0), first(0)), (7, 1): (exp_part(1),),
                     (8, 0): (copy_v, copy_xTf), (8, 1): (first(1), second(0)), (9, 0): (copy_kf,), (9, 1): (second(1),)}
            at_first = dict(steps)
            at_first[2, 1] = (copy_xTf, lambda n: split_hi(2))
            at_first[8, 0] = (copy_v,)
            at_first[4, 1] = (lambda n: split_hi(3),)
            at_first[6, 0] = (lambda n: split_hi(4),)
            start(tile, at_first)
            loop(act, run_steps(act, tile, steps))

        @block.vector
        def _(dve):
            def split_lo(n):
                dve.wait_ge(w_split, n + 1)
                nc.vector.tensor_tensor(weights[n][1][:, :, :], raw(n, weights[n]), weights[n][0][:, :, :].bitcast(F32),
                                        ALU.subtract).then_inc(w_done[n], 1)

            def tile(b, j):
                s = j % FT0
                dve.wait_ge(silu_done, FT0 * b + j + 1)
                nc.vector.tensor_tensor(h[s % 2][:, :], h[s % 2][:, :], psG[:, 2 * (s % 2) + 1, :], ALU.mult).then_inc(mult_done, 1)
                if s in (0, FRONT_TILES):
                    i = int(s > 0)
                    dve.wait_ge(cbc_in[i], 16 * len(cbc_pieces[i]) * (b + j // FT0 + 1))
                dve.wait_ge(mult_done, FT0 * b + j + 1)
                nc.vector.tensor_tensor(h[s % 2][:, :], h[s % 2][:, :], cbc[:, s * SEQ:(s + 1) * SEQ], ALU.mult).then_inc(weighted, 1)

            def moments(n):
                norm.moments(dve, n, xacc)

            def normalise(n):
                dve.wait_ge(memory_ps, n)
                norm.apply(dve, n, xacc, xn)

            def split_xT(n):
                dve.wait_ge(xhi, n + 1)
                nc.vector.tensor_tensor(xT[1][:, :, :], psT[:, :, :], xT[0][:, :, :].bitcast(F32), ALU.subtract).then_inc(xlo, 1)

            def route(n):
                dve.wait_ge(logits_ps, n + 1)
                routing.choose(dve, n, psT[:, 0, 0:TILES * E].rearrange("p (t e) -> p t e", e=E))

            def route_weights(n):
                routing.weigh(dve, n, comb[:, :, :])

            def copy_cT(n):
                dve.wait_ge(combT_ps, n + 1)
                dve.wait_ge(cT_stored, 16 * n)
                nc.vector.tensor_copy(cT[:, :], psT[0:E, 1, :]).then_inc(cT_copied, 1)

            def rotate(i):
                def step(n):
                    dve.wait_ge(qk_ps, 2 * n + i + 1)
                    dve.wait_ge(qf_stored, 16 * n)
                    dve.wait_ge(kfT_ps, n)
                    dve.wait_ge(part_done[2], 2 * n)
                    for h in range(KT):
                        nc.vector.tensor_tensor(qk[:, 2 * i + h, :], psT[:, h, :], cos[:, :], ALU.mult)
                        nc.vector.tensor_tensor(rot[:, 2 * i + h, :], psT[:, 1 - h, :], sin[:, :],
                                                ALU.mult).then_inc(sined, 1)
                    dve.wait_ge(sined, 4 * n + 2 * i + 2)
                    nc.vector.tensor_tensor(qk[:, 2 * i, :], qk[:, 2 * i, :], rot[:, 2 * i, :], ALU.subtract)
                    nc.vector.tensor_tensor(qk[:, 2 * i + 1, :], qk[:, 2 * i + 1, :], rot[:, 2 * i + 1, :],
                                            ALU.add).then_inc(rotated, 1)
                    dve.wait_ge(rotated, 2 * n + i + 1)
                    half = slice(KT * i, KT * (i + 1))
                    nc.vector.tensor_scalar(rot[:, half, :], qk[:, half, :], 0.0, None, ALU.min).then_inc(min_done, 1)
                return step

            def feature(i):
                def step(n):
                    half = slice(KT * i, KT * (i + 1))
                    dve.wait_ge(exp_done, 2 * n + i + 1)
                    nc.vector.scalar_tensor_tensor(rot[:, half, :], qk[:, half, :], 0.0, rot[:, half, :],
                                                   ALU.max, ALU.add).then_inc(features, 1)
                return step

            def copy_xTf(n):
                dve.wait_ge(gate_up_ps, FT0 * n)
                dve.wait_ge(xlo, n + 1)
                nc.vector.tensor_copy(xTf[1][:, :, :], xT[1][:, :, :].bitcast(F32)).then_inc(xf_lo, 1)

            def memory(n):
                dve.wait_ge(memory_ps, n + 1)
                for k in range(KT):
                    at = mem[:, bass.ds(n * KT + k, 1), :].rearrange("p a n -> p (a n)")
                    nc.vector.tensor_tensor(at, psT[:, 0, MW * k:MW * (k + 1)], headmask[:, :], ALU.mult).then_inc(memory_copied, 1)

            def add(b):
                dve.wait_ge(down_ps, FT0 * b + FT0)
                x = xacc[:, bass.ds(b * TILES, TILES), :]
                nc.vector.tensor_tensor(x, psO[:, :, :], x, ALU.add).then_inc(added, 1)

            steps = {(0, 0): (moments,), (1, 0): (normalise,), (2, 0): (split_xT,), (3, 0): (route,), (4, 0): (route_weights,),
                     (5, 0): (copy_cT,), (6, 0): (rotate(0),), (7, 0): (rotate(1),), (7, 1): (feature(0),), (8, 0): (feature(1), copy_xTf),
                     (10, 0): (memory,)}
            dve.wait_ge(x0_in, 16)
            at_first = dict(steps)
            at_first[0, 1] = (lambda n: split_lo(0), lambda n: split_lo(1))
            at_first[2, 1] = (copy_xTf,)
            at_first[8, 0] = (feature(1),)
            at_first[5, 1] = (lambda n: dve.wait_ge(consts_in, 48), lambda n: dve.wait_ge(ones, 2))
            start(tile, at_first)
            dve.wait_ge(x_in, 16 * (BATCHES - 1))

            def run(b, last):
                run_steps(dve, tile, steps)(b, last)
                add(b)

            loop(dve, run)

        @block.tensor
        def _(pe):
            def tile(b, j):
                s = j % FT0
                if s == 0:
                    pe.wait_ge(xf_hi, b + j // FT0 + 1)
                    pe.wait_ge(xf_lo, b + j // FT0 + 1)
                pe.wait_ge(mult_done, FT0 * b + last_use(j, 2))
                c = slice(s * P, (s + 1) * P)
                for i, w in enumerate((wg, wu)):
                    mm = three(nc, psG[:, 2 * (s % 2) + i, :],
                               [(w[0][:, k, c], w[1][:, k, c], xTf[0][:, k, :], xTf[1][:, k, :]) for k in range(KT)])
                mm.then_inc(gate_up_ps, 1)

            def down(b, j):
                if j == 0:
                    pe.wait_ge(added, b)
                pe.wait_ge(lo_done, FT0 * b + j + 1)
                hi, lo = hh[j % HSLOTS]
                for t in range(TILES):
                    c = slice(t * P, (t + 1) * P)
                    mm = three(nc, psO[:, t, :], [(hi[:, c], lo[:, c], wd[0][:, j, :], wd[1][:, j, :])],
                               start=j == 0 and t % 2 == 0, last=j == FT0 - 1)
                mm.then_inc(down_ps, 1)

            def turn_x(n):
                pe.wait_ge(memory_copied, KT * n)
                pe.wait_ge(norm.xn_done, TILES * n + TILES)
                for t in range(TILES):
                    for k in range(KT):
                        mm = nc.tensor.transpose(psT[:, k, t * P:(t + 1) * P], xn[:, t, k * P:(k + 1) * P], ident[:, :])
                mm.then_inc(xT_ps, 1)

            def logits(n):
                pe.wait_ge(xlo, n + 1)
                for t in range(TILES):
                    c = slice(t * P, (t + 1) * P)
                    mm = three(nc, psT[:, 0, t * E:(t + 1) * E],
                               [(xT[0][:, k, c], xT[1][:, k, c], wv[0][:, k, D:D + E], wv[1][:, k, D:D + E])
                                for k in range(KT)])
                mm.then_inc(logits_ps, 1)

            def turn_comb(n):
                pe.wait_ge(routing.comb_done, n + 1)
                for t in range(TILES):
                    mm = nc.tensor.transpose(psT[0:E, 1, t * P:(t + 1) * P], comb[:, t, :], ident[:, :])
                mm.then_inc(combT_ps, 1)

            def project_qk(i):
                def step(n):
                    if i == 0:
                        pe.wait_ge(routing.copied, n + 1)
                        pe.wait_ge(cT_copied, n + 1)
                    else:
                        pe.wait_ge(sined, 4 * n + 2)
                    for m in range(KT):
                        c = slice((KT * i + m) * P, (KT * i + m + 1) * P)
                        mm = three(nc, psT[:, m, :], [(wqk[0][:, k, c], wqk[1][:, k, c], xT[0][:, k, :], xT[1][:, k, :])
                                                      for k in range(KT)])
                    mm.then_inc(qk_ps, 1)
                return step

            def project_v(n):
                pe.wait_ge(sined, 4 * n + 4)
                for t in range(TILES):
                    c = slice(t * P, (t + 1) * P)
                    mm = three(nc, psT[:, t // 2, t % 2 * D:(t % 2 + 1) * D],
                               [(xT[0][:, k, c], xT[1][:, k, c], wv[0][:, k, 0:D], wv[1][:, k, 0:D]) for k in range(KT)])
                mm.then_inc(v_ps, 1)

            def turn_kf(n):
                pe.wait_ge(v_copied, n + 1)
                pe.wait_ge(features, 2 * n + 2)
                for t in range(TILES):
                    for k in range(KT):
                        at = t % 2 * D + k * P
                        mm = nc.tensor.transpose(psT[:, t // 2, at:at + P], rot[:, KT + k, t * P:(t + 1) * P], ident[:, :])
                mm.then_inc(kfT_ps, 1)

            def memorise(n):
                pe.wait_ge(kf_copied, n + 1)
                for k in range(KT):
                    for t in range(TILES):
                        mm = nc.tensor.matmul(psT[:, 0, MW * k:MW * (k + 1)], kf[:, t, k * P:(k + 1) * P],
                                              v32[:, t, HH * k:HH * (k + 1), 0:HD + 1], start=t == 0, stop=t == TILES - 1,
                                              skip_group_check=True)
                mm.then_inc(memory_ps, 1)

            steps = {(1, 1): (turn_x,), (2, 1): (logits,), (4, 1): (turn_comb,), (5, 1): (project_qk(0),),
                     (6, 1): (project_qk(1),), (7, 1): (project_v,), (8, 1): (turn_kf,), (9, 1): (memorise,)}
            at_first = dict(steps)
            at_first[0, 0] = (lambda n: pe.wait_ge(ident_in, 16),)
            at_first[2, 0] = (lambda n: pe.wait_ge(w_done[0], 1), lambda n: pe.wait_ge(w_done[1], 1))
            at_first[8, 0] = (lambda n: pe.wait_ge(ones, 2),)
            at_first[6, 2] = (lambda n: pe.wait_ge(w_done[2], 1), lambda n: pe.wait_ge(w_done[3], 1), lambda n: tile(0, 0))
            at_first[7, 2] = (lambda n: tile(0, 1),)
            start(None, at_first)

            pe.wait_ge(w_done[4], 1)

            def run(b, last):
                for t in tiles(b, last, tile, steps):
                    down(b, t)

            loop(pe, run)


RW = E + HD
PSLOTS = 2


def middle(nc, io, scratch, keep):
    with ExitStack() as ctx:
        def sb(name, shape, dt=F32):
            return ctx.enter_context(nc.sbuf_tensor("b_" + name, shape, dt))

        def sem(name):
            return stage_semaphore(nc, keep, "b_" + name)

        def sems(name, n):
            return [sem(f"{name}{i}") for i in range(n)]

        xacc, mem, xT1, comb1 = keep["xacc"], keep["mem"], keep["xT1"], keep["comb1"]
        decay, cdec = keep["decay"], keep["cdec"]
        ident, identb = sb("ident", [P, P]), sb("identb", [P, P], BF16)
        expert = keep["raw"]
        qst = [buffer[0:STACKM, :].bitcast(BF16).rearrange("p (h t) -> p h t", h=HG) for buffer in expert]
        qst.append(sb("qst3", [STACKM, HG, SEQ], BF16))
        kst = [sb(f"kst{g}", [STACKM, HG, SEQ], BF16) for g in range(GROUPS)]
        vst = [sb(f"vst{g}", [P, TILES, HG * VW]) for g in range(GROUPS)]
        probs = [sb(f"probs{k}", [P, HG, SEQ]) for k in range(PSLOTS)]
        negmax = [sb(f"negmax{i}", [P, TILES, HG]) for i in range(2)]
        nmparts = [sb(f"nmparts{i}", [P, TILES, 2, HG], BF16) for i in range(2)]
        nmT = [sb(f"nmT{i}", [2 * HG, SEQ], BF16) for i in range(2)]
        outT = sb("outT", [P, GROUPS, SEQ])
        norm, routing = Norm(nc, sb, sem), Routing(nc, sb, sem)
        sel = sb("sel", [P, HG * (HD + 1)])
        gates = sb("gates", [P, 2, HEADS])
        after, before = sb("after", [P, P]), sb("before", [P, 1])
        rel, causal = sb("rel", [P, P]), sb("causal", [P, P])
        ldrows, ldall = sb("ldrows", [P, KT]), sb("ldall", [P, HEADS])
        qdec, kdec = sb("qdec", [P, KT, P]), sb("kdec", [P, HEADS])
        wo, wg2 = sb("wo", [P, KT, D]), sb("wg2", [HD, D])
        rqk, rkv = outT[:, 0:KT, :], outT[:, KT:2 * KT, :]
        rr = sb("rr", [P, KT, RW])
        wqk = [sb(f"wqk{i}", [P, KT, 2 * D], F32R) for i in range(2)]
        wkv = [sb(f"wkv{i}", [P, KT, 2 * D], F32R) for i in range(2)]
        wr = [sb(f"wr{i}", [P, KT, RW], F32R) for i in range(2)]
        qf = sb("qf", [P, KT, SEQ])
        scale, both = sb("scale", [P, 2, HEADS]), sb("both", [P, 2, D])
        combined = sb("combined", [P, TILES, D])
        xn = combined
        combT = sb("combT", [P, KT, SEQ])
        kk = combT[:, :, :].rearrange("p k (t n) -> p (k t) n", n=D)
        xT = [sb(f"xT{i}", [P, KT, SEQ], F32R) for i in range(2)]
        half = sb("half", [P, KT, SEQ])
        parts = [sb(f"part{i}", [P, KT, SEQ], BF16) for i in range(3)]
        v32 = sb("v32", [P, TILES, HEADS, VW])
        low, lowT, sg = sb("low", [P, TILES, HD]), sb("lowT", [HD, SEQ]), sb("sg", [P, TILES, D])
        qd, kd = sb("qd", [P, KT, SEQ]), sb("kd", [P, TILES, D])

        psE = [ctx.enter_context(nc.psum_tensor(f"b_psE{i}", [P, SEQ], F32)) for i in range(2)]
        psM = ctx.enter_context(nc.psum_tensor("b_psM", [P, 2, SEQ], F32))
        psV = ctx.enter_context(nc.psum_tensor("b_psV", [P, SEQ], F32))
        psN = ctx.enter_context(nc.psum_tensor("b_psN", [P, SEQ], BF16))
        psX = ctx.enter_context(nc.psum_tensor("b_psX", [P, 2, SEQ], F32))

        ident_in, ones, identb_done = sem("ident_in"), sem("ones"), sem("identb")
        stack_in, max_in, max_out = sems("stack_in", GROUPS), sems("max_in", GROUPS), sem("max_out")
        scores_ready, scores_used = sem("scores_ready"), sems("scores_used", 2)
        probs_used = sem("probs_used")
        rows_ready, rows_used = sem("rows_ready"), sems("rows_used", 2)
        negmax_hi, negmax_parts = sem("negmax_hi"), sem("negmax_parts")
        nmT_ready, nmT_copied, out_copied = sem("nmT_ready"), sem("nmT_copied"), sem("out_copied")
        consts_in, weights_in, w_hi, w_lo, tables, masked, g_done, omg_done, padded = (
            sem(n) for n in ("consts_in", "weights_in", "w_hi", "w_lo", "tables", "masked", "g_done", "omg_done", "padded"))
        qf_in, heads_ps, recips, scaled, terms, combined_done = (
            sem(n) for n in ("qf_in", "heads_ps", "recips", "scaled", "terms", "combined"))
        combT_ps, combT_done, y_ps, residual_done, xT_ps, xhi, xlo, kept = (
            sem(n) for n in ("combT_ps", "combT_done", "y_ps", "residual", "xT_ps", "xhi", "xlo", "kept"))
        half_ps, half_done, rest_done, qd_done, kd_done = (
            sem(n) for n in ("half_ps", "half", "rest", "qd", "kd"))
        part_done = sems("part", 3)
        part_stored, stored = keep["part_stored"], keep["stored"]
        low_ps, low_done, lowT_ps, lowT_done, gate_ps, gate_done, kk_ps, kk_done, v_ps, v_done = (
            sem(n) for n in ("low_ps", "low", "lowT_ps", "lowT", "gate_ps", "gate", "kk_ps", "kk", "v_ps", "v"))
        LOADED = 16 * (2 * len(Q_PARTS) + 1)
        CONSTS, WEIGHTS = 8 * 16, 8 * 16
        TABLES = HEADS + KT + 2
        STORES, PARTS = 16 * STORES1, 16 * PARTS1
        SLOTS = GROUPS * TILES

        def loop(eng, attend, steps, ready=lambda: None):
            def batch(b, beside, last):
                for g in range(GROUPS):
                    attend(b, g, last, lambda k: [step(beside) for step in steps.get(TILES * g + k, ()) if beside is not None])

            batch(0, None, False)
            ready()
            with eng.Fori(0, BATCHES - 2) as b:
                batch(b + 1, b, False)
            batch(BATCHES - 1, BATCHES - 2, True)
            for slot in sorted(steps):
                for step in steps[slot]:
                    step(BATCHES - 1)

        def alone(n):
            return isinstance(n, int) and n == BATCHES - 1

        def second(n):
            return psM if alone(n) else psX

        block = ctx.enter_context(nc.Block())

        @block.sync
        def _(sp):
            def load(b, g):
                for op, dst, order in ((0, qst, Q_PARTS), (1, kst, K_PARTS)):
                    for i, part in enumerate(order):
                        row = (g % 2) * HG * HD
                        src = scratch["parts"][b, part, KT * op + g // 2, row:row + HG * HD, :]
                        sp.dma_start(dst[g][i * HD:(i + 1) * HD, :, :],
                                     src.rearrange("(h d) t -> d h t", d=HD)).then_inc(stack_in[g], 16)
                sp.dma_start(vst[g][:, :, :], scratch["v"][b, :, g * HG * VW:(g + 1) * HG * VW]
                             .rearrange("(t p) n -> p t n", p=P)).then_inc(stack_in[g], 16)

            def send_max(n, g, i, before=None):
                sp.wait_ge(nmT_copied, n)
                if before is not None:
                    sp.wait_ge(max_in[(g - 1) % GROUPS], before)
                sp.dma_start(scratch["max"], nmT[i][:, :]).then_inc(max_out, 16)
                sp.wait_ge(max_out, 16 * n)
                sp.dma_start(qst[g][STACK:STACKM, :, :],
                             scratch["max"].rearrange("(a h) t -> a h t", a=2)).then_inc(max_in[g], 16)

            load(0, 0)
            sp.dma_start(ident[:, :], io["ident"]).then_inc(ident_in, 16)
            load(0, 1)
            for dst, src in ((sel[:, :], io["sel17"]), (after[:, :], io["after"]), (rel[:, :], io["rel"]), (causal[:, :], io["causal"]),
                             (before[:, :], io["before"]), (ldrows[:, :], io["log_decay_rows"]),
                             (ldall[:, :], io["log_decay"].to_broadcast((P, HEADS))),
                             (gates[:, 1, :], io["gate_attn"].to_broadcast((P, HEADS)))):
                sp.dma_start(dst, src).then_inc(consts_in, 16)
            routing.load(sp, io)
            for dst, src in ((rqk[:, :, 0:D], "Wq1"), (rqk[:, :, D:2 * D], "Wk1"), (rkv[:, :, 0:D], "Wk1"),
                             (rkv[:, :, D:2 * D], "Wv1"), (rr[:, :, 0:E], "router1"), (rr[:, :, E:RW], "Wg1"),
                             (wo[:, :, :], "Wo0")):
                sp.dma_start(dst, io[src].rearrange("(k p) n -> p k n", p=P)).then_inc(weights_in, 16)
            sp.dma_start(wg2[:, :], io["Wg2"]).then_inc(weights_in, 16)
            load(0, 2)
            send_max(1, 0, 0)
            load(0, 3)

            def attend(b, g, last, beside):
                if not (last and g == GROUPS - 1):
                    send_max(GROUPS * b + g + 2, (g + 1) % GROUPS, (g + 1) % 2, 16 * b + 16)
                if g == 1:
                    sp.wait_ge(heads_ps, TILES * b)
                    sp.dma_start(qf[:, :, :], scratch["qf"][b].rearrange("k p n -> p k n")).then_inc(qf_in, 16)
                for k in range(TILES - 1):
                    beside(k)
                if not last:
                    sp.wait_ge(probs_used, TILES * (GROUPS * b + g + 1))
                    load(b + 1, g)
                elif g < len(expert):
                    sp.wait_ge(probs_used, TILES * (GROUPS * b + g + 1))
                    name, k = EXPERT_WEIGHTS[g]
                    sp.dma_start(expert[g][:, :].rearrange("p (k n) -> p k n", k=k),
                                 io[name][0].rearrange("(k p) n -> p k n", p=P)).then_inc(keep["raw_in"][g], 16)

                beside(TILES - 1)

            def store_q(n):
                sp.wait_ge(qd_done, n + 1)
                sp.dma_start(scratch["qd"][n].rearrange("k p n -> p k n"), qd[:, :, :]).then_inc(stored, 16)
                for j in range(3):
                    sp.wait_ge(part_done[j], 2 * n + 1)
                    sp.dma_start(scratch["parts1"][n, j, 0:KT].rearrange("k p n -> p k n"),
                                 parts[j][:, :, :]).then_inc(part_stored, 16)

            def store_gate(n):
                sp.wait_ge(gate_done, n + 1)
                sp.dma_start(scratch["sg"][n].rearrange("(t p) n -> p t n", p=P), sg[:, :, :]).then_inc(stored, 16)

            def store(n):
                sp.wait_ge(kd_done, n + 1)
                sp.dma_start(scratch["kd"][n].rearrange("(t p) n -> p t n", p=P), kd[:, :, :]).then_inc(stored, 16)
                for j in range(3):
                    sp.wait_ge(part_done[j], 2 * n + 2)
                    sp.dma_start(scratch["parts1"][n, j, KT:2 * KT].rearrange("k p n -> p k n"),
                                 parts[j][:, :, :]).then_inc(part_stored, 16)
                sp.wait_ge(v_done, n + 1)
                sp.dma_start(scratch["v1"][n].rearrange("(t p) n -> p t n", p=P),
                             v32[:, :, :, :].rearrange("p t h w -> p t (h w)")).then_inc(stored, 16)

            loop(sp, attend, {SLOTS - 4: (store_q,), SLOTS - 3: (store_gate,), SLOTS - 1: (store,)})

        @block.gpsimd
        def _(pool):
            def attend(b, g, last, beside):
                for k in range(TILES):
                    beside(k)

            def combine(t):
                def step(n):
                    pool.wait_ge(terms, TILES * n + t + 1)
                    nc.gpsimd.tensor_tensor(combined[:, t, :], both[:, 0, :], both[:, 1, :], ALU.add).then_inc(combined_done, 1)
                return step

            def decay_q(n):
                pool.wait_ge(half_done, 2 * n + 1)
                pool.wait_ge(stored, STORES * n)
                nc.gpsimd.tensor_tensor(qd[:, :, :].rearrange("p k (c n) -> p k c n", n=CH),
                                        half[:, :, :].rearrange("p k (c n) -> p k c n", n=CH),
                                        qdec[:, :, :].unsqueeze(2).to_broadcast((P, KT, SEQ // CH, CH)), ALU.mult).then_inc(qd_done, 1)

            def power(n):
                norm.power(pool, n)

            def keep_xT(i):
                def step(n):
                    pool.wait_ge((xhi, xlo)[i], n + 1)
                    nc.gpsimd.tensor_copy(xT1[i][:, :, bass.ds(n * SEQ, SEQ)], xT[i][:, :, :].bitcast(F32)).then_inc(kept, 1)
                return step

            def rest(i):
                def step(n):
                    pool.wait_ge(part_done[0], 2 * n + i + 1)
                    if i == 0:
                        pool.wait_ge(qd_done, n + 1)
                    nc.gpsimd.tensor_tensor(half[:, :, :], half[:, :, :], parts[0][:, :, :], ALU.subtract).then_inc(rest_done, 1)
                return step

            def third(n):
                pool.wait_ge(part_done[1], 2 * n + 1)
                nc.gpsimd.tensor_tensor(parts[2][:, :, :], half[:, :, :], parts[1][:, :, :], ALU.subtract).then_inc(part_done[2], 1)

            for g in range(GROUPS):
                nc.gpsimd.memset(kst[g][STACK:STACKM, :, :], 1.0).then_inc(ones, 1)
            pool.wait_ge(ones, GROUPS)
            norm.setup(pool)
            nc.gpsimd.memset(v32[:, :, :, HD:VW], 0.0).then_inc(padded, 1)
            for i, (dst, src) in enumerate(((wqk, rqk), (wkv, rkv), (wr, rr))):
                pool.wait_ge(w_hi, i + 1)
                nc.gpsimd.tensor_tensor(dst[1][:, :, :], src[:, :, :], dst[0][:, :, :].bitcast(F32), ALU.subtract).then_inc(w_lo, 1)
            pool.wait_ge(consts_in, CONSTS)
            pool.wait_ge(tables, TABLES)
            nc.gpsimd.tensor_tensor(decay[:, :, :], decay[:, :, :], causal[:, :].unsqueeze(1).to_broadcast((P, HEADS, CH)),
                                    ALU.mult).then_inc(masked, 1)
            loop(pool, attend, {0: (combine(0),), 1: (combine(1),), 2: (combine(2),), 3: (combine(3),), 6: (power,), 9: (keep_xT(0),), 10: (decay_q,), 11: (rest(0),), 12: (third,), 13: (rest(1),), 14: (keep_xT(1),)})

        @block.scalar
        def _(act):
            def attend(b, g, last, beside):
                for k in range(TILES):
                    G = GROUPS * b + g
                    if k >= PSLOTS:
                        act.wait_ge(probs_used, TILES * G + k - PSLOTS + 1)
                    else:
                        act.wait_ge(probs_used, TILES * G)
                    for h in range(HG):
                        act.wait_ge(scores_ready, HG * (TILES * G + k) + h + 1)
                        nc.scalar.activation(probs[k % PSLOTS][:, h, :], psE[h % 2][:, :], ACT.Exp,
                                             scale=float(HD) ** -0.5).then_inc(scores_used[h % 2], 1)
                    beside(k)

            def copy_combT(n):
                act.wait_ge(combT_ps, n + 1)
                act.wait_ge(kd_done, n)
                nc.scalar.activation(combT[:, :, :], psX[:, :, :], ACT.Copy).then_inc(combT_done, 1)

            def copy_xT(n):
                act.wait_ge(xT_ps, n + 1)
                act.wait_ge(kept, 2 * n)
                nc.scalar.activation(xT[0][:, :, :], psX[:, :, :], ACT.Copy).then_inc(xhi, 1)

            def silu_half(i):
                def step(n):
                    act.wait_ge(half_ps, 2 * n + i + 1)
                    act.wait_ge(part_done[2], 2 * n + i)
                    nc.scalar.activation(half[:, :, :], psX[:, :, :], ACT.Silu).then_inc(half_done, 1)
                return step

            def first_part(n):
                act.wait_ge(half_done, 2 * n + 1)
                act.wait_ge(part_stored, PARTS * 2 * n)
                nc.scalar.activation(parts[0][:, :, :], half[:, :, :], ACT.Copy).then_inc(part_done[0], 1)

            def second_part(n):
                act.wait_ge(rest_done, 2 * n + 1)
                nc.scalar.activation(parts[1][:, :, :], half[:, :, :], ACT.Copy).then_inc(part_done[1], 1)

            def gap_exp(n):
                routing.exp(act, n)

            def gate(n):
                act.wait_ge(gate_ps, n + 1)
                act.wait_ge(stored, STORES * n)
                nc.scalar.activation(sg[:, :, :], second(n)[:, :, :].rearrange("p a (t n) -> p (a t) n", n=D),
                                     ACT.Sigmoid).then_inc(gate_done, 1)

            def silu_kk(n):
                act.wait_ge(kk_ps, n + 1)
                nc.scalar.activation(kk, psX[:, :, :].rearrange("p a (t n) -> p (a t) n", n=D), ACT.Silu).then_inc(kk_done, 1)

            def silu_v(n):
                act.wait_ge(v_ps, n + 1)
                nc.scalar.activation(v32[:, :, :, 0:HD], second(n)[:, :, :].rearrange("p a (t h d) -> p (a t) h d", t=2, d=HD),
                                     ACT.Silu).then_inc(v_done, 1)

            act.wait_ge(consts_in, CONSTS)
            nc.scalar.activation(gates[:, 1, :], gates[:, 1, :], ACT.Sigmoid).then_inc(g_done, 1)
            for k in range(KT):
                nc.scalar.activation(qdec[:, k, :], after[:, :], ACT.Exp, scale=ldrows[:, k:k + 1]).then_inc(tables, 1)
            nc.scalar.activation(kdec[:, :], ldall[:, :], ACT.Exp, scale=before[:, 0:1]).then_inc(tables, 1)
            nc.scalar.activation(cdec[:, :], ldrows[:, :], ACT.Exp, scale=float(CH)).then_inc(tables, 1)
            for n in range(HEADS):
                nc.scalar.activation(decay[:, n, :], rel[:, :], ACT.Exp, scale=ldall[:, n:n + 1]).then_inc(tables, 1)
            act.wait_ge(weights_in, WEIGHTS)
            act.wait_ge(padded, 1)
            for dst, src in ((wqk, rqk), (wkv, rkv), (wr, rr)):
                nc.scalar.activation(dst[0][:, :, :], src[:, :, :], ACT.Copy).then_inc(w_hi, 1)
            loop(act, attend, {4: (copy_combT,), 8: (copy_xT,), 9: (silu_half(0),), 10: (first_part,), 11: (second_part, gap_exp),
                               12: (silu_half(1),), 13: (gate,), 14: (silu_kk,),
                               15: (silu_v,)})

        @block.vector
        def _(dve):
            def reduce(n, i, t):
                for h in range(HG):
                    dve.wait_ge(rows_ready, 16 * n + HG * t + h + 1)
                    nc.vector.tensor_reduce(negmax[i][:, t, h:h + 1], psM[:, h % 2, :], AX_X, ALU.max,
                                            negate=True).then_inc(rows_used[h % 2], 1)

            def split_max(n, i, reused=True):
                if reused:
                    dve.wait_ge(nmT_ready, n - 1)
                for used in rows_used:
                    dve.wait_ge(used, 8 * n + 8)
                nc.vector.tensor_copy(nmparts[i][:, :, 0, :], negmax[i][:, :, :]).then_inc(negmax_hi, 1)
                dve.wait_ge(negmax_hi, n + 1)
                nc.vector.tensor_tensor(nmparts[i][:, :, 1, :], negmax[i][:, :, :], nmparts[i][:, :, 0, :],
                                        ALU.subtract).then_inc(negmax_parts, 1)

            def attend(b, g, last, beside):
                G = GROUPS * b + g
                ahead = not (last and g >= GROUPS - 2)
                for t in range(TILES):
                    if ahead:
                        reduce(G + 2, g % 2, t)
                    if t == 0 and not (last and g == GROUPS - 1):
                        dve.wait_ge(max_out, 16 * G)
                        dve.wait_ge(nmT_ready, G + 2)
                        nc.vector.tensor_copy(nmT[(g + 1) % 2][:, :], psN[0:2 * HG, :]).then_inc(nmT_copied, 1)
                    beside(t)
                    if t == TILES - 1 and ahead:
                        split_max(G + 2, g % 2)
                dve.wait_ge(probs_used, TILES * (G + 1))
                if g == 0:
                    dve.wait_ge(heads_ps, TILES * b)
                nc.vector.tensor_copy(outT[:, g, :], psV[:, :]).then_inc(out_copied, 1)

            def weigh_terms(t):
                def step(n):
                    T = TILES * n + t + 1
                    dve.wait_ge(heads_ps, T)
                    dve.wait_ge(terms, T - 1)
                    sums = (second(n) if t % 2 else psX)[:, :, 0:HEADS * (HD + 1)].rearrange("p a (h w) -> p a h w", w=HD + 1)
                    nc.vector.reciprocal(scale[:, :, :], sums[:, :, :, HD]).then_inc(recips, 1)
                    dve.wait_ge(recips, T)
                    nc.vector.tensor_tensor(scale[:, :, :], scale[:, :, :], gates[:, :, :], ALU.mult).then_inc(scaled, 1)
                    dve.wait_ge(scaled, T)
                    dve.wait_ge(combined_done, T - 1)
                    nc.vector.tensor_tensor(both[:, :, :].rearrange("p a (h e) -> p a h e", e=HD), sums[:, :, :, 0:HD],
                                            scale[:, :, :].unsqueeze(3).to_broadcast((P, 2, HEADS, HD)), ALU.mult).then_inc(terms, 1)
                return step

            def residual(n):
                dve.wait_ge(y_ps, n + 1)
                x = xacc[:, bass.ds(n * TILES, TILES), :]
                nc.vector.tensor_tensor(x, psX[:, :, :].rearrange("p a (t n) -> p (a t) n", n=D), x, ALU.add).then_inc(residual_done, 1)

            def moments(n):
                dve.wait_ge(omg_done, 1)
                dve.wait_ge(residual_done, n + 1)
                norm.moments(dve, n, xacc)

            def normalise(n):
                norm.apply(dve, n, xacc, xn)

            def split_xT(n):
                dve.wait_ge(xhi, n + 1)
                dve.wait_ge(kept, 2 * n)
                nc.vector.tensor_tensor(xT[1][:, :, :], psX[:, :, :], xT[0][:, :, :].bitcast(F32), ALU.subtract).then_inc(xlo, 1)

            def decay_k(n):
                dve.wait_ge(kk_done, n + 1)
                nc.vector.tensor_tensor(kd[:, :, :].rearrange("p t (h e) -> p t h e", e=HD),
                                        kk.rearrange("p t (h e) -> p t h e", e=HD),
                                        kdec[:, :].unsqueeze(1).unsqueeze(3).to_broadcast((P, TILES, HEADS, HD)), ALU.mult).then_inc(kd_done, 1)

            def first_part(n):
                dve.wait_ge(half_done, 2 * n + 2)
                dve.wait_ge(part_stored, PARTS * (2 * n + 1))
                nc.vector.tensor_copy(parts[0][:, :, :], half[:, :, :]).then_inc(part_done[0], 1)

            def second_part(n):
                dve.wait_ge(rest_done, 2 * n + 2)
                nc.vector.tensor_copy(parts[1][:, :, :], half[:, :, :]).then_inc(part_done[1], 1)

            def third_part(n):
                dve.wait_ge(part_done[1], 2 * n + 2)
                nc.vector.tensor_tensor(parts[2][:, :, :], half[:, :, :], parts[1][:, :, :], ALU.subtract).then_inc(part_done[2], 1)

            def copy_low(n):
                small = second(n)[:, 0, 0:TILES * RW].rearrange("p (t n) -> p t n", n=RW)
                dve.wait_ge(low_ps, n + 1)
                nc.vector.tensor_copy(low[:, :, :], small[:, :, E:RW]).then_inc(low_done, 1)
                routing.choose(dve, n, small[:, :, 0:E])

            def copy_lowT(n):
                dve.wait_ge(lowT_ps, n + 1)
                nc.vector.tensor_copy(lowT[:, :], second(n)[0:HD, 1, :]).then_inc(lowT_done, 1)

            def route_weights(n):
                routing.weigh(dve, n, comb1[:, bass.ds(n * TILES, TILES), :])

            dve.wait_ge(ident_in, 16)
            nc.vector.tensor_copy(identb[:, :], ident[:, :]).then_inc(identb_done, 1)
            for t in range(TILES):
                reduce(0, 0, t)
            split_max(0, 0, reused=False)
            for t in range(TILES):
                reduce(1, 1, t)
                if t == 0:
                    dve.wait_ge(nmT_ready, 1)
                    nc.vector.tensor_copy(nmT[0][:, :], psN[0:2 * HG, :]).then_inc(nmT_copied, 1)
            split_max(1, 1, reused=False)
            dve.wait_ge(g_done, 1)
            nc.vector.tensor_scalar(gates[:, 0, :], gates[:, 1, :], -1.0, 1.0, ALU.mult, ALU.add).then_inc(omg_done, 1)
            dve.wait_ge(omg_done, 1)
            dve.wait_ge(tables, TABLES)
            dve.wait_ge(w_lo, 3)
            loop(dve, attend, {0: (weigh_terms(0),), 1: (weigh_terms(1),), 2: (weigh_terms(2),), 3: (weigh_terms(3),), 5: (residual,), 6: (moments,),
                               7: (normalise,), 8: (split_xT,), 10: (copy_low,), 11: (copy_lowT,), 12: (route_weights,),
                               13: (first_part,), 14: (second_part,), 15: (third_part, decay_k)})

        @block.tensor
        def _(pe):
            def rows(n, g, t, b, heads):
                if t == 0 and heads[0] == 0:
                    pe.wait_ge(stack_in[g], LOADED * (b + 1))
                for h in heads:
                    pe.wait_ge(rows_used[h % 2], 8 * n + 2 * t + h // 2)
                    nc.tensor.matmul(psM[:, h % 2, :], qst[g][0:STACK, h, t * P:(t + 1) * P], kst[g][0:STACK, h, :],
                                     start=True, stop=True).then_inc(rows_ready, 1)

            def turn_max(n, i):
                pe.wait_ge(negmax_parts, n + 1)
                pe.wait_ge(nmT_copied, n)
                for t in range(TILES):
                    mm = nc.tensor.transpose(psN[0:2 * HG, t * P:(t + 1) * P],
                                             nmparts[i][:, t, :, :].rearrange("p a h -> p (a h)"), identb[:, :])
                mm.then_inc(nmT_ready, 1)

            def attend(b, g, last, beside):
                G = GROUPS * b + g
                pe.wait_ge(max_in[g], 16 * b + 16)

                def scores(k, heads):
                    for h in heads:
                        pe.wait_ge(scores_used[h % 2], 2 * (TILES * G + k) + h // 2)
                        nc.tensor.matmul(psE[h % 2][:, :], kst[g][0:STACKM, h, k * P:(k + 1) * P],
                                         qst[g][0:STACKM, h, :], start=True, stop=True).then_inc(scores_ready, 1)

                def values(k):
                    for used in scores_used:
                        pe.wait_ge(used, 2 * (TILES * G + k + 1))
                    if k == 0:
                        pe.wait_ge(out_copied, G)
                    for h in range(HG):
                        mm = nc.tensor.matmul(psV[VW * h:VW * (h + 1), :], vst[g][:, k, VW * h:VW * (h + 1)],
                                              probs[k % PSLOTS][:, h, :], start=k == 0, stop=k == TILES - 1,
                                              tile_position=(0, VW * h), skip_group_check=True)
                    mm.then_inc(probs_used, 1)

                for k in range(TILES):
                    ahead = not (last and g >= GROUPS - 2)
                    next_rows = G + 2, (g + 2) % GROUPS, k, b if g < 2 else b + 1
                    scores(k, (0, 1))
                    if k == 1 and not (last and g == GROUPS - 1):
                        turn_max(G + 1, (g + 1) % 2)
                    if ahead:
                        rows(*next_rows, (0, 1))
                    if k:
                        values(k - 1)
                    scores(k, (2, 3))
                    beside(k)
                    if ahead:
                        rows(*next_rows, (2, 3))
                values(TILES - 1)

            def heads(t):
                def step(n):
                    if t == 0:
                        pe.wait_ge(out_copied, GROUPS * (n + 1))
                        pe.wait_ge(qf_in, 16 * n + 16)
                        pe.wait_ge(v_done, n)
                    elif not alone(n):
                        pe.wait_ge(terms, TILES * n + t)
                    elif t == 1:
                        for used in rows_used:
                            pe.wait_ge(used, 2 * TILES * GROUPS * BATCHES)
                    else:
                        pe.wait_ge(terms, TILES * n + t - 1)
                    ps = second(n) if t % 2 else psX
                    c, w = slice(t * P, (t + 1) * P), HG * (HD + 1)
                    for g in range(GROUPS):
                        nc.tensor.matmul(ps[:, 0, g * w:(g + 1) * w], outT[:, g, c], sel[:, :], start=True, stop=True,
                                         skip_group_check=True)
                    for k in range(KT):
                        mm = nc.tensor.matmul(ps[:, 1, MW * k:MW * (k + 1)], qf[:, k, c],
                                              mem[:, bass.ds(n * KT + k, 1), :].rearrange("p a n -> p (a n)"),
                                              start=True, stop=True, skip_group_check=True)
                    mm.then_inc(heads_ps, 1)
                return step

            def turn_combined(n):
                pe.wait_ge(combined_done, TILES * n + TILES)
                for t in range(TILES):
                    for k in range(KT):
                        mm = nc.tensor.transpose(psX[:, k, t * P:(t + 1) * P], combined[:, t, k * P:(k + 1) * P], ident[:, :])
                mm.then_inc(combT_ps, 1)

            def project_out(n):
                pe.wait_ge(combT_done, n + 1)
                for t in range(TILES):
                    for k in range(KT):
                        mm = nc.tensor.matmul(psX[:, t // 2, t % 2 * D:(t % 2 + 1) * D], combT[:, k, t * P:(t + 1) * P], wo[:, k, :],
                                              start=k == 0, stop=k == KT - 1, skip_group_check=True)
                mm.then_inc(y_ps, 1)

            def turn_x(n):
                pe.wait_ge(norm.xn_done, TILES * n + TILES)
                for t in range(TILES):
                    for k in range(KT):
                        mm = nc.tensor.transpose(psX[:, k, t * P:(t + 1) * P], xn[:, t, k * P:(k + 1) * P], ident[:, :])
                mm.then_inc(xT_ps, 1)

            def project_half(i):
                def step(n):
                    if i == 0:
                        pe.wait_ge(xlo, n + 1)
                    elif not alone(n):
                        pe.wait_ge(lowT_done, n + 1)
                        pe.wait_ge(routing.copied, n + 1)
                    else:
                        pe.wait_ge(half_done, 2 * n + 1)
                    for m in range(KT):
                        c = slice((KT * i + m) * P, (KT * i + m + 1) * P)
                        mm = three(nc, psX[:, m, :], [(wqk[0][:, k, c], wqk[1][:, k, c], xT[0][:, k, :], xT[1][:, k, :])
                                                      for k in range(KT)])
                    mm.then_inc(half_ps, 1)
                return step

            def logits_low(n):
                if not alone(n):
                    pe.wait_ge(half_done, 2 * n + 1)
                for t in range(TILES):
                    c = slice(t * P, (t + 1) * P)
                    mm = three(nc, second(n)[:, 0, t * RW:(t + 1) * RW],
                               [(xT[0][:, k, c], xT[1][:, k, c], wr[0][:, k, :], wr[1][:, k, :]) for k in range(KT)])
                mm.then_inc(low_ps, 1)

            def turn_low(n):
                pe.wait_ge(low_done, n + 1)
                for t in range(TILES):
                    mm = nc.tensor.transpose(second(n)[0:HD, 1, t * P:(t + 1) * P], low[:, t, :], ident[:, :])
                mm.then_inc(lowT_ps, 1)

            def project_gate(n):
                pe.wait_ge(lowT_done, n + 1)
                pe.wait_ge(routing.copied, n + 1)
                if not alone(n):
                    pe.wait_ge(half_done, 2 * n + 2)
                for t in range(TILES):
                    mm = nc.tensor.matmul(second(n)[:, t // 2, (t % 2) * D:(t % 2 + 1) * D], lowT[:, t * P:(t + 1) * P],
                                          wg2[:, :], start=True, stop=True, skip_group_check=True)
                mm.then_inc(gate_ps, 1)

            def project_tokens(i, free, done):
                def step(n):
                    ps = second(n) if i else psX
                    if not alone(n):
                        pe.wait_ge(free, n + 1)
                    elif i:
                        pe.wait_ge(gate_done, n + 1)
                    else:
                        pe.wait_ge(half_done, 2 * n + 2)
                    for t in range(TILES):
                        c = slice(t * P, (t + 1) * P)
                        mm = three(nc, ps[:, t // 2, (t % 2) * D:(t % 2 + 1) * D],
                                   [(xT[0][:, k, c], xT[1][:, k, c], wkv[0][:, k, i * D:(i + 1) * D], wkv[1][:, k, i * D:(i + 1) * D])
                                    for k in range(KT)])
                    mm.then_inc(done, 1)
                return step

            for t in range(TILES):
                rows(0, 0, t, 0, range(HG))
            pe.wait_ge(identb_done, 1)
            for t in range(TILES):
                rows(1, 1, t, 0, range(HG))
                if t == 0:
                    turn_max(0, 0)
            pe.wait_ge(ones, GROUPS)

            def ready():
                pe.wait_ge(consts_in, CONSTS)
                pe.wait_ge(weights_in, WEIGHTS)
                pe.wait_ge(w_lo, 3)

            loop(pe, attend, {0: (heads(0),), 1: (heads(1),), 2: (heads(2),), 3: (heads(3),), 4: (turn_combined,), 5: (project_out,),
                              8: (turn_x,), 9: (project_half(0),), 10: (logits_low,), 11: (turn_low,), 12: (project_half(1),),
                              13: (project_gate,), 14: (project_tokens(0, gate_done, kk_ps),),
                              15: (project_tokens(1, kk_done, v_ps),)}, ready)


AHEAD = 2
NC = SEQ // CH
UPDATES = NC - 1
SPAN = BATCHES * HT1 * 2 // NC


def layer1_main(nc, io, scratch, keep, out):
    with ExitStack() as ctx:
        def sb(name, shape, dt=F32):
            return ctx.enter_context(nc.sbuf_tensor("d_" + name, shape, dt))

        def sem(name):
            return stage_semaphore(nc, keep, "d_" + name)

        def sems(name, n):
            return [sem(f"{name}{i}") for i in range(n)]

        xacc, xT, comb1 = keep["xacc"], keep["xT1"], keep["comb1"]
        decay, cdec = keep["decay"], keep["cdec"]
        G, U, DN = KT * H1, KT * H1, HT1 * D
        raw, raw_in = keep["raw"], keep["raw_in"]
        w = [[[sb(f"w{e}{i}{j}", [P, n], F32R) for j in range(2)] for i, n in enumerate((G, U, DN))] for e in range(2)]
        h = [sb(f"h{i}", [P, SEQ]) for i in range(HSLOTS)]
        hh = [[sb(f"hh{i}{j}", [P, SEQ], F32R) for j in range(2)] for i in range(HSLOTS)]
        ident, sel, blockmask = sb("ident", [P, P]), sb("sel", [P, HG * HD]), sb("blockmask", [P, P])
        normw, neghalf, wo = sb("normw", [P, D]), sb("neghalf", [P, HEADS]), sb("wo", [P, KT, D])
        qst, kst = ([sb(f"{n}{s}", [STACK, HEADS, CH], BF16) for s in range(2)] for n in ("qst", "kst"))
        v = [sb(f"v{s}", [P, HEADS, VW]) for s in range(2)]
        kd, sg, qd = ([sb(f"{n}{s}", [P, D]) for s in range(2)] for n in ("kd", "sg", "qd"))
        probs = [sb(f"probs{g}", [P, HG * CH]) for g in range(GROUPS)]
        headsT = sb("headsT", [P, GROUPS * CH])
        state, update = sb("state", [P, KT, P]), sb("update", [P, KT, P])
        o, sq, ss, rs = sb("o", [P, D]), sb("sq", [P, D]), sb("ss", [P, HEADS]), sb("rs", [P, HEADS])
        normed, normT = sb("normed", [P, D]), sb("normT", [P, KT, P])

        psG = ctx.enter_context(nc.psum_tensor("d_psG", [P, 4, SEQ], F32))
        psY = ctx.enter_context(nc.psum_tensor("d_psY", [P, TILES, D], F32))
        ps0, ps1 = (ctx.enter_context(nc.psum_tensor(f"d_ps{i}", [P, SEQ], F32)) for i in range(2))

        w_hi, w_lo = sems("w_hi", 3), sems("w_lo", 3)
        gate_up_ps, silu_done, hi_done, added = sem("gate_up_ps"), sem("silu"), sem("hi"), sem("added")
        mult_done, lo_done, down_ps = sems("mult", 2), sems("lo", HSLOTS), sems("down_ps", HSLOTS)
        consts_in, neghalf_set = sem("consts"), sem("neghalf")
        chunk_in, gated = sems("chunk_in", 2), sems("gated", 2)
        scores_ps, probs_done, probs_used = sems("scores_ps", GROUPS), sems("probs", GROUPS), sem("probs_used")
        heads_copied, update_ps, update_done, state_done = (sem(n) for n in ("heads_copied", "update_ps", "update", "state"))
        out_ps, squared, summed, ss_done, rs_done = (sem(n) for n in ("out_ps", "squared", "summed", "ss", "rs"))
        scaled, normed_done, normT_ps, normT_done, y_ps, y_done = (
            sem(n) for n in ("scaled", "normed", "normT_ps", "normT", "y_ps", "y"))
        stored = sem("stored")
        N = BATCHES * HT1
        PAIR = 2 * N
        CONSTS = 5
        CHUNK_IN = 16 * (2 * len(Q_PARTS) + 4)

        def loop(eng, run):
            with eng.Fori(0, E // 2 - 1) as i:
                run(i, False)
            run(E // 2 - 1, True)

        def tiles(i, last, tile, steps):
            for t in range(PAIR):
                if step := steps.get((t % SPAN, -1)):
                    step(i, t // SPAN)
                if t + AHEAD < PAIR:
                    tile(i, t + AHEAD, last)
                elif not last:
                    tile(i + 1, t + AHEAD - PAIR, False)
                yield t, steps.get((t % SPAN, 0)), steps.get((t % SPAN, 1))

        def view(t, k):
            return t[:, :].rearrange("p (k n) -> p k n", k=k)

        def other_expert(i, t, last):
            half, piece = t // N, t % N - 1
            if not 0 <= piece < 3 or (last and half):
                return None
            return piece, 2 * i + 1 + half, PAIR // HSLOTS * i + half * N // HSLOTS

        block = ctx.enter_context(nc.Block())

        @block.sync
        def _(sp):
            def load_weights(x):
                for i, (name, k) in enumerate(EXPERT_WEIGHTS):
                    sp.wait_ge(w_lo[i], x)
                    weights = io[name][x] if isinstance(x, int) else io[name][bass.ds(x, 1), :, :].rearrange("a r n -> (a r) n")
                    sp.dma_start(view(raw[i], k), weights.rearrange("(k p) n -> p k n", p=P)).then_inc(raw_in[i], 16)

            def load_chunk(b, c):
                s, t = c % 2, slice(c * CH, (c + 1) * CH)
                sp.wait_ge(gated[s], 2 * b + c // 2)
                for op, dst, order in ((0, qst, Q_PARTS), (1, kst, K_PARTS)):
                    for n, part in enumerate(order):
                        sp.dma_start(dst[s][n * HD:(n + 1) * HD, :, :],
                                     scratch["parts1"][b, part, KT * op:KT * (op + 1), :, t]
                                     .rearrange("k (h d) t -> d (k h) t", d=HD)).then_inc(chunk_in[s], 16)
                sp.dma_start(v[s][:, :, :].rearrange("p h w -> p (h w)"), scratch["v1"][b, t, :]).then_inc(chunk_in[s], 16)
                sp.dma_start(kd[s][:, :], scratch["kd"][b, t, :]).then_inc(chunk_in[s], 16)
                sp.dma_start(sg[s][:, :], scratch["sg"][b, t, :]).then_inc(chunk_in[s], 16)
                sp.dma_start(view(qd[s], KT), scratch["qd"][b, :, :, t].rearrange("k p n -> p k n")).then_inc(chunk_in[s], 16)

            sp.wait_ge(keep["stored"], 16 * STORES1 * BATCHES)
            sp.wait_ge(keep["part_stored"], 16 * PARTS1 * 2 * BATCHES)
            load_chunk(0, 0)
            load_weights(1)
            for dst, src in ((ident[:, :], io["ident"]), (sel[:, :], io["sel16"]), (blockmask[:, :], io["blockmask"]),
                             (normw[:, :], io["norm_w"].to_broadcast((P, D))),
                             (wo[:, :, :], io["Wo1"].rearrange("(k p) n -> p k n", p=P))):
                sp.dma_start(dst, src).then_inc(consts_in, 16)
            load_chunk(0, 1)

            def run(i, last):
                load_chunk(i, 2)
                if not last:
                    load_weights(2 * i + 2)
                load_chunk(i, 3)
                if not last:
                    load_weights(2 * i + 3)
                    load_chunk(i + 1, 0)
                    load_chunk(i + 1, 1)

            loop(sp, run)
            for b in range(BATCHES):
                sp.wait_ge(added, 2 * BATCHES * (E // 2 - 1) + BATCHES + b + 1)
                sp.wait_ge(y_done, NC * min(b + 1, BATCHES))
                sp.dma_start(out[b * SEQ:(b + 1) * SEQ, :].rearrange("(t p) d -> p t d", p=P),
                             xacc[:, b * TILES:(b + 1) * TILES, :]).then_inc(stored, 16)
            sp.wait_ge(stored, 16 * BATCHES)

        @block.gpsimd
        def _(pool):
            def tile(i, t, last):
                s = t % HSLOTS
                pool.wait_ge(hi_done, PAIR * i + t + 1)
                nc.gpsimd.tensor_tensor(hh[s][1][:, :], h[s][:, :], hh[s][0][:, :].bitcast(F32),
                                        ALU.subtract).then_inc(lo_done[s], 1)

            def power(i, c):
                pool.wait_ge(ss_done, NC * i + c + 1)
                nc.gpsimd.tensor_tensor(rs[:, :], ss[:, :], neghalf[:, :], ALU.pow).then_inc(rs_done, 1)

            nc.gpsimd.memset(neghalf[:, :], -0.5).then_inc(neghalf_set, 1)
            pool.wait_ge(neghalf_set, 1)
            for t in range(AHEAD):
                tile(0, t, False)

            def run(i, last):
                for t, *steps in tiles(i, last, tile, {(5, 0): power}):
                    for step in filter(None, steps):
                        step(i, t // SPAN)

            loop(pool, run)

        @block.scalar
        def _(act):
            def split_hi(e, piece, x):
                act.wait_ge(raw_in[piece], 16 * x + 16)
                nc.scalar.activation(w[e][piece][0][:, :], raw[piece][:, :], ACT.Copy).then_inc(w_hi[piece], 1)

            def tile(i, t, last):
                s = t % HSLOTS
                act.wait_ge(gate_up_ps, PAIR * i + t + 1)
                act.wait_ge(lo_done[s], PAIR // HSLOTS * i + t // HSLOTS)
                nc.scalar.activation(h[s][:, :], psG[:, 2 * (t % 2), :], ACT.Silu).then_inc(silu_done, 1)
                if found := other_expert(i, t, last):
                    act.wait_ge(down_ps[HSLOTS - 1], found[2])
                    split_hi((t // N + 1) % 2, found[0], found[1])
                act.wait_ge(mult_done[t % 2], PAIR // 2 * i + t // 2 + 1)
                act.wait_ge(down_ps[s], PAIR // HSLOTS * i + t // HSLOTS)
                nc.scalar.activation(hh[s][0][:, :], h[s][:, :], ACT.Copy).then_inc(hi_done, 1)

            def copy_heads(i, c):
                act.wait_ge(probs_used, NC * i + c + 1)
                act.wait_ge(out_ps, NC * i + c)
                nc.scalar.activation(headsT[:, :], ps0[:, :], ACT.Copy).then_inc(heads_copied, 1)

            def copy_normT(i, c):
                act.wait_ge(normT_ps, NC * i + c + 1)
                act.wait_ge(y_ps, NC * i + c)
                nc.scalar.activation(normT[:, :, :], ps1[:, 0:KT * P].rearrange("p (k n) -> p k n", k=KT),
                                     ACT.Copy).then_inc(normT_done, 1)

            for piece in range(3):
                split_hi(0, piece, 0)
            for t in range(AHEAD):
                tile(0, t, False)

            def run(i, last):
                for t, *steps in tiles(i, last, tile, {(3, 1): copy_heads, (6, 1): copy_normT}):
                    for step in filter(None, steps):
                        step(i, t // SPAN)

            loop(act, run)

        @block.vector
        def _(dve):
            def split_lo(e, piece, x):
                dve.wait_ge(w_hi[piece], x + 1)
                nc.vector.tensor_tensor(w[e][piece][1][:, :], raw[piece][:, :], w[e][piece][0][:, :].bitcast(F32),
                                        ALU.subtract).then_inc(w_lo[piece], 1)

            def tile(i, t, last):
                s = t % HSLOTS
                dve.wait_ge(silu_done, PAIR * i + t + 1)
                nc.vector.tensor_tensor(h[s][:, :], h[s][:, :], psG[:, 2 * (t % 2) + 1, :],
                                        ALU.mult).then_inc(mult_done[t % 2], 1)
                if found := other_expert(i, t, last):
                    split_lo((t // N + 1) % 2, found[0], found[1])

            def add(i, t):
                dve.wait_ge(down_ps[HSLOTS - 1], PAIR // HSLOTS * i + t // HSLOTS + 1)
                dve.wait_ge(y_done, NC * i + (t + 1) // SPAN)
                for k in range(TILES):
                    rows = t // HT1 % BATCHES * TILES + k
                    weight = comb1[:, rows, bass.ds(2 * i + t // N, 1)] if not isinstance(i, int) else \
                        comb1[:, rows, 2 * i + t // N:2 * i + t // N + 1]
                    last = nc.vector.scalar_tensor_tensor(xacc[:, rows, :], psY[:, k, :], weight,
                                                          xacc[:, rows, :], ALU.mult, ALU.add)
                last.then_inc(added, 1)

            def weigh(g):
                def step(i, c):
                    dve.wait_ge(scores_ps[g], NC * i + c + 1)
                    dve.wait_ge(probs_used, NC * i + c)
                    nc.vector.tensor_tensor(probs[g][:, :], (ps1 if g % 2 else ps0)[:, :],
                                            decay[:, HG * g:HG * g + HG, :].rearrange("p h c -> p (h c)"),
                                            ALU.mult).then_inc(probs_done[g], 1)
                return step

            def take_update(i, c):
                if c == NC - 1:
                    return
                dve.wait_ge(consts_in, 16 * CONSTS)
                dve.wait_ge(update_ps, UPDATES * i + c + 1)
                nc.vector.tensor_tensor((update if c else state)[:, :, :], ps1[:, 0:KT * P].rearrange("p (k n) -> p k n", k=KT),
                                        blockmask[:, :].unsqueeze(1).to_broadcast((P, KT, P)), ALU.mult).then_inc(update_done, 1)

            def gate(i, c):
                s = c % 2
                dve.wait_ge(out_ps, NC * i + c + 1)
                nc.vector.tensor_tensor(o[:, :], ps0[:, 0:D], sg[s][:, :], ALU.mult).then_inc(gated[s], 1)
                if 0 < c < NC - 1:
                    dve.wait_ge(update_done, UPDATES * i + c + 1)
                    dve.wait_ge(state_done, (UPDATES - 1) * i + c - 1)
                    for k in range(KT):
                        last = nc.vector.scalar_tensor_tensor(state[:, k, :], state[:, k, :], cdec[:, k:k + 1], update[:, k, :],
                                                              ALU.mult, ALU.add)
                    last.then_inc(state_done, 1)
                dve.wait_ge(gated[s], 2 * i + c // 2 + 1)
                nc.vector.tensor_tensor(sq[:, :], o[:, :], o[:, :], ALU.mult).then_inc(squared, 1)
                dve.wait_ge(squared, NC * i + c + 1)
                nc.vector.tensor_reduce(ss[:, :], sq[:, :].rearrange("p (h d) -> p h d", d=HD), AX_X, ALU.add).then_inc(summed, 1)
                dve.wait_ge(summed, NC * i + c + 1)
                nc.vector.tensor_scalar(ss[:, :], ss[:, :], 1.0 / HD, EPS, ALU.mult, ALU.add).then_inc(ss_done, 1)

            def normalise(i, c):
                dve.wait_ge(rs_done, NC * i + c + 1)
                nc.vector.tensor_tensor(o[:, :].rearrange("p (h d) -> p h d", d=HD), o[:, :].rearrange("p (h d) -> p h d", d=HD),
                                        rs[:, :].unsqueeze(2).to_broadcast((P, HEADS, HD)), ALU.mult).then_inc(scaled, 1)
                dve.wait_ge(scaled, NC * i + c + 1)
                dve.wait_ge(normT_ps, NC * i + c)
                nc.vector.tensor_tensor(normed[:, :], o[:, :], normw[:, :], ALU.mult).then_inc(normed_done, 1)

            def residual(i, c):
                dve.wait_ge(y_ps, NC * i + c + 1)
                dve.wait_ge(added, PAIR // HT1 * i + (SPAN * (c + 1) - 1) // HT1)
                x = xacc[:, bass.ds(NC * i + c, 1), :].rearrange("p a d -> p (a d)")
                nc.vector.tensor_tensor(x, ps0[:, 0:D], x, ALU.add).then_inc(y_done, 1)

            for piece in range(3):
                split_lo(0, piece, 0)
            for t in range(AHEAD):
                tile(0, t, False)

            def run(i, last):
                steps = {(0, 0): weigh(0), (0, 1): weigh(1), (1, 1): weigh(2), (2, 0): weigh(3), (4, 0): take_update,
                         (5, 0): gate, (6, -1): normalise, (7, 1): residual}
                for t, *found in tiles(i, last, tile, steps):
                    for step in filter(None, found):
                        step(i, t // SPAN)
                    if t % HT1 == HT1 - 1:
                        add(i, t)

            loop(dve, run)

        @block.tensor
        def _(pe):
            def tile(i, t, last):
                pe.wait_ge(mult_done[t % 2], PAIR // 2 * i + t // 2)
                m, chunk = t % HT1, t // HT1 % BATCHES
                for j in range(2):
                    if t % N == 0:
                        pe.wait_ge(w_lo[j], 2 * i + t // N + 1)
                    hi, lo = (view(x, KT)[:, :, m * P:(m + 1) * P] for x in w[t // N][j])
                    c = slice(chunk * SEQ, (chunk + 1) * SEQ)
                    mm = three(nc, psG[:, 2 * (t % 2) + j, :], [(hi[:, k, :], lo[:, k, :], xT[0][:, k, c], xT[1][:, k, c])
                                                                for k in range(KT)])
                mm.then_inc(gate_up_ps, 1)

            def down(i, t):
                s, m, chunk = t % HSLOTS, t % HT1, t // HT1
                if t % N == 0:
                    pe.wait_ge(w_lo[2], 2 * i + t // N + 1)
                if m == 0:
                    pe.wait_ge(added, PAIR // HT1 * i + chunk)
                pe.wait_ge(lo_done[s], PAIR // HSLOTS * i + t // HSLOTS + 1)
                hi, lo = (view(x, HT1)[:, m, :] for x in w[t // N][2])
                for k in range(TILES):
                    c = slice(k * P, (k + 1) * P)
                    mm = three(nc, psY[:, k, :], [(hh[s][0][:, c], hh[s][1][:, c], hi, lo)],
                               start=m == 0 and k % 2 == 0, last=m == HT1 - 1)
                mm.then_inc(down_ps[s], 1)

            def scores(g):
                def step(i, c):
                    s = c % 2
                    if g == 0:
                        pe.wait_ge(chunk_in[s], CHUNK_IN * (2 * i + c // 2 + 1))
                        pe.wait_ge(y_done, NC * i + c)
                    elif g == 1:
                        pe.wait_ge(normT_done, NC * i + c)
                    else:
                        pe.wait_ge(probs_done[g - 2], NC * i + c + 1)
                    for n in range(HG):
                        mm = nc.tensor.matmul((ps1 if g % 2 else ps0)[:, n * CH:(n + 1) * CH], kst[s][:, HG * g + n, :],
                                              qst[s][:, HG * g + n, :], start=True, stop=True, skip_group_check=True)
                    mm.then_inc(scores_ps[g], 1)
                return step

            def own(i, c):
                for g in range(GROUPS):
                    pe.wait_ge(probs_done[g], NC * i + c + 1)
                for g in range(GROUPS):
                    for n in range(HG):
                        mm = nc.tensor.matmul(ps0[VW * n:VW * (n + 1), g * CH:(g + 1) * CH], v[c % 2][:, HG * g + n, :],
                                              probs[g][:, n * CH:(n + 1) * CH], start=True, stop=True,
                                              tile_position=(0, VW * n), skip_group_check=True)
                mm.then_inc(probs_used, 1)

            def updates(i, c):
                if c == NC - 1:
                    return
                pe.wait_ge(probs_done[GROUPS - 1], NC * i + c + 1)
                for k in range(KT):
                    mm = nc.tensor.matmul(ps1[:, k * P:(k + 1) * P], kd[c % 2][:, k * P:(k + 1) * P],
                                          v[c % 2][:, k * HH:(k + 1) * HH, 0:HD], start=True, stop=True, skip_group_check=True)
                mm.then_inc(update_ps, 1)

            def outputs(i, c):
                pe.wait_ge(consts_in, 16 * CONSTS)
                pe.wait_ge(heads_copied, NC * i + c + 1)
                if c == 1:
                    pe.wait_ge(update_done, UPDATES * i + 1)
                elif c:
                    pe.wait_ge(state_done, (UPDATES - 1) * i + c - 1)
                if c:
                    for k in range(KT):
                        nc.tensor.matmul(ps0[:, k * P:(k + 1) * P], qd[c % 2][:, k * P:(k + 1) * P], state[:, k, :],
                                         start=k == 0, stop=False, skip_group_check=True)
                for g in range(GROUPS):
                    mm = nc.tensor.matmul(ps0[:, g * HG * HD:(g + 1) * HG * HD], headsT[:, g * CH:(g + 1) * CH], sel[:, :],
                                          start=c == 0 and g == 0, stop=g == GROUPS - 1, skip_group_check=True)
                mm.then_inc(out_ps, 1)

            def turn(i, c):
                pe.wait_ge(normed_done, NC * i + c + 1)
                if c < NC - 1:
                    pe.wait_ge(update_done, UPDATES * i + c + 1)
                for k in range(KT):
                    mm = nc.tensor.transpose(ps1[:, k * P:(k + 1) * P], normed[:, k * P:(k + 1) * P], ident[:, :])
                mm.then_inc(normT_ps, 1)

            def project(i, c):
                pe.wait_ge(normT_done, NC * i + c + 1)
                pe.wait_ge(gated[c % 2], 2 * i + c // 2 + 1)
                for k in range(KT):
                    mm = nc.tensor.matmul(ps0[:, 0:D], normT[:, k, :], wo[:, k, :], start=k == 0, stop=k == KT - 1)
                mm.then_inc(y_ps, 1)

            for t in range(AHEAD):
                tile(0, t, False)

            def run(i, last):
                steps = {(0, 0): scores(0), (0, 1): scores(1), (1, 1): scores(2), (2, 0): scores(3), (3, 1): own,
                         (4, 0): updates, (5, 0): outputs, (6, 1): turn, (7, 1): project}
                for t, before, behind in tiles(i, last, tile, steps):
                    if before:
                        before(i, t // SPAN)
                    down(i, t)
                    if behind:
                        behind(i, t // SPAN)

            loop(pe, run)


def two_layers(nc, io, out):
    with ExitStack() as ctx:
        def sb(name, shape, dt=F32):
            return ctx.enter_context(nc.sbuf_tensor(name, shape, dt))

        def dram(name, shape, dt=F32):
            return nc.dram_tensor("scratch_" + name, shape, dt, kind="Internal").ap()

        scratch = {
            "cT": dram("cT", (BATCHES, E, SEQ)),
            "v": dram("v", (BATCHES, SEQ, HEADS * VW)),
            "qf": dram("qf", (BATCHES, KT, P, SEQ)),
            "parts": dram("parts", (BATCHES, 3, 2 * KT, P, SEQ), BF16),
            "max": dram("max", (2 * HG, SEQ), BF16),
            "v1": dram("v1", (BATCHES, SEQ, HEADS * VW)),
            "kd": dram("kd", (BATCHES, SEQ, D)),
            "qd": dram("qd", (BATCHES, KT, P, SEQ)),
            "parts1": dram("parts1", (BATCHES, 3, 2 * KT, P, SEQ), BF16),
            "sg": dram("sg", (BATCHES, SEQ, D)),
        }
        keep = {"xacc": sb("xacc", [P, TOK // P, D]), "semaphores": []}
        with ExitStack() as inner:
            keep["mem"] = inner.enter_context(nc.sbuf_tensor("mem", [P, BATCHES * KT, MW], F32))
            layer0_front(nc, io, scratch, keep)
            end_stage(nc, keep)
            keep["xT1"] = [inner.enter_context(nc.sbuf_tensor(f"xT1{i}", [P, KT, TOK], F32R)) for i in range(2)]
            keep["comb1"] = inner.enter_context(nc.sbuf_tensor("comb1", [P, TOK // P, E], F32))
            keep["stored"], keep["part_stored"] = (nc.alloc_semaphore(n) for n in ("stored", "part_stored"))
            keep["raw"] = [inner.enter_context(nc.sbuf_tensor(name + "_raw", [P, D * H1 // P], F32)) for name, _ in EXPERT_WEIGHTS]
            keep["raw_in"] = [nc.alloc_semaphore(name + "_in") for name, _ in EXPERT_WEIGHTS]
            keep["decay"] = inner.enter_context(nc.sbuf_tensor("decay", [P, HEADS, CH], F32))
            keep["cdec"] = inner.enter_context(nc.sbuf_tensor("cdec", [P, KT], F32))
            middle(nc, io, scratch, keep)
            end_stage(nc, keep)
            layer1_main(nc, io, scratch, keep, out)


def constants():
    import numpy as np
    f = np.arange(512, dtype=np.float32)[None, :] * (np.float32(1.0) / np.float32(10000.0) ** (np.arange(0, 256, 2, dtype=np.float32) / np.float32(256)))[:, None]
    p = np.arange(128)
    c = {}
    c['ident'] = np.eye(128, dtype=np.float32)
    c['cos'], c['sin'] = np.cos(f).astype(np.float32), np.sin(f).astype(np.float32)
    c['blockmask'] = (p[:, None] // 16 == p[None, :] // 16).astype(np.float32)
    c['headmask'] = np.repeat((p[:, None] // 16 == np.arange(8)[None, :]).astype(np.float32), 17, axis=1)
    c['iota8'] = np.tile(np.arange(8, dtype=np.float32), (128, 4))
    sel = np.zeros((128, 4, 17), np.float32)
    for g in range(4):
        for j in range(17):
            sel[32 * g + j, g, j] = 1
    c['sel17'] = sel.reshape(128, 68)
    c['sel16'] = np.ascontiguousarray(sel[:, :, :16]).reshape(128, 64)
    c['rel'] = np.maximum(p[None, :] - p[:, None], 0).astype(np.float32)
    c['causal'] = (p[None, :] >= p[:, None]).astype(np.float32)
    c['after'] = np.tile((p + 1).astype(np.float32), (128, 1))
    c['before'] = (127 - p).astype(np.float32)[:, None].copy()
    return c


def layout(g):
    import numpy as np
    C = np.ascontiguousarray
    arrays = {"x": g["L0_attn_hidden_states"]}
    for n in ("Wq", "Wk", "Wv", "Wo"):
        arrays[n + "0"] = C(g["L0_attn_" + n].T)
        arrays[n + "1"] = g["L1_attn_" + n]
    arrays["gate_attn"] = C(g["L0_attn_gate"].reshape(1, HEADS))
    arrays["router0"] = C(g["L0_ffn_gate_w"].T)
    arrays["gate0"] = C(g["L0_ffn_gate_proj"].reshape(E * F0, D).T)
    arrays["up0"] = C(g["L0_ffn_up_proj"].reshape(E * F0, D).T)
    arrays["down0"] = C(g["L0_ffn_down_proj"].transpose(0, 2, 1)).reshape(E * F0, D)
    arrays["log_decay"] = g["L1_attn_log_decay"].reshape(1, HEADS)
    arrays["log_decay_rows"] = C(np.repeat(g["L1_attn_log_decay"].reshape(KT, HH), HD, axis=1).T)
    arrays["Wg1"], arrays["Wg2"] = g["L1_attn_Wg1"], g["L1_attn_Wg2"]
    arrays["norm_w"] = g["L1_attn_norm_w"].reshape(1, D)
    arrays["router1"] = g["L1_ffn_w_router"]
    arrays["gate1"], arrays["up1"], arrays["down1"] = g["L1_ffn_w_gate"], g["L1_ffn_w_up"], g["L1_ffn_w_down"]
    return arrays


def kernel(**inputs):
    import numpy as np
    import concourse.bacc as bacc
    from concourse.bass_utils import run_bass_kernel_spmd

    arrays = layout({name: np.asarray(a) for name, a in inputs.items()})
    arrays.update(constants())
    nc = bacc.Bacc("TRN2", target_bir_lowering=False, num_devices=1)
    io = {}
    for name, a in arrays.items():
        io[name] = nc.dram_tensor(f"in_{name}_dram", a.shape, mybir.dt.from_np(a.dtype), kind="ExternalInput").ap()
    out = nc.dram_tensor("out_0_dram", (BATCHES, SEQ, D), F32, kind="ExternalOutput").ap()
    two_layers(nc, io, out.rearrange("b s d -> (b s) d"))
    r = run_bass_kernel_spmd(nc, [{f"in_{name}_dram": np.ascontiguousarray(a) for name, a in arrays.items()}], core_ids=[0])
    return r.results[0]["out_0_dram"]
```
